# Optimizing a Trainium2 kernel written in Bass

```python
import numpy as np
import jax
import jax.numpy as jnp

def _softmax(x, axis=-1):
    return jax.nn.softmax(x, axis=axis)
def _gelu(x):
    return jax.nn.gelu(x, approximate=True)
def _silu(x):
    return jax.nn.silu(x)
def _sigmoid(x):
    return jax.nn.sigmoid(x)
def _layernorm(x, axis=-1, eps=1e-5):
    m = jnp.mean(x, axis=axis, keepdims=True)
    v = jnp.var(x, axis=axis, keepdims=True)
    return (x - m) / jnp.sqrt(v + eps)
def _scatter_add(tgt, idx, src, axis=0):
    return tgt.at[idx].add(src)
def _segment_sum(src, seg, n):
    return jax.ops.segment_sum(src, seg, n)

kernel_name = 'mk_conv_seq_d4_conv_nchw256_d52063'

def setup_inputs(seed: int = 0):
    np.random.seed(seed)
    _w = jnp.asarray
    def _rec_inputs():
        import jax
        import jax.numpy as jnp
        _gk = jax.random.key(seed)
        x = -0.0005207 + 1.001 * jax.random.normal(jax.random.fold_in(_gk, 1), (2, 256, 64, 64), jnp.float32)
        return x
    x = _rec_inputs()
    def _L0_conv_setup():
        import jax, jax.numpy as jnp
        import numpy as np
        B, C, H, W = (2, 256, 64, 64)
        NH = 4
        G = 32
        EPS = 1e-05
        key = jax.random.key(seed)
        ks = jax.random.split(key, 7)
        s = 1.0 / np.sqrt(C).astype(np.float32)
        return {'x': jax.random.normal(ks[0], (B, C, H, W), jnp.float32), 'gn_scale': 1.0 + 0.02 * jax.random.normal(ks[1], (C,), jnp.float32), 'gn_bias': 0.02 * jax.random.normal(ks[2], (C,), jnp.float32), 'w_qkv': s * jax.random.normal(ks[3], (3 * C, C), jnp.float32), 'b_qkv': jnp.zeros((3 * C,), jnp.float32), 'w_proj': s * jax.random.normal(ks[4], (C, C), jnp.float32), 'b_proj': jnp.zeros((C,), jnp.float32)}
    _L0_conv_all = _L0_conv_setup()
    _L0_conv_in = {k: v for k, v in _L0_conv_all.items() if k in ('gn_scale', 'gn_bias', 'w_qkv', 'b_qkv', 'w_proj', 'b_proj', )}
    del _L0_conv_all

    def _L1_conv_setup():
        import jax, jax.numpy as jnp
        import numpy as np
        B, C, H, W = (8, 256, 64, 64)
        HEADS, RS = (8, 16)
        D = C // HEADS
        SCALE = 1.0 / D

        def _interp_matrix(n_in, n_out):
            pos = np.arange(n_out) * (n_in - 1) / (n_out - 1)
            i0 = np.floor(pos).astype(np.int64)
            i1 = np.minimum(i0 + 1, n_in - 1)
            w = (pos - i0).astype(np.float32)
            M = np.zeros((n_out, n_in), np.float32)
            M[np.arange(n_out), i0] += 1.0 - w
            M[np.arange(n_out), i1] += w
            return jnp.asarray(M)
        _M = _interp_matrix(H, RS)

        def _rel_pos_index(h, w):
            ch, cw = np.meshgrid(np.arange(h), np.arange(w), indexing='ij')
            coords = np.stack([ch, cw]).reshape(2, -1)
            rel = (coords[:, :, None] - coords[:, None, :]).transpose(1, 2, 0)
            rel[:, :, 0] += h - 1
            rel[:, :, 1] += w - 1
            rel[:, :, 0] *= 2 * h - 1
            return rel.sum(-1)
        _RPI = jnp.asarray(_rel_pos_index(RS, RS).reshape(-1))

        def _batchnorm(x, g, b, eps=1e-05):
            mu = x.mean(axis=(0, 2, 3), keepdims=True)
            var = x.var(axis=(0, 2, 3), keepdims=True)
            return (x - mu) * jax.lax.rsqrt(var + eps) * g[None, :, None, None] + b[None, :, None, None]

        def _dw_sep_conv(x, dw, pw):
            y = jax.lax.conv_general_dilated(x, dw, (1, 1), 'SAME', dimension_numbers=('NCHW', 'OIHW', 'NCHW'), feature_group_count=x.shape[1])
            return jnp.einsum('bchw,oc->bohw', y, pw)

        def _heads_split(t, hh, ww):
            b = t.shape[0]
            return t.reshape(b, D, HEADS, hh, ww).transpose(0, 2, 3, 4, 1).reshape(b, HEADS, hh * ww, D)

        def _per_head_ln(t, g, b, eps=1e-06):
            mu = t.mean(-1, keepdims=True)
            var = ((t - mu) ** 2).mean(-1, keepdims=True)
            return (t - mu) * jax.lax.rsqrt(var + eps) * g[None, :, None, :] + b[None, :, None, :]

        def _rel_pos_bias(table):
            bias = table[_RPI].reshape(RS, RS, RS * RS, HEADS)
            bias = jnp.repeat(bias, H // RS, axis=0)
            bias = jnp.repeat(bias, W // RS, axis=1)
            return bias.reshape(H * W, RS * RS, HEADS).transpose(2, 0, 1)[None]
        key = jax.random.key(seed)
        ks = jax.random.split(key, 8)
        n = lambda i, shape, s=1.0: jax.random.normal(ks[i], shape, dtype=jnp.float32) * s
        return {'x': n(0, (B, C, H, W)), 'bn1_g': jnp.ones((C,), jnp.float32), 'bn1_b': jnp.zeros((C,), jnp.float32), 'qkv_dw': n(1, (C, 1, 3, 3), 0.1), 'qkv_pw': n(2, (3 * C, C), 0.05), 'rel_table': n(3, ((2 * RS - 1) ** 2, HEADS), 0.02), 'nq_g': jnp.ones((HEADS, D), jnp.float32), 'nq_b': jnp.zeros((HEADS, D), jnp.float32), 'nk_g': jnp.ones((HEADS, D), jnp.float32), 'nk_b': jnp.zeros((HEADS, D), jnp.float32), 'out_dw': n(4, (C, 1, 3, 3), 0.1), 'out_pw': n(5, (C, C), 0.05), 'bn2_g': jnp.ones((C,), jnp.float32), 'bn2_b': jnp.zeros((C,), jnp.float32), 'mlp_w': n(6, (C, C), 0.05)}
    _L1_conv_all = _L1_conv_setup()
    _L1_conv_in = {k: v for k, v in _L1_conv_all.items() if k in ('bn1_g', 'bn1_b', 'qkv_dw', 'qkv_pw', 'rel_table', 'nq_g', 'nq_b', 'nk_g', 'nk_b', 'out_dw', 'out_pw', 'bn2_g', 'bn2_b', 'mlp_w', )}
    del _L1_conv_all

    def _L2_conv_setup():
        import jax, jax.numpy as jnp
        import numpy as np
        B, C, H, W = (8, 256, 56, 56)
        R = 2
        E = C // R
        key = jax.random.key(seed)
        ks = jax.random.split(key, 10)
        s = 0.02
        return {'x': jax.random.normal(ks[0], (B, C, H, W), jnp.float32), 'Wq': jax.random.normal(ks[1], (E, C), jnp.float32) * s, 'bq': jax.random.normal(ks[2], (E,), jnp.float32) * s, 'Wk': jax.random.normal(ks[3], (E, C), jnp.float32) * s, 'bk': jax.random.normal(ks[4], (E,), jnp.float32) * s, 'Wv': jax.random.normal(ks[5], (E, C), jnp.float32) * s, 'bv': jax.random.normal(ks[6], (E,), jnp.float32) * s, 'Wcat': jax.random.normal(ks[7], (1, 2 * E), jnp.float32) * s, 'Wexp': jax.random.normal(ks[8], (C, E), jnp.float32) * s, 'bexp': jax.random.normal(ks[9], (C,), jnp.float32) * s}
    _L2_conv_all = _L2_conv_setup()
    _L2_conv_in = {k: v for k, v in _L2_conv_all.items() if k in ('Wq', 'bq', 'Wk', 'bk', 'Wv', 'bv', 'Wcat', 'Wexp', 'bexp', )}
    del _L2_conv_all

    def _L3_conv_setup():
        import jax, jax.numpy as jnp
        import numpy as np
        NUM_GROUPS = 32
        NUM_FEATURES = 256
        EPS = 1e-05
        key = jax.random.key(seed)
        x = jax.random.normal(key, (32, NUM_FEATURES, 64, 64), dtype=jnp.float32)
        gamma = jnp.ones((NUM_FEATURES,), jnp.float32)
        beta = jnp.zeros((NUM_FEATURES,), jnp.float32)
        return {'x': x, 'gamma': gamma, 'beta': beta}
    _L3_conv_all = _L3_conv_setup()
    _L3_conv_in = {k: v for k, v in _L3_conv_all.items() if k in ('gamma', 'beta', )}
    del _L3_conv_all

    return {
        "x": x,
        "L0_conv_gn_scale": _L0_conv_in["gn_scale"],
        "L0_conv_gn_bias": _L0_conv_in["gn_bias"],
        "L0_conv_w_qkv": _L0_conv_in["w_qkv"],
        "L0_conv_b_qkv": _L0_conv_in["b_qkv"],
        "L0_conv_w_proj": _L0_conv_in["w_proj"],
        "L0_conv_b_proj": _L0_conv_in["b_proj"],
        "L1_conv_bn1_g": _L1_conv_in["bn1_g"],
        "L1_conv_bn1_b": _L1_conv_in["bn1_b"],
        "L1_conv_qkv_dw": _L1_conv_in["qkv_dw"],
        "L1_conv_qkv_pw": _L1_conv_in["qkv_pw"],
        "L1_conv_rel_table": _L1_conv_in["rel_table"],
        "L1_conv_nq_g": _L1_conv_in["nq_g"],
        "L1_conv_nq_b": _L1_conv_in["nq_b"],
        "L1_conv_nk_g": _L1_conv_in["nk_g"],
        "L1_conv_nk_b": _L1_conv_in["nk_b"],
        "L1_conv_out_dw": _L1_conv_in["out_dw"],
        "L1_conv_out_pw": _L1_conv_in["out_pw"],
        "L1_conv_bn2_g": _L1_conv_in["bn2_g"],
        "L1_conv_bn2_b": _L1_conv_in["bn2_b"],
        "L1_conv_mlp_w": _L1_conv_in["mlp_w"],
        "L2_conv_Wq": _L2_conv_in["Wq"],
        "L2_conv_bq": _L2_conv_in["bq"],
        "L2_conv_Wk": _L2_conv_in["Wk"],
        "L2_conv_bk": _L2_conv_in["bk"],
        "L2_conv_Wv": _L2_conv_in["Wv"],
        "L2_conv_bv": _L2_conv_in["bv"],
        "L2_conv_Wcat": _L2_conv_in["Wcat"],
        "L2_conv_Wexp": _L2_conv_in["Wexp"],
        "L2_conv_bexp": _L2_conv_in["bexp"],
        "L3_conv_gamma": _L3_conv_in["gamma"],
        "L3_conv_beta": _L3_conv_in["beta"],
    }

def reference(x, L0_conv_gn_scale, L0_conv_gn_bias, L0_conv_w_qkv, L0_conv_b_qkv, L0_conv_w_proj, L0_conv_b_proj, L1_conv_bn1_g, L1_conv_bn1_b, L1_conv_qkv_dw, L1_conv_qkv_pw, L1_conv_rel_table, L1_conv_nq_g, L1_conv_nq_b, L1_conv_nk_g, L1_conv_nk_b, L1_conv_out_dw, L1_conv_out_pw, L1_conv_bn2_g, L1_conv_bn2_b, L1_conv_mlp_w, L2_conv_Wq, L2_conv_bq, L2_conv_Wk, L2_conv_bk, L2_conv_Wv, L2_conv_bv, L2_conv_Wcat, L2_conv_Wexp, L2_conv_bexp, L3_conv_gamma, L3_conv_beta):
    import jax
    import jax.numpy as jnp
    def _L0_conv_ref(x, gn_scale, gn_bias, w_qkv, b_qkv, w_proj, b_proj):
        import jax, jax.numpy as jnp
        import numpy as np
        B, C, H, W = (2, 256, 64, 64)
        NH = 4
        G = 32
        EPS = 1e-05
        b, c = (x.shape[0], x.shape[1])
        spatial = x.shape[2:]
        t = int(np.prod(spatial))
        xf = x.reshape(b, c, t)
        xg = xf.reshape(b, G, c // G, t)
        mu = xg.mean(axis=(2, 3), keepdims=True)
        var = xg.var(axis=(2, 3), keepdims=True)
        xn = ((xg - mu) * jax.lax.rsqrt(var + EPS)).reshape(b, c, t)
        xn = xn * gn_scale[None, :, None] + gn_bias[None, :, None]
        qkv = jnp.einsum('oc,bct->bot', w_qkv, xn) + b_qkv[None, :, None]
        ch = c // NH
        qkv_h = qkv.reshape(b * NH, 3 * ch, t)
        q, k, v = jnp.split(qkv_h, 3, axis=1)
        scale = 1.0 / np.sqrt(np.sqrt(ch)).astype(np.float32)
        w = jnp.einsum('bct,bcs->bts', q * scale, k * scale)
        w = jax.nn.softmax(w.astype(jnp.float32), axis=-1).astype(qkv.dtype)
        a = jnp.einsum('bts,bcs->bct', w, v).reshape(b, c, t)
        h = jnp.einsum('oc,bct->bot', w_proj, a) + b_proj[None, :, None]
        return (xf + h).reshape(b, c, *spatial)

    def _L1_conv_ref(x, bn1_g, bn1_b, qkv_dw, qkv_pw, rel_table, nq_g, nq_b, nk_g, nk_b, out_dw, out_pw, bn2_g, bn2_b, mlp_w):
        import jax, jax.numpy as jnp
        import numpy as np
        B, C, H, W = (8, 256, 64, 64)
        HEADS, RS = (8, 16)
        D = C // HEADS
        SCALE = 1.0 / D

        def _interp_matrix(n_in, n_out):
            pos = np.arange(n_out) * (n_in - 1) / (n_out - 1)
            i0 = np.floor(pos).astype(np.int64)
            i1 = np.minimum(i0 + 1, n_in - 1)
            w = (pos - i0).astype(np.float32)
            M = np.zeros((n_out, n_in), np.float32)
            M[np.arange(n_out), i0] += 1.0 - w
            M[np.arange(n_out), i1] += w
            return jnp.asarray(M)
        _M = _interp_matrix(H, RS)

        def _rel_pos_index(h, w):
            ch, cw = np.meshgrid(np.arange(h), np.arange(w), indexing='ij')
            coords = np.stack([ch, cw]).reshape(2, -1)
            rel = (coords[:, :, None] - coords[:, None, :]).transpose(1, 2, 0)
            rel[:, :, 0] += h - 1
            rel[:, :, 1] += w - 1
            rel[:, :, 0] *= 2 * h - 1
            return rel.sum(-1)
        _RPI = jnp.asarray(_rel_pos_index(RS, RS).reshape(-1))

        def _batchnorm(x, g, b, eps=1e-05):
            mu = x.mean(axis=(0, 2, 3), keepdims=True)
            var = x.var(axis=(0, 2, 3), keepdims=True)
            return (x - mu) * jax.lax.rsqrt(var + eps) * g[None, :, None, None] + b[None, :, None, None]

        def _dw_sep_conv(x, dw, pw):
            y = jax.lax.conv_general_dilated(x, dw, (1, 1), 'SAME', dimension_numbers=('NCHW', 'OIHW', 'NCHW'), feature_group_count=x.shape[1])
            return jnp.einsum('bchw,oc->bohw', y, pw)

        def _heads_split(t, hh, ww):
            b = t.shape[0]
            return t.reshape(b, D, HEADS, hh, ww).transpose(0, 2, 3, 4, 1).reshape(b, HEADS, hh * ww, D)

        def _per_head_ln(t, g, b, eps=1e-06):
            mu = t.mean(-1, keepdims=True)
            var = ((t - mu) ** 2).mean(-1, keepdims=True)
            return (t - mu) * jax.lax.rsqrt(var + eps) * g[None, :, None, :] + b[None, :, None, :]

        def _rel_pos_bias(table):
            bias = table[_RPI].reshape(RS, RS, RS * RS, HEADS)
            bias = jnp.repeat(bias, H // RS, axis=0)
            bias = jnp.repeat(bias, W // RS, axis=1)
            return bias.reshape(H * W, RS * RS, HEADS).transpose(2, 0, 1)[None]
        h = _batchnorm(x, bn1_g, bn1_b)
        qkv = _dw_sep_conv(h, qkv_dw, qkv_pw)
        q, k, v = jnp.split(qkv, 3, axis=1)
        k = jnp.einsum('bcij,oi,pj->bcop', k, _M, _M)
        v = jnp.einsum('bcij,oi,pj->bcop', v, _M, _M)
        q = _per_head_ln(_heads_split(q, H, W), nq_g, nq_b)
        k = _per_head_ln(_heads_split(k, RS, RS), nk_g, nk_b)
        v = _heads_split(v, RS, RS)
        attn = jnp.einsum('bhid,bhjd->bhij', q, k)
        attn = (attn + _rel_pos_bias(rel_table)) * SCALE
        o = jnp.einsum('bhij,bhjd->bhid', attn, v)
        o = o.reshape(x.shape[0], HEADS, H, W, D).transpose(0, 4, 1, 2, 3).reshape(x.shape[0], C, H, W)
        o = _dw_sep_conv(o, out_dw, out_pw)
        out = o + x
        res = out
        out = jax.nn.relu(_batchnorm(out, bn2_g, bn2_b))
        out = jnp.einsum('bchw,oc->bohw', out, mlp_w)
        return out + res

    def _L2_conv_ref(x, Wq, bq, Wk, bk, Wv, bv, Wcat, Wexp, bexp):
        import jax, jax.numpy as jnp
        import numpy as np
        B, C, H, W = (8, 256, 56, 56)
        R = 2
        E = C // R
        b, c, h, w = x.shape
        n = h * w
        xf = x.reshape(b, c, n)
        q = jnp.einsum('ec,bcn->ben', Wq, xf) + bq[None, :, None]
        k = jnp.einsum('ec,bcn->ben', Wk, xf) + bk[None, :, None]
        v = jnp.einsum('ec,bcn->bne', Wv, xf) + bv[None, None, :]
        wq_c, wk_c = (Wcat[0, :E], Wcat[0, E:])
        s = jax.nn.relu(jnp.einsum('e,ben->bn', wq_c, q) + jnp.einsum('e,ben->bn', wk_c, k))
        attn = jnp.broadcast_to(s[:, :, None], (b, n, n)) / n
        embed = jnp.einsum('bij,bje->bie', attn, v)
        out = jnp.einsum('ce,bne->bcn', Wexp, embed) + bexp[None, :, None]
        return out.reshape(b, c, h, w) + x

    def _L3_conv_ref(x, gamma, beta):
        import jax, jax.numpy as jnp
        import numpy as np
        NUM_GROUPS = 32
        NUM_FEATURES = 256
        EPS = 1e-05
        B, C, H, W = x.shape
        k = NUM_FEATURES // NUM_GROUPS
        x_flat = x.reshape(B, C, H * W)
        nrm = jnp.linalg.norm(x_flat, axis=2, keepdims=True)
        x_n = x_flat / jnp.maximum(nrm, 1e-12)
        cos = jnp.einsum('bcn,bdn->cd', x_n, x_n) / B
        _, idx = jax.lax.top_k(-jnp.abs(cos).T, k)
        s = x.sum(axis=(2, 3))
        sq = (x * x).sum(axis=(2, 3))
        gs = s + s[:, idx[:, 1:]].sum(axis=-1)
        gsq = sq + sq[:, idx[:, 1:]].sum(axis=-1)
        N = k * H * W
        mean = gs / N
        var = gsq / N - mean * mean
        inv = jax.lax.rsqrt(var + EPS)
        x_hat = (x - mean[:, :, None, None]) * inv[:, :, None, None]
        return gamma[None, :, None, None] * x_hat + beta[None, :, None, None]

    def _gn(v, G=32, eps=1e-5):
        B_, C_, H_, W_ = v.shape
        g = v.reshape(B_, G, C_ // G, H_, W_)
        m = jnp.mean(g, axis=(2, 3, 4), keepdims=True)
        s = jnp.var(g, axis=(2, 3, 4), keepdims=True)
        return ((g - m) / jnp.sqrt(s + eps)).reshape(v.shape)

    def _ln_c(v, eps=1e-6):
        m = jnp.mean(v, axis=1, keepdims=True)
        s = jnp.var(v, axis=1, keepdims=True)
        return (v - m) / jnp.sqrt(s + eps)

    def _ln_t(v, eps=1e-5):
        m = jnp.mean(v, axis=-1, keepdims=True)
        s = jnp.var(v, axis=-1, keepdims=True)
        return (v - m) / jnp.sqrt(s + eps)

    def _to_tokens(v):
        B_, C_, H_, W_ = v.shape
        return v.reshape(B_, C_, H_ * W_).transpose(0, 2, 1)
    def _from_tokens(t, like):
        B_, C_, H_, W_ = like.shape
        return t.transpose(0, 2, 1).reshape(B_, C_, H_, W_)

    x = _L0_conv_ref(x, L0_conv_gn_scale, L0_conv_gn_bias, L0_conv_w_qkv, L0_conv_b_qkv, L0_conv_w_proj, L0_conv_b_proj)
    x = _L1_conv_ref(x, L1_conv_bn1_g, L1_conv_bn1_b, L1_conv_qkv_dw, L1_conv_qkv_pw, L1_conv_rel_table, L1_conv_nq_g, L1_conv_nq_b, L1_conv_nk_g, L1_conv_nk_b, L1_conv_out_dw, L1_conv_out_pw, L1_conv_bn2_g, L1_conv_bn2_b, L1_conv_mlp_w)
    x = _L2_conv_ref(x, L2_conv_Wq, L2_conv_bq, L2_conv_Wk, L2_conv_bk, L2_conv_Wv, L2_conv_bv, L2_conv_Wcat, L2_conv_Wexp, L2_conv_bexp)
    x = _L3_conv_ref(x, L3_conv_gamma, L3_conv_beta)
    return x


_drawn_inputs = setup_inputs


def setup_inputs(seed=0):
    import zlib

    import numpy as np

    out = dict(_drawn_inputs(seed))
    spreads = {'L0_conv_b_qkv': (0.0, 0.1),
     'L0_conv_b_proj': (0.0, 0.1),
     'L1_conv_bn1_g': (1.0, 0.2),
     'L1_conv_bn1_b': (0.0, 0.1),
     'L1_conv_nq_g': (1.0, 0.2),
     'L1_conv_nq_b': (0.0, 0.1),
     'L1_conv_nk_g': (1.0, 0.2),
     'L1_conv_nk_b': (0.0, 0.1),
     'L1_conv_bn2_g': (1.0, 0.2),
     'L1_conv_bn2_b': (0.0, 0.1),
     'L3_conv_gamma': (1.0, 0.2),
     'L3_conv_beta': (0.0, 0.1)}
    factors = {'L1_conv_rel_table': 15.207,
     'L2_conv_Wq': 4.54,
     'L2_conv_bq': 7.532,
     'L2_conv_bk': 5.235,
     'L2_conv_bv': 3.866,
     'L2_conv_Wcat': 3.138}
    for name, (base, spread) in spreads.items():
        noise = np.random.default_rng([zlib.crc32(name.encode()), seed]).standard_normal(out[name].shape)
        drawn = base * np.exp(spread * noise) if base else spread * noise
        out[name] = jnp.asarray(drawn.astype(out[name].dtype))
    for name, factor in factors.items():
        out[name] = (out[name] * factor).astype(out[name].dtype)
    return out
```

```python
from contextlib import ExitStack

import concourse.bass as bass
from concourse import mybir

F32 = mybir.dt.float32
BF16 = mybir.dt.bfloat16
U32 = mybir.dt.uint32
ALU = mybir.AluOpType
ACT = mybir.ActivationFunctionType
AX = mybir.AxisListType
ds = bass.ds

P = 128
B, C, IMG = 2, 256, 64
HW = IMG * IMG
KT = C // P
TB = 512
NTB = HW // TB

NH, DH = 4, 64
QKV = 3 * DH
V_COL = 2 * DH * NH
EPS_GN = 1e-5
GROUP0 = C // 32
SCALE0 = 1.0 / DH ** 0.5
NPAIR = HW // (2 * P)
POOL_PAIRS = 12
DVE_PAIRS = NPAIR - POOL_PAIRS
NBUF = 4
SUBS = TB // P
UNITS = SUBS * NTB
PER_SLOT = 3


def unit_slots():
    slots, u = [[] for _ in range(NPAIR)], 0
    for j in range(1, NPAIR):
        while u < UNITS and len(slots[j]) < PER_SLOT:
            slots[j].append(u)
            u += 1
    return slots


SLOTS = unit_slots()
LAST_UNIT_SLOT = max(j for j in range(NPAIR) if SLOTS[j])
assert SLOTS[LAST_UNIT_SLOT][-1] == UNITS - 1 and LAST_UNIT_SLOT + 2 < NPAIR
TURN_SLOT = LAST_UNIT_SLOT + 2
assert TURN_SLOT <= NPAIR - 2

SUM_SLOT, INV_SLOT = 2, 3
PROJ_SLOTS = (5, 7)
LO_ROW = 32
PARTS = 4
CONSTS = 6
assert max(PROJ_SLOTS) < TURN_SLOT

HEADS1, RS = 8, 16
D1 = C // HEADS1
NKEY = RS * RS
JT = NKEY // P
REP = IMG // RS
TABLE = 2 * RS - 1
ROWS = TB // IMG
PAD = IMG + 2
TAPS = [(dy, dx) for dy in range(3) for dx in range(3)]
PE_TAPS = 3
DVE_TAPS = len(TAPS) - PE_TAPS
EPS_BN = 1e-5
EPS_LN = 1e-6
RATIO = (IMG - 1) / (RS - 1)
PERIOD = 5
PERIOD_ROWS = int(PERIOD * RATIO)
GROUPS = RS // PERIOD
assert PERIOD_ROWS == PERIOD * RATIO and GROUPS * PERIOD + 1 == RS and GROUPS * PERIOD_ROWS + 1 == IMG
E2 = C // 2
NSEL = C // 32
EPS_L3 = 1e-5
BIAS_RUN = (RS - 1) * TABLE + RS + (P // RS) * TABLE


VEC_NAMES = {"gn_scale": KT, "gn_bias": KT, "b_qk": NH, "b_v": KT, "b_proj": KT,
             "bn1_g": KT, "bn1_b": KT, "dw1": KT * 9, "dw2": KT * 9, "nq_g": KT, "nq_b": KT, "bn2_g": KT,
             "bn2_b": KT, "bexp": KT, "bq": 1, "bk": 1, "bv": 1, "wq_c": 1, "wk_c": 1, "gamma": KT, "beta": KT}
VEC, NVEC = {}, 0
for _name, _n in VEC_NAMES.items():
    VEC[_name] = NVEC
    NVEC += _n


ARENA_WORDS = 36200


def np_f32(v):
    import numpy as np
    return float(np.float32(v))


def build(nc, x, w_qkv_t, w_proj_t, vectors, w1_t, w_out_t, mlp_t, k_norm, rel_table, w2_qk, w2_v_t, w2_exp_t, out):
    ctx = ExitStack()
    with ctx:
        def sb(name, shape, dt=F32):
            return ctx.enter_context(nc.sbuf_tensor(name, shape, dt))

        def sem(name):
            return ctx.enter_context(nc.semaphore(name))

        X = sb("X", [P, B, KT, HW])
        vec = sb("vec", [P, NVEC])
        ident = sb("ident", [P, P])
        ones = sb("ones", [P, P])
        mean8 = sb("mean8", [P, P])
        mean32 = sb("mean32", [P, P])
        eps = sb("eps", [P, 2])

        def col(name, k=0, n=1):
            return vec[:, VEC[name] + k:VEC[name] + k + n]

        arena = sb("arena", [P, ARENA_WORDS])

        def carver(start, end):
            at = [start]

            def take(shape, dt=F32):
                n = 1
                for d in shape[1:]:
                    n *= d
                words = (n + 1) // 2 if dt == BF16 else n
                assert at[0] + words <= end, (at, words, end)
                tile = arena[0:shape[0], at[0]:at[0] + words]
                at[0] += words
                if dt != F32:
                    tile = tile.bitcast(dt)[:, 0:n]
                if len(shape) > 2:
                    names = " ".join("abcdef"[:len(shape) - 1])
                    tile = tile.rearrange(f"p ({names}) -> p {names}",
                                          **{c: d for c, d in zip("abcdef", shape[1:])})
                return tile
            return take

        early = carver(0, ARENA_WORDS)
        late = carver(0, ARENA_WORDS)

        Y = early([P, KT, HW])
        q_hh = early([P, HW], BF16)
        k_hl = early([P, HW], BF16)
        q_lm = early([P, HW], BF16)
        k_h1 = early([P, HW], BF16)
        v_sb = early([P, HW // P, DH])
        prob = early([P, NBUF, 2, TB])
        acc_pool = early([P, 2, TB])
        acc_dve = early([P, 2, TB])
        pool_total = early([P, TB])
        total = early([P, TB])
        inv_cols = early([P, SUBS])
        o_raw = early([P, TB])
        o_norm = early([P, TB])
        wqkv = early([P, KT, NH * QKV])
        wproj = early([P, KT, C])
        wproj2 = early([P, NH, C])
        w_head = early([P, KT, QKV])
        wp_head = early([P, C])
        b_head = early([P, 1])
        stats = early([P, KT, NTB, 6])
        mv = early([P, KT, 2])
        gn = early([P, 8, KT])
        b_qk = early([P, NH])
        b_v = early([P, KT])
        b_out = early([P, KT])
        part_max = early([P, SUBS, NTB])
        neg_max = early([P, SUBS])
        max_cols = early([P, SUBS, LO_ROW + 1], BF16)
        ident_bf = early([P, P], BF16)

        H = late([P, KT, PAD, PAD])
        Z = late([P, KT, HW])
        w1 = late([P, KT, 3 * C])
        w_out = late([P, KT, C])
        w_mlp = late([P, KT, C])
        k_gb = late([P, 2, C])
        table = late([P, HEADS1, BIAS_RUN + TABLE - RS])
        diag = late([P, 2, KT, PE_TAPS, P])
        stats1 = late([P, KT, B, NTB, 6])
        mv1 = late([P, KT, 2])
        bn = late([P, 4, KT])
        q_mean = late([P, KT, HEADS1])
        rows_n, part_n = KT * RS * IMG, KT * (PERIOD - 1) * GROUPS * IMG
        shared = late([P, rows_n + part_n])
        rows_i = shared[:, 0:rows_n].rearrange("p (k r c) -> p k r c", k=KT, r=RS)
        part_i = shared[:, rows_n:].rearrange("p (k r c) -> p k r c", k=KT, r=PERIOD - 1)
        zi = late([P, KT, NKEY])
        z_rev = late([P, KT, NKEY])
        kn = late([P, JT, C])
        vv = late([P, JT, C])
        k_sq = shared[:, 0:C]
        k_st = late([P, 4, HEADS1])
        kv = late([P, KT, P])
        kvg = late([P, KT, P])
        kv_c = late([P, KT])
        bias_v = late([P, KT, NKEY])
        q_sq = shared[:, 0:1 * KT * TB].rearrange("p (k n) -> p k n", k=KT)
        q_rs = shared[:, 1 * KT * TB:2 * KT * TB].rearrange("p (k n) -> p k n", k=KT)
        q_n = shared[:, 2 * KT * TB:3 * KT * TB].rearrange("p (k n) -> p k n", k=KT)
        spare, used = Z[:, :, :].rearrange("p k n -> p (k n)"), [0]

        def carve(n, *names, **sizes):
            used[0] += n
            part = spare[:, used[0] - n:used[0]]
            return part.rearrange(f"p ({' '.join(names)}) -> p {' '.join(names)}", **sizes) if names else part

        w2q = late([P, 2, C])
        w2v = late([P, KT, E2])
        w2e = late([P, C])
        u_all = carve(KT * P, "k", "c", k=KT)
        u_col = late([P, KT])
        b2all = carve(2 * P, "k", "c", k=2)
        c2 = late([P, 4])
        relu_h = carve(KT * TB, "k", "n", k=KT)
        xsum = late([P, B, KT, NTB])
        xs = late([P, B, KT])
        v_sum = late([P, B])
        mixed = late([P, B, KT])
        s_relu = carve(TB)
        sums3 = late([P, 2, B, KT, NTB])
        tot3 = late([P, KT, 2, B])
        junk = carve(TB)
        xt = carve(4 * C, "r", "c", r=4)
        inv3 = late([P, B, KT])
        gram_s = carve(KT * C, "k", "c", k=KT)
        cos = carve(KT * C, "k", "c", k=KT)
        top = late([P, KT, 8])
        top_i = late([P, KT, 8], U32)
        top_f = late([P, KT, 8])
        count = late([P, C])
        pick = carve(KT * C, "k", "c", k=KT)
        pick_t = carve(KT * C, "k", "c", k=KT)
        g3 = late([P, KT, 2, B])
        st3 = late([P, 6, KT, B])

        st = [ctx.enter_context(nc.psum_tensor(f"st{i}", [P, 2, TB], F32)) for i in range(2)]
        mx = [ctx.enter_context(nc.psum_tensor(f"mx{i}", [P, TB], F32)) for i in range(2)]
        pvo = ctx.enter_context(nc.psum_tensor("pvo", [P, TB], F32))
        misc = ctx.enter_context(nc.psum_tensor("misc", [P, TB], F32))
        bank = [st[0][:, 0, :], st[0][:, 1, :], st[1][:, 0, :], st[1][:, 1, :], mx[0][:, :], mx[1][:, :],
                pvo[:, :], misc[:, :]]

        consts_ready = sem("consts_ready")
        ident_ready = sem("ident_ready")
        x_loaded = [sem(f"x_loaded{b}") for b in range(B)]
        weights_loaded = sem("weights_loaded")
        pool_chain = sem("pool_chain")
        dve_chain = sem("dve_chain")
        ch_mean_ready = sem("ch_mean_ready")
        group_mean_ready = sem("group_mean_ready")
        ch_spread_ready = sem("ch_spread_ready")
        group_var_ready = sem("group_var_ready")
        sd_ready = sem("sd_ready")
        affine_ready = sem("affine_ready")
        bias_ready = sem("bias_ready")
        bv_ready = sem("bv_ready")
        out_bias_ready = sem("out_bias_ready")
        y_init = sem("y_init")
        head_w_ready = sem("head_w_ready")
        head_wp_ready = sem("head_wp_ready")
        qk_ready = sem("qk_ready")
        hi_done = sem("hi_done")
        lo_done = sem("lo_done")
        v_ready = sem("v_ready")
        v_copied = sem("v_copied")
        mx_ready = sem("mx_ready")
        mx_free = sem("mx_free")
        neg_max_ready = sem("neg_max_ready")
        max_turned = sem("max_turned")
        max_hi_ready = sem("max_hi_ready")
        max_cols_ready = sem("max_cols_ready")
        max_row_ready = sem("max_row_ready")
        st_ready = sem("st_ready")
        exp_done = sem("exp_done")
        pv_done = sem("pv_done")
        pool_sums = sem("pool_sums")
        dve_sums = sem("dve_sums")
        pool_total_ready = sem("pool_total_ready")
        dve_folded = sem("dve_folded")
        total_ready = sem("total_ready")
        total_turned = sem("total_turned")
        inv_ready = sem("inv_ready")
        inv_spread = sem("inv_spread")
        o_copied = sem("o_copied")
        o_norm_ready = sem("o_norm_ready")
        proj_ready = sem("proj_ready")
        y_added = sem("y_added")
        layer0_done = sem("layer0_done")

        weights1_loaded = sem("weights1_loaded")
        table_loaded = sem("table_loaded")
        pool1_chain = sem("pool1_chain")
        dve1_chain = sem("dve1_chain")
        var1_ready = sem("var1_ready")
        sd1_ready = sem("sd1_ready")
        affine1_ready = sem("affine1_ready")
        border_ready = sem("border_ready")
        diag_ready = sem("diag_ready")
        wq1_ready = sem("wq1_ready")
        h_ready = sem("h_ready")
        conv_part = sem("conv_part")
        conv_taken = sem("conv_taken")
        conv_step = sem("conv_step")
        zi_ready = sem("zi_ready")
        kv_ready = sem("kv_ready")
        v_got = sem("v_got")
        k_var_ready = sem("k_var_ready")
        k_sd_ready = sem("k_sd_ready")
        kn_ready = sem("kn_ready")
        kk_ready = sem("kk_ready")
        kvm_ready = sem("kvm_ready")
        kvc_ready = sem("kvc_ready")
        bias_part = sem("bias_part")
        bias_v_ready = sem("bias_v_ready")
        q_ready = sem("q_ready")
        q_sq_ready = sem("q_sq_ready")
        q_var_ready = sem("q_var_ready")
        q_ln_done = sem("q_ln_done")
        q_rs_ready = sem("q_rs_ready")
        q_n_ready = sem("q_n_ready")
        o_ready = sem("o_ready")
        o_placed = sem("o_placed")
        pw_ready = sem("pw_ready")
        x_added = sem("x_added")
        mlp_in = sem("mlp_in")
        mlp_ready = sem("mlp_ready")
        mlp_added = sem("mlp_added")
        l2_a = sem("l2_a")
        l2_b = sem("l2_b")
        mix_a = sem("mix_a")
        mix_b = sem("mix_b")
        gate_ready = sem("gate_ready")
        s_relu_ready = sem("s_relu_ready")
        x3_ready = sem("x3_ready")
        sq3_ready = sem("sq3_ready")
        turned3 = sem("turned3")
        xt_ready = sem("xt_ready")
        gram_ready = sem("gram_ready")
        norm3_ready = sem("norm3_ready")
        nrm3_ready = sem("nrm3_ready")
        gram_scaled = sem("gram_scaled")
        gram_turned = sem("gram_turned")
        cos_added = sem("cos_added")
        pick_ready = sem("pick_ready")
        pick_turned = sem("pick_turned")
        pick_t_ready = sem("pick_t_ready")
        group_sums = sem("group_sums")
        var3_ready = sem("var3_ready")
        sd3_ready = sem("sd3_ready")
        affine3_ready = sem("affine3_ready")
        out_ready = [sem(f"out_ready{k}") for k in range(KT)]
        stored = sem("stored")

        def exps(g, j):
            return g * NPAIR + (j + 1)

        def pvs(g, j):
            return g * NPAIR + (j + 1 + NBUF)

        def pool_summed(g, j):
            return g * POOL_PAIRS + (POOL_PAIRS + j + 1)

        def dve_summed(g, j):
            return g * DVE_PAIRS + (DVE_PAIRS + j + 1)

        def convs(n, i):
            return (i + n * NTB) * KT

        def conv_steps(n, i):
            return (i + n * NTB) * (KT * (DVE_TAPS - 1))

        x_t = x.rearrange("b (k p) h w -> b p k (h w)", p=P)
        out_t = out.rearrange("b (k p) h w -> b p k (h w)", p=P)
        block = ctx.enter_context(nc.Block())

        @block.sync
        def _(sp):
            sp.dma_start(vec[:, :], vectors).then_inc(weights_loaded, 16)
            for b in range(B):
                for k in range(KT):
                    sp.dma_start(X[:, b, k, :], x_t[b, :, k, :]).then_inc(x_loaded[b], 16)
                if b == 0:
                    sp.dma_start(wqkv[:, :, :], w_qkv_t.rearrange("(k p) o -> p k o", p=P)).then_inc(weights_loaded, 16)
                    sp.dma_start(wproj[:, :, :], w_proj_t.rearrange("(k p) o -> p k o", p=P)).then_inc(weights_loaded, 16)
                    for half in range(2):
                        sp.dma_start(wproj2[half * DH:(half + 1) * DH, :, :],
                                     w_proj_t.rearrange("(h d) o -> d h o", d=DH)).then_inc(weights_loaded, 16)

            def load_weights():
                for dst, src in ((w1, w1_t), (w_out, w_out_t), (w_mlp, mlp_t), (w2v, w2_v_t)):
                    sp.dma_start(dst[:, :, :], src.rearrange("(k p) o -> p k o", p=P)).then_inc(weights1_loaded, 16)
                sp.dma_start(k_gb[:, :, :], k_norm).then_inc(weights1_loaded, 16)
                sp.dma_start(w2q[:, :, :], w2_qk).then_inc(weights1_loaded, 16)
                sp.dma_start(w2e[:, :], w2_exp_t).then_inc(weights1_loaded, 16)

            def load_table():
                for r in range(P // RS):
                    first = rel_table[:, r * TABLE:r * TABLE + BIAS_RUN]
                    src = bass.AP(first.tensor, first.offset, [[1, RS], [TABLE * TABLE, HEADS1], [1, BIAS_RUN]])
                    sp.dma_start(table[r * RS:(r + 1) * RS, :, 0:BIAS_RUN], src).then_inc(table_loaded, 16)

            def store_out():
                for b in range(B):
                    for k in range(KT):
                        sp.wait_ge(out_ready[k], b + 1)
                        sp.dma_start(out_t[b, :, k, :], X[:, b, k, :]).then_inc(stored, 16)
                sp.wait_ge(stored, 16 * B * KT)

            sp.wait_ge(layer0_done, B)
            load_weights()
            load_table()
            store_out()

        @block.gpsimd
        def _(pool):
            pool.memset(eps[:, 0:1], EPS_BN).then_inc(consts_ready, 1)
            pool.memset(eps[:, 1:2], EPS_LN).then_inc(consts_ready, 1)
            pool.memset(ones[:, :], 1.0).then_inc(consts_ready, 1)
            pool.memset(ident[:, :], 0.0).then_inc(pool_chain, 1)
            pool.memset(mean8[:, :], 1.0 / GROUP0).then_inc(pool_chain, 1)
            pool.memset(mean32[:, :], 1.0 / 32).then_inc(pool_chain, 1)
            pool.wait_ge(pool_chain, 3)
            pool.affine_select(out=ident[:, :], in_=ident[:, :], compare_op=ALU.not_equal, fill=1.0,
                               base=0, pattern=[[-1, P]], channel_multiplier=1).then_inc(ident_ready, 1)
            chain = 3
            for m, n in ((mean8, GROUP0), (mean32, 32)):
                blocks = m[:, :].rearrange("p (a c) -> p a c", c=n)
                pool.affine_select(out=blocks, in_=blocks, compare_op=ALU.is_ge, fill=0.0, base=0,
                                   pattern=[[-n, P // n], [0, n]], channel_multiplier=1).then_inc(pool_chain, 1)
                chain += 1
                pool.wait_ge(pool_chain, chain)
                pool.affine_select(out=blocks, in_=blocks, compare_op=ALU.is_ge, fill=0.0, base=n - 1,
                                   pattern=[[n, P // n], [0, n]], channel_multiplier=-1).then_inc(consts_ready, 1)

            def later_constants():
                pool.wait_ge(consts_ready, CONSTS)
                for n, name in enumerate(("dw1", "dw2")):
                    for k in range(KT):
                        for t in range(PE_TAPS):
                            pool.tensor_scalar(diag[:, n, k, t, :], ident[:, :], col(name, k * 9 + t), 0.0,
                                               ALU.mult, ALU.add).then_inc(diag_ready, 1)
                pool.iota(count[:, :], pattern=[[1, C]], base=0, channel_multiplier=0,
                          allow_small_or_imprecise_dtypes=True).then_inc(diag_ready, 1)

            pool.sem_inc(pool_sums, POOL_PAIRS)
            pool.sem_inc(pool_total_ready, 1)

            def sums(g):
                for j in range(1, POOL_PAIRS):
                    pool.wait_ge(exp_done, exps(g, j))
                    if j == 1:
                        pool.wait_ge(pool_total_ready, g + 1)
                        pool.tensor_tensor(acc_pool[:, :, :], prob[:, 0, :, :], prob[:, 1, :, :],
                                           ALU.add).then_inc(pool_sums, 2)
                    else:
                        pool.wait_ge(pool_sums, pool_summed(g, j - 1))
                        pool.tensor_tensor(acc_pool[:, :, :], acc_pool[:, :, :], prob[:, j % NBUF, :, :],
                                           ALU.add).then_inc(pool_sums, 1)
                pool.wait_ge(pool_sums, pool_summed(g, POOL_PAIRS - 1))
                pool.tensor_tensor(pool_total[:, :], acc_pool[:, 0, :], acc_pool[:, 1, :],
                                   ALU.add).then_inc(pool_total_ready, 1)

            for b in range(B):
                with pool.Fori(0, NH) as h:
                    hh = h + b * NH
                    pool.wait_ge(y_added, hh * (NTB * KT) + KT)
                    pool.wait_ge(weights_loaded, 16 * 5)
                    pool.tensor_copy(wp_head[:, :], wproj2[:, ds(h, 1), :].rearrange("p a o -> p (a o)"))\
                        .then_inc(head_wp_ready, 1)
                    with pool.Fori(0, NTB) as tb:
                        sums(hh * NTB + tb)
            pool.wait_ge(layer0_done, B)
            pool.memset(H[:, :, :, :], 0.0).then_inc(border_ready, 1)
            later_constants()

        @block.scalar
        def _(act):
            def attention_layer():
                def prepare(hh):
                    act.wait_ge(head_w_ready, hh + 1)
                    q, k = slice(0, DH), slice(DH, P)
                    for i in range(NTB):
                        cols = slice(i * TB, (i + 1) * TB)
                        act.wait_ge(qk_ready, hh * NTB + (i + 1))
                        for dst, half in ((q_hh[q, cols], q), (k_hl[k, cols], k), (q_hh[k, cols], q), (k_h1[k, cols], k)):
                            act.activation(dst, st[i // 2 % 2][half, i % 2, :], ACT.Identity,
                                           bias=b_head[half, 0:1]).then_inc(hi_done, 1)
                        act.wait_ge(v_ready, hh * NTB + (i + 1))
                        act.activation(v_sb[:, SUBS * i:SUBS * (i + 1), :],
                                       pvo[:, 0:SUBS * DH].rearrange("p (s d) -> p s d", d=DH),
                                       ACT.Copy).then_inc(v_copied, 1)

                def max_row(g, tb):
                    act.wait_ge(max_turned, g + 1)
                    act.activation(q_lm[0:LO_ROW + 1, ds(tb * TB, TB)], misc[0:LO_ROW + 1, :], ACT.Copy)\
                        .then_inc(max_row_ready, 1)

                def copy_out(g):
                    act.wait_ge(pv_done, pvs(g, NPAIR - 1))
                    act.activation(o_raw[:, :], pvo[:, :], ACT.Copy).then_inc(o_copied, 1)

                def step(g, tb, tail, turn):
                    for j in range(NPAIR):
                        act.wait_ge(st_ready, exps(g, j))
                        act.wait_ge(pv_done, g * NPAIR + (j + 1))
                        if j >= NBUF:
                            act.wait_ge(pool_sums, pool_summed(g, j - NBUF))
                        else:
                            act.wait_ge(dve_sums, g * DVE_PAIRS + (j + 1))
                        act.activation(prob[:, j % NBUF, :, :], st[j % 2][:, :, :], ACT.Exp,
                                       scale=SCALE0).then_inc(exp_done, 1)
                        if j == 0 and tail:
                            copy_out(g + (-1))
                        if turn and j == TURN_SLOT:
                            max_row(g + 1, tb + 1)

                act.wait_ge(consts_ready, CONSTS)
                act.sem_inc(o_copied, 1)
                for b in range(B):
                    act.wait_ge(group_var_ready, b + 1)
                    act.activation(gn[:, 3, :], misc[:, 4:4 + KT], ACT.Sqrt, bias=eps[:, 0:1]).then_inc(sd_ready, 1)
                    with act.Fori(0, NH) as h:
                        hh = h + b * NH
                        prepare(hh)
                        max_row(hh * NTB, 0)
                        step(hh * NTB, 0, tail=False, turn=True)
                        with act.Fori(1, NTB - 1) as tb:
                            step(hh * NTB + tb, tb, tail=True, turn=True)
                        step(hh * NTB + (NTB - 1), NTB - 1, tail=True, turn=False)
                        copy_out(hh * NTB + (NTB - 1))

            def later_layers():
                def sqrt_of(dst, src, e):
                    return act.activation(dst, src, ACT.Sqrt, bias=eps[:, e:e + 1])

                def fill_h(b):
                    if b > 0:
                        act.wait_ge(conv_step, conv_steps(2 * b, 0))
                        act.wait_ge(conv_part, convs(2 * b, 0))
                    for k in range(KT):
                        act.activation(H[:, k, 1:1 + IMG, 1:1 + IMG],
                                       X[:, b, k, :].rearrange("p (r c) -> p r c", c=IMG), ACT.Identity,
                                       scale=bn[:, 2, k:k + 1], bias=bn[:, 3, k:k + 1]).then_inc(h_ready, 1)

                def keys(b):
                    for j in range(JT):
                        act.wait_ge(kv_ready, b * JT + j + 1)
                        act.activation(vv[:, j, :], bank[4 + j][:, C:2 * C], ACT.Copy).then_inc(v_got, 1)
                    for j in range(JT):
                        act.wait_ge(k_var_ready, b * JT + j + 1)
                        sqrt_of(k_st[:, 2, :], k_st[:, 1, :], 1).then_inc(k_sd_ready, 1)

                def queries(b):
                    with act.Fori(0, NTB) as i:
                        n = (i + b * NTB) * KT
                        for m in range(KT):
                            act.wait_ge(q_ready, n + (m + 1))
                            act.activation(q_sq[:, m, :], bank[m][:, :], ACT.Square).then_inc(q_sq_ready, 1)
                        for m in range(KT):
                            act.wait_ge(q_var_ready, n + (m + 1))
                            act.activation(q_rs[:, m, :], bank[2 + m][:, :], ACT.Ln, bias=eps[:, 1:2])\
                                .then_inc(q_ln_done, 1)
                            act.wait_ge(q_ln_done, n + (m + 1))
                            act.activation(q_rs[:, m, :], q_rs[:, m, :], ACT.Exp, scale=-0.5).then_inc(q_rs_ready, 1)

                def layer1():
                    act.wait_ge(var1_ready, 1)
                    sqrt_of(bn[:, 0, :], mv1[:, :, 1], 0).then_inc(sd1_ready, 1)
                    act.wait_ge(affine1_ready, 1)
                    act.wait_ge(border_ready, 1)
                    for b in range(B):
                        fill_h(b)
                        keys(b)
                        queries(b)
                    act.wait_ge(var1_ready, 2)
                    sqrt_of(bn[:, 0, :], mv1[:, :, 1], 0).then_inc(sd1_ready, 1)

                def mlp(b):
                    with act.Fori(0, NTB) as i:
                        n = (i + b * NTB) * KT
                        act.wait_ge(mlp_ready, n + KT)
                        for k in range(KT):
                            act.activation(relu_h[:, k, :], X[:, b, k, ds(i * TB, TB)], ACT.Relu,
                                           scale=bn[:, 2, k:k + 1], bias=bn[:, 3, k:k + 1]).then_inc(mlp_in, 1)

                def gates(b):
                    for i in range(NTB):
                        n = b * NTB + i
                        act.wait_ge(gate_ready, n + 1)
                        if n > 0:
                            act.wait_ge(x3_ready, n * KT)
                        act.activation(s_relu[:, :], bank[n % 2][:, :], ACT.Relu, bias=c2[:, 1:2]).then_inc(s_relu_ready, 1)
                        for k in range(KT):
                            act.wait_ge(x3_ready, n * KT + k + 1)
                            if n * KT + k > 0:
                                act.wait_ge(sq3_ready, n * KT + k)
                            act.activation(junk[:, :], X[:, b, k, i * TB:(i + 1) * TB], ACT.Square,
                                           accum_out=sums3[:, 1, b, k, i:i + 1]).then_inc(sq3_ready, 1)

                def layer23():
                    act.wait_ge(affine1_ready, 2)
                    for b in range(B):
                        mlp(b)
                    for b in range(B):
                        gates(b)
                    act.wait_ge(norm3_ready, 1)
                    act.activation(st3[:, 0, :, :], tot3[:, :, 1, :], ACT.Sqrt).then_inc(nrm3_ready, 1)
                    act.wait_ge(var3_ready, 1)
                    sqrt_of(st3[:, 3, :, :], st3[:, 2, :, :], 0).then_inc(sd3_ready, 1)
                    act.wait_ge(affine3_ready, 1)
                    for b in range(B):
                        act.activation(X[:, b, 0, :], X[:, b, 0, :], ACT.Identity, scale=st3[:, 4, 0, b:b + 1],
                                       bias=st3[:, 5, 0, b:b + 1]).then_inc(out_ready[0], 1)

                layer1()
                layer23()

            attention_layer()
            later_layers()

        @block.vector
        def _(dve):
            def attention_layer():
                chain = [0]

                def link(ins):
                    chain[0] += 1
                    ins.then_inc(dve_chain, 1)
                    dve.wait_ge(dve_chain, chain[0])

                dve.sem_inc(mx_free, 2)
                dve.sem_inc(dve_sums, DVE_PAIRS)
                dve.sem_inc(y_added, KT)
                dve.memset(q_lm[0:DH, :], 0.0)
                dve.memset(max_cols[:, :, :], 0.0)
                link(dve.memset(k_h1[0:DH, :], 0.0))
                dve.memset(k_h1[0:1, :], 1.0)
                link(dve.memset(k_h1[LO_ROW:LO_ROW + 1, :], 1.0))
                dve.wait_ge(ident_ready, 1)
                dve.tensor_copy(ident_bf[:, :], ident[:, :]).then_inc(consts_ready, 1)

                def group_norm(b):
                    dve.wait_ge(x_loaded[b], 16 * KT)
                    for k in range(KT):
                        for i in range(NTB):
                            last = dve.bn_stats(stats[:, k, i, :], X[:, b, k, i * TB:(i + 1) * TB])
                        link(last)
                    for k in range(KT):
                        last = dve.bn_aggr(mv[:, k, :], stats[:, k, :, :].rearrange("p i s -> p (i s)"))
                    link(last)
                    link(dve.tensor_copy(gn[:, 0, :], mv[:, :, 0]))
                    dve.tensor_copy(gn[:, 1, :], mv[:, :, 1]).then_inc(ch_mean_ready, 1)
                    dve.wait_ge(ch_mean_ready, b + 1)
                    dve.wait_ge(group_mean_ready, b + 1)
                    link(dve.tensor_copy(gn[:, 2, :], misc[:, 0:KT]))
                    link(dve.tensor_tensor(gn[:, 4, :], gn[:, 0, :], gn[:, 2, :], ALU.subtract))
                    link(dve.tensor_tensor(gn[:, 4, :], gn[:, 4, :], gn[:, 4, :], ALU.mult))
                    dve.tensor_tensor(gn[:, 4, :], gn[:, 4, :], gn[:, 1, :], ALU.add).then_inc(ch_spread_ready, 1)
                    dve.wait_ge(sd_ready, b + 1)
                    link(dve.reciprocal(gn[:, 5, :], gn[:, 3, :]))
                    link(dve.tensor_tensor(gn[:, 5, :], gn[:, 5, :], col("gn_scale", 0, KT), ALU.mult))
                    link(dve.tensor_tensor(gn[:, 6, :], gn[:, 2, :], gn[:, 5, :], ALU.mult))
                    dve.tensor_tensor(gn[:, 6, :], col("gn_bias", 0, KT), gn[:, 6, :], ALU.subtract)\
                        .then_inc(affine_ready, 1)
                    dve.wait_ge(bias_ready, b + 1)
                    link(dve.tensor_tensor(b_qk[:, :], misc[:, 8:8 + NH], col("b_qk", 0, NH), ALU.add))
                    dve.tensor_tensor(b_v[:, :], misc[:, 16:16 + KT], col("b_v", 0, KT), ALU.add).then_inc(bv_ready, 1)
                    dve.wait_ge(out_bias_ready, b + 1)
                    link(dve.tensor_tensor(b_out[:, :], misc[:, 24:24 + KT], col("b_proj", 0, KT), ALU.add))
                    for k in range(KT):
                        last = dve.tensor_scalar(Y[:, k, :], X[:, b, k, :], b_out[:, k:k + 1], None, ALU.add)
                    last.then_inc(y_init, 1)
                    dve.wait_ge(y_init, b + 1)

                def prepare(hh, h):
                    dve.tensor_copy(b_head[:, :], b_qk[:, ds(h, 1)])
                    for k in range(KT):
                        dve.tensor_scalar(w_head[:, k, 0:2 * DH], wqkv[:, k, ds(h * (2 * DH), 2 * DH)],
                                          gn[:, 5, k:k + 1], None, ALU.mult)
                        last = dve.tensor_scalar(w_head[:, k, 2 * DH:QKV], wqkv[:, k, ds(h * DH + V_COL, DH)],
                                                 gn[:, 5, k:k + 1], None, ALU.mult)
                    last.then_inc(head_w_ready, 1)
                    dve.wait_ge(head_w_ready, hh + 1)
                    q, k = slice(0, DH), slice(DH, P)
                    for i in range(NTB + 1):
                        if i < NTB:
                            cols = slice(i * TB, (i + 1) * TB)
                            his = (hh * NTB + i) * PARTS
                            for n, (dst, half, hi) in enumerate(((q_lm[k, cols], q, q_hh[q, cols]),
                                                                 (k_hl[q, cols], k, k_hl[k, cols]))):
                                dve.wait_ge(hi_done, his + PARTS)
                                dve.scalar_tensor_tensor(dst, st[i // 2 % 2][half, i % 2, :], b_head[half, 0:1], hi,
                                                         ALU.add, ALU.subtract).then_inc(lo_done, 1)
                        if i > 0:
                            for u in range((i - 1) * SUBS, i * SUBS):
                                unit_max(hh * NTB, u)

                def unit_max(g, u):
                    dve.wait_ge(mx_ready, g * UNITS + (u + 1))
                    dve.tensor_reduce(part_max[:, u % SUBS, u // SUBS:u // SUBS + 1], mx[u % 2][:, :], AX.X,
                                      ALU.max).then_inc(mx_free, 1)

                def row_max(g):
                    dve.wait_ge(mx_free, g * UNITS + (UNITS + 2))
                    dve.tensor_reduce(neg_max[:, :], part_max[:, :, :], AX.X, ALU.max, negate=True)\
                        .then_inc(neg_max_ready, 1)
                    dve.wait_ge(neg_max_ready, g + 1)
                    dve.tensor_copy(max_cols[:, :, 0], neg_max[:, :]).then_inc(max_hi_ready, 1)
                    dve.wait_ge(max_hi_ready, g + 1)
                    dve.tensor_tensor(max_cols[:, :, LO_ROW], neg_max[:, :], max_cols[:, :, 0], ALU.subtract)\
                        .then_inc(max_cols_ready, 1)

                def pair_sum(g, i):
                    j = POOL_PAIRS + i
                    dve.wait_ge(exp_done, exps(g, j))
                    if i == 0:
                        dve.tensor_copy(acc_dve[:, :, :], prob[:, j % NBUF, :, :]).then_inc(dve_sums, 1)
                    else:
                        dve.wait_ge(dve_sums, dve_summed(g, i - 1))
                        dve.tensor_tensor(acc_dve[:, :, :], acc_dve[:, :, :], prob[:, j % NBUF, :, :],
                                          ALU.add).then_inc(dve_sums, 1)

                def all_sums(g):
                    pair_sum(g, DVE_PAIRS - 1)
                    dve.wait_ge(dve_sums, dve_summed(g, DVE_PAIRS - 1))
                    dve.tensor_tensor(total[:, :], acc_dve[:, 0, :], acc_dve[:, 1, :], ALU.add).then_inc(dve_folded, 1)
                    dve.wait_ge(dve_folded, g + 1)
                    dve.wait_ge(pool_total_ready, g + 2)
                    dve.tensor_tensor(total[:, :], total[:, :], pool_total[:, :], ALU.add).then_inc(total_ready, 1)

                def invert(g):
                    dve.wait_ge(total_turned, g + 1)
                    dve.reciprocal(inv_cols[:, :], misc[:, 0:SUBS]).then_inc(inv_ready, 1)

                def normalise(g):
                    dve.wait_ge(o_copied, g + 2)
                    dve.wait_ge(inv_spread, g + 1)
                    dve.tensor_tensor(o_norm[:, :], o_raw[:, :], misc[:, :], ALU.mult).then_inc(o_norm_ready, 1)

                def add_out(g, tb, m):
                    dve.wait_ge(proj_ready, g * KT + (m + 1))
                    y = Y[:, m, ds(tb * TB, TB)]
                    dve.tensor_tensor(y, misc[:, :], y, ALU.add).then_inc(y_added, 1)

                def step(g, tb, tail, turn):
                    if tail:
                        all_sums(g + (-1))
                    for j in range(NPAIR):
                        if turn:
                            for u in SLOTS[j]:
                                unit_max(g + 1, u)
                        if tail and j == SUM_SLOT:
                            invert(g + (-1))
                        if tail and j == INV_SLOT:
                            normalise(g + (-1))
                        if tail and j in PROJ_SLOTS:
                            add_out(g + (-1), tb + (-1), PROJ_SLOTS.index(j))
                        if turn and j == LAST_UNIT_SLOT:
                            row_max(g + 1)
                        if j > POOL_PAIRS:
                            pair_sum(g, j - 1 - POOL_PAIRS)

                def tail_alone(g, tb):
                    all_sums(g)
                    invert(g)
                    normalise(g)
                    for m in range(KT):
                        add_out(g, tb, m)

                for b in range(B):
                    if b == 0:
                        dve.wait_ge(weights_loaded, 16 * 5)
                    group_norm(b)
                    with dve.Fori(0, NH) as h:
                        hh = h + b * NH
                        prepare(hh, h)
                        row_max(hh * NTB)
                        step(hh * NTB, 0, tail=False, turn=True)
                        with dve.Fori(1, NTB - 1) as tb:
                            step(hh * NTB + tb, tb, tail=True, turn=True)
                        step(hh * NTB + (NTB - 1), NTB - 1, tail=True, turn=False)
                        tail_alone(hh * NTB + (NTB - 1), NTB - 1)
                    dve.wait_ge(y_added, (b + 1) * NH * NTB * KT + KT)
                    for k in range(KT):
                        last = dve.tensor_copy(X[:, b, k, :], Y[:, k, :])
                    last.then_inc(layer0_done, 1)
                    dve.wait_ge(layer0_done, b + 1)

            def later_layers():
                chain1 = [0]

                def link1(ins):
                    chain1[0] += 1
                    ins.then_inc(dve1_chain, 1)
                    dve.wait_ge(dve1_chain, chain1[0])

                def batch_stats(g, beta, n):
                    for k in range(KT):
                        for b in range(B):
                            for i in range(NTB):
                                last = dve.bn_stats(stats1[:, k, b, i, :], X[:, b, k, i * TB:(i + 1) * TB])
                        link1(last)
                    for k in range(KT):
                        last = dve.bn_aggr(mv1[:, k, :], stats1[:, k, :, :, :].rearrange("p b i s -> p (b i s)"))
                    last.then_inc(var1_ready, 1)
                    dve.wait_ge(var1_ready, n)
                    dve.wait_ge(sd1_ready, n)
                    link1(dve.reciprocal(bn[:, 1, :], bn[:, 0, :]))
                    link1(dve.tensor_tensor(bn[:, 2, :], bn[:, 1, :], col(g, 0, KT), ALU.mult))
                    link1(dve.tensor_tensor(bn[:, 1, :], mv1[:, :, 0], bn[:, 2, :], ALU.mult))
                    dve.tensor_tensor(bn[:, 3, :], col(beta, 0, KT), bn[:, 1, :], ALU.subtract).then_inc(affine1_ready, 1)

                def centre_wq():
                    for k in range(KT):
                        w = w1[:, k, 0:C].rearrange("p (h d) -> p h d", d=D1)
                        link1(dve.tensor_reduce(q_mean[:, k, :], w, AX.X, ALU.add))
                        link1(dve.tensor_scalar(q_mean[:, k, :], q_mean[:, k, :], 1.0 / D1, None, ALU.mult))
                        dve.tensor_tensor(w, w, q_mean[:, k, :].unsqueeze(2).broadcast_to([P, HEADS1, D1]),
                                          ALU.subtract).then_inc(wq1_ready, 1)

                def convolve(n, name, after=None):
                    out_of = Z

                    def blk(i):
                        steps = conv_steps(n, i)
                        for t in range(PE_TAPS, 9):
                            dy, dx = TAPS[t]
                            for k in range(KT):
                                src = H[:, k, ds(i * ROWS + dy, ROWS), dx:dx + IMG]
                                dst = out_of[:, k, ds(i * TB, TB)].rearrange("p (r c) -> p r c", c=IMG)
                                w = col(name, k * 9 + t)
                                if t == PE_TAPS:
                                    dve.wait_ge(conv_part, convs(n, i) + (k + 1))
                                    part = bank[k][:, :].rearrange("p (r c) -> p r c", c=IMG)
                                    dve.scalar_tensor_tensor(dst, src, w, part, ALU.mult, ALU.add)\
                                        .then_inc(conv_taken, 1)
                                else:
                                    if t == PE_TAPS + 1:
                                        dve.wait_ge(conv_taken, convs(n, i) + (k + 1 + KT))
                                    else:
                                        dve.wait_ge(conv_step, steps + ((t - PE_TAPS - 2) * KT + k + 1))
                                    dve.scalar_tensor_tensor(dst, src, w, dst, ALU.mult, ALU.add).then_inc(conv_step, 1)

                    if after is None:
                        with dve.Fori(0, NTB) as i:
                            blk(i)
                    else:
                        blk(0)
                        with dve.Fori(1, NTB) as i:
                            blk(i)
                            after(i + (-1))
                        after(NTB - 1)

                def downsample(b):
                    dve.wait_ge(conv_step, conv_steps(2 * b + 1, 0))
                    if b > 0:
                        dve.wait_ge(kv_ready, b * JT)
                    weights = []
                    for r in range(1, PERIOD):
                        f = np_f32(r * RATIO - int(r * RATIO))
                        weights.append((np_f32(1.0 - f), f, int(r * RATIO)))
                    for k in range(KT):
                        src = Z[:, k, :].rearrange("p (r c) -> p r c", c=IMG)
                        dst = rows_i[:, k, :, :]
                        last = dve.tensor_copy(dst[:, 0:RS:PERIOD, :], src[:, 0:IMG:PERIOD_ROWS, :])
                        for r, (_, f, i0) in enumerate(weights):
                            tmp = part_i[:, k, r, :].rearrange("p (g c) -> p g c", c=IMG)
                            last = dve.tensor_scalar(tmp, src[:, i0 + 1:i0 + 2 + (GROUPS - 1) * PERIOD_ROWS:PERIOD_ROWS, :],
                                                     f, None, ALU.mult)
                    link1(last)
                    for k in range(KT):
                        src = Z[:, k, :].rearrange("p (r c) -> p r c", c=IMG)
                        dst = rows_i[:, k, :, :]
                        for r, (w0, _, i0) in enumerate(weights):
                            tmp = part_i[:, k, r, :].rearrange("p (g c) -> p g c", c=IMG)
                            last = dve.scalar_tensor_tensor(
                                dst[:, r + 1:r + 2 + (GROUPS - 1) * PERIOD:PERIOD, :],
                                src[:, i0:i0 + 1 + (GROUPS - 1) * PERIOD_ROWS:PERIOD_ROWS, :], w0, tmp, ALU.mult, ALU.add)
                    link1(last)
                    for k in range(KT):
                        src = rows_i[:, k, :, :]
                        dst = zi[:, k, :].rearrange("p (r c) -> p r c", c=RS)
                        last = dve.tensor_copy(dst[:, :, 0:RS:PERIOD], src[:, :, 0:IMG:PERIOD_ROWS])
                        for r, (_, f, i0) in enumerate(weights):
                            tmp = part_i[:, k, r, 0:RS * GROUPS].rearrange("p (r g) -> p r g", g=GROUPS)
                            last = dve.tensor_scalar(tmp, src[:, :, i0 + 1:i0 + 2 + (GROUPS - 1) * PERIOD_ROWS:PERIOD_ROWS],
                                                     f, None, ALU.mult)
                    link1(last)
                    for k in range(KT):
                        src = rows_i[:, k, :, :]
                        dst = zi[:, k, :].rearrange("p (r c) -> p r c", c=RS)
                        for r, (w0, _, i0) in enumerate(weights):
                            tmp = part_i[:, k, r, 0:RS * GROUPS].rearrange("p (r g) -> p r g", g=GROUPS)
                            last = dve.scalar_tensor_tensor(
                                dst[:, :, r + 1:r + 2 + (GROUPS - 1) * PERIOD:PERIOD],
                                src[:, :, i0:i0 + 1 + (GROUPS - 1) * PERIOD_ROWS:PERIOD_ROWS], w0, tmp, ALU.mult, ALU.add)
                    link1(last)
                    for k in range(KT):
                        last = dve.tensor_copy(z_rev[:, k, :], zi[:, k, ::-1])
                    last.then_inc(zi_ready, 1)

                def keys(b):
                    def per_head(a):
                        return a.rearrange("p (h d) -> p h d", d=D1)

                    def spread(a):
                        return a.unsqueeze(2).broadcast_to([P, HEADS1, D1])

                    for j in range(JT):
                        dve.wait_ge(v_got, b * JT + j + 1)
                        k_in = bank[4 + j][:, 0:C]
                        link1(dve.tensor_reduce(k_st[:, 0, :], per_head(k_in), AX.X, ALU.add))
                        link1(dve.tensor_scalar(k_st[:, 0, :], k_st[:, 0, :], 1.0 / D1, None, ALU.mult))
                        link1(dve.tensor_tensor(per_head(kn[:, j, :]), per_head(k_in), spread(k_st[:, 0, :]), ALU.subtract))
                        link1(dve.tensor_tensor(k_sq[:, :], kn[:, j, :], kn[:, j, :], ALU.mult))
                        link1(dve.tensor_reduce(k_st[:, 1, :], per_head(k_sq[:, :]), AX.X, ALU.add))
                        dve.tensor_scalar(k_st[:, 1, :], k_st[:, 1, :], 1.0 / D1, None, ALU.mult).then_inc(k_var_ready, 1)
                        dve.wait_ge(k_sd_ready, b * JT + j + 1)
                        link1(dve.reciprocal(k_st[:, 3, :], k_st[:, 2, :]))
                        link1(dve.tensor_tensor(per_head(kn[:, j, :]), per_head(kn[:, j, :]), spread(k_st[:, 3, :]), ALU.mult))
                        link1(dve.tensor_tensor(kn[:, j, :], kn[:, j, :], k_gb[:, 0, :], ALU.mult))
                        dve.tensor_tensor(kn[:, j, :], kn[:, j, :], k_gb[:, 1, :], ALU.add).then_inc(kn_ready, 1)
                    for m in range(KT):
                        dve.wait_ge(kk_ready, b * KT + m + 1)
                        link1(dve.tensor_tensor(kv[:, m, :], bank[6][:, m * P:(m + 1) * P], mean32[:, :], ALU.mult))
                        dve.tensor_scalar(kvg[:, m, :], kv[:, m, :], col("nq_g", m), None, ALU.mult).then_inc(kvm_ready, 1)
                    dve.wait_ge(kvc_ready, b + 1)
                    link1(dve.tensor_copy(kv_c[:, :], bank[7][:, 0:KT]))
                    for m in range(KT):
                        dve.wait_ge(bias_part, b * KT + m + 1)
                        dve.tensor_scalar(bias_v[:, m, :], bank[4 + m][:, 0:NKEY], 1.0 / D1, kv_c[:, m:m + 1],
                                          ALU.mult, ALU.add).then_inc(bias_v_ready, 1)
                    dve.wait_ge(bias_v_ready, (b + 1) * KT)

                def queries(b):
                    with dve.Fori(0, NTB) as i:
                        n = (i + b * NTB) * KT
                        for m in range(KT):
                            dve.wait_ge(q_rs_ready, n + (m + 1))
                            dve.tensor_tensor(q_n[:, m, :], bank[m][:, :], q_rs[:, m, :], ALU.mult).then_inc(q_n_ready, 1)
                        for m in range(KT):
                            dve.wait_ge(o_ready, n + (m + 1))
                            for r in range(ROWS // REP):
                                cells = bias_v[:, m, ds((i * (ROWS // REP) + r) * RS, RS)]
                                half = slice(r * REP * IMG, (r + 1) * REP * IMG)
                                last = dve.tensor_tensor(
                                    H[:, m, ds(i * ROWS + (1 + r * REP), REP), 1:1 + IMG].rearrange("p r (a c) -> p r a c", c=REP),
                                    bank[4 + m][:, half].rearrange("p (r a c) -> p r a c", a=RS, c=REP),
                                    cells.unsqueeze(1).unsqueeze(3).broadcast_to([P, REP, RS, REP]), ALU.add)
                            last.then_inc(o_placed, 1)

                def add_attention(b):
                    def f(i):
                        n = (i + b * NTB) * KT
                        for m in range(KT):
                            dve.wait_ge(pw_ready, n + (m + 1))
                            xx = X[:, b, m, ds(i * TB, TB)]
                            dve.tensor_tensor(xx, bank[2 + m][:, :], xx, ALU.add).then_inc(x_added, 1)
                    return f

                def layer1():
                    dve.sem_inc(conv_taken, KT)
                    dve.sem_inc(q_n_ready, KT)
                    dve.sem_inc(mlp_added, KT)
                    dve.sem_inc(x_added, KT)
                    dve.sem_inc(o_placed, KT)
                    batch_stats("bn1_g", "bn1_b", 1)
                    dve.wait_ge(weights1_loaded, 16 * 7)
                    centre_wq()
                    for b in range(B):
                        dve.wait_ge(h_ready, (b + 1) * KT)
                        convolve(2 * b, "dw1")
                        downsample(b)
                        keys(b)
                        queries(b)
                        dve.wait_ge(o_placed, (b + 1) * NTB * KT + KT)
                        convolve(2 * b + 1, "dw2", add_attention(b))
                    dve.wait_ge(x_added, B * NTB * KT + KT)
                    batch_stats("bn2_g", "bn2_b", 2)

                def layer2_weights():
                    dve.wait_ge(l2_a, 1)
                    link1(dve.tensor_copy(u_col[:, :], bank[6][:, 0:KT]))
                    for k in range(KT):
                        dve.tensor_scalar(u_all[:, k, :], ones[:, :], u_col[:, k:k + 1], None, ALU.mult)
                    dve.tensor_scalar(b2all[:, 0, :], ones[:, :], col("bq"), None, ALU.mult)
                    dve.tensor_scalar(b2all[:, 1, :], ones[:, :], col("bk"), None, ALU.mult).then_inc(l2_b, 1)
                    dve.wait_ge(l2_a, 2)
                    link1(dve.tensor_copy(c2[:, 2:3], bank[6][:, 8:9]))
                    link1(dve.tensor_tensor(c2[:, 1:2], bank[6][:, 7:8], c2[:, 2:3], ALU.subtract))
                    dve.tensor_scalar(c2[:, 0:1], col("bv"), float(HW), None, ALU.mult).then_inc(l2_b, 1)
                    dve.wait_ge(l2_b, 2)

                def mlp(b):
                    with dve.Fori(0, NTB) as i:
                        n = (i + b * NTB) * KT
                        for m in range(KT):
                            dve.wait_ge(mlp_ready, n + (m + 1 + KT))
                            xx = X[:, b, m, ds(i * TB, TB)]
                            dve.scalar_tensor_tensor(xx, bank[4 + m][:, :], col("bexp", m), xx, ALU.add, ALU.add)\
                                .then_inc(mlp_added, 1)

                def mixing(b):
                    for k in range(KT):
                        last = dve.tensor_reduce(xs[:, b, k:k + 1], X[:, b, k, :], AX.X, ALU.add)
                    link1(last)
                    for k in range(KT):
                        last = dve.scalar_tensor_tensor(xs[:, b, k:k + 1], col("bexp", k), -float(HW), xs[:, b, k:k + 1],
                                                        ALU.mult, ALU.add)
                    last.then_inc(mix_a, 1)
                    dve.wait_ge(mix_b, 2 * b + 1)
                    dve.tensor_tensor(v_sum[:, b:b + 1], bank[7][:, 0:1], c2[:, 0:1], ALU.add).then_inc(mix_a, 1)
                    dve.wait_ge(mix_b, 2 * b + 2)
                    link1(dve.tensor_scalar(mixed[:, b, :], bank[7][:, 4:4 + KT], 1.0 / HW, None, ALU.mult))

                def apply_gates(b):
                    for i in range(NTB):
                        n = b * NTB + i
                        dve.wait_ge(s_relu_ready, n + 1)
                        for k in range(KT):
                            xx = X[:, b, k, i * TB:(i + 1) * TB]
                            dve.scalar_tensor_tensor(xx, s_relu[:, :], mixed[:, b, k:k + 1], xx, ALU.mult, ALU.add,
                                                     accum_out=sums3[:, 0, b, k, i:i + 1]).then_inc(x3_ready, 1)

                def evacuate_turned(b):
                    for c in range(HW // P):
                        n = b * (HW // P) + c
                        dve.wait_ge(turned3, n + 1)
                        dve.tensor_copy(xt[:, n % 4, :], bank[2 + n % 2][:, 0:C]).then_inc(xt_ready, 1)

                def layer3():
                    dve.wait_ge(x3_ready, B * NTB * KT)
                    dve.wait_ge(sq3_ready, B * NTB * KT)
                    for q in range(2):
                        for b in range(B):
                            last = dve.tensor_reduce(tot3[:, :, q, b], sums3[:, q, b, :, :], AX.X, ALU.add)
                    last.then_inc(norm3_ready, 1)
                    dve.wait_ge(nrm3_ready, 1)
                    link1(dve.tensor_scalar(st3[:, 1, :, :], st3[:, 0, :, :], 1e-12, None, ALU.max))
                    link1(dve.reciprocal(st3[:, 0, :, :], st3[:, 1, :, :]))
                    for b in range(B):
                        evacuate_turned(b)
                        dve.wait_ge(gram_ready, b + 1)
                        for m in range(KT):
                            last = dve.tensor_scalar(gram_s[:, m, :], bank[4 + m][:, 0:C], st3[:, 0, m, b:b + 1], None,
                                                     ALU.mult)
                        last.then_inc(gram_scaled, 1)
                        dve.wait_ge(gram_turned, b + 1)
                        for m in range(KT):
                            if b == 0:
                                last = dve.tensor_scalar(cos[:, m, :], bank[6 + m][:, 0:C], st3[:, 0, m, b:b + 1], None,
                                                         ALU.mult)
                            else:
                                last = dve.scalar_tensor_tensor(cos[:, m, :], bank[6 + m][:, 0:C], st3[:, 0, m, b:b + 1],
                                                                cos[:, m, :], ALU.mult, ALU.add)
                        last.then_inc(cos_added, 1)
                        dve.wait_ge(cos_added, b + 1)
                    for m in range(KT):
                        last = dve.tensor_scalar(gram_s[:, m, :], cos[:, m, :], 1.0 / B, None, ALU.mult)
                    link1(last)
                    for m in range(KT):
                        last = dve.scalar_tensor_tensor(cos[:, m, :], gram_s[:, m, :], -1.0, gram_s[:, m, :],
                                                        ALU.mult, ALU.min)
                    link1(last)
                    dve.wait_ge(diag_ready, 2 * KT * PE_TAPS + 1)
                    for m in range(KT):
                        last = dve.max(top[:, m, :], cos[:, m, :])
                    link1(last)
                    for m in range(KT):
                        last = dve.max_index(top_i[:, m, :], top[:, m, :], cos[:, m, :])
                    link1(last)
                    link1(dve.tensor_copy(top_f[:, :, :], top_i[:, :, :]))
                    for n in range(1, NSEL):
                        for m in range(KT):
                            one = top_f[:, m, n:n + 1]
                            if n == 1:
                                last = dve.tensor_scalar(pick[:, m, :], count[:, :], one, None, ALU.is_equal)
                            else:
                                last = dve.scalar_tensor_tensor(pick[:, m, :], count[:, :], one, pick[:, m, :],
                                                                ALU.is_equal, ALU.add)
                        if n < NSEL - 1:
                            link1(last)
                    last.then_inc(pick_ready, 1)
                    for d in range(KT):
                        dve.wait_ge(pick_turned, d + 1)
                        dve.tensor_copy(pick_t[:, d, :], bank[d][:, 0:C]).then_inc(pick_t_ready, 1)
                    dve.wait_ge(group_sums, 1)
                    for m in range(KT):
                        last = dve.tensor_tensor(g3[:, m, :, :].rearrange("p q b -> p (q b)"), bank[2][:, m * 4:m * 4 + 4],
                                                 tot3[:, m, :, :].rearrange("p q b -> p (q b)"), ALU.add)
                    link1(last)
                    count3 = 1.0 / (NSEL * HW)
                    mean, sq = g3[:, :, 0, :], g3[:, :, 1, :]
                    link1(dve.tensor_scalar(g3[:, :, :, :], g3[:, :, :, :], count3, None, ALU.mult))
                    link1(dve.tensor_tensor(st3[:, 5, :, :], mean, mean, ALU.mult))
                    dve.tensor_tensor(st3[:, 2, :, :], sq, st3[:, 5, :, :], ALU.subtract).then_inc(var3_ready, 1)
                    dve.wait_ge(sd3_ready, 1)
                    link1(dve.reciprocal(st3[:, 1, :, :], st3[:, 3, :, :]))
                    for k in range(KT):
                        last = dve.tensor_scalar(st3[:, 4, k, :], st3[:, 1, k, :], col("gamma", k), None, ALU.mult)
                    link1(last)
                    link1(dve.tensor_tensor(st3[:, 2, :, :], mean, st3[:, 4, :, :], ALU.mult))
                    for k in range(KT):
                        last = dve.tensor_scalar(st3[:, 5, k, :], st3[:, 2, k, :], -1.0, col("beta", k), ALU.mult, ALU.add)
                    last.then_inc(affine3_ready, 1)
                    dve.wait_ge(affine3_ready, 1)
                    for b in range(B):
                        dve.tensor_scalar(X[:, b, 1, :], X[:, b, 1, :], st3[:, 4, 1, b:b + 1], st3[:, 5, 1, b:b + 1],
                                          ALU.mult, ALU.add).then_inc(out_ready[1], 1)

                layer1()
                layer2_weights()
                for b in range(B):
                    mlp(b)
                dve.wait_ge(mlp_added, B * NTB * KT + KT)
                for b in range(B):
                    mixing(b)
                    apply_gates(b)
                layer3()

            attention_layer()
            later_layers()

        @block.tensor
        def _(pe):
            def attention_layer():
                pe.wait_ge(consts_ready, CONSTS)
                pe.wait_ge(weights_loaded, 16 * 5)
                pe.sem_inc(pv_done, NBUF)

                def group_norm(b):
                    pe.wait_ge(ch_mean_ready, b + 1)
                    pe.matmul(misc[:, 0:KT], mean8[:, :], gn[:, 0, :], start=True, stop=True).then_inc(group_mean_ready, 1)
                    pe.wait_ge(ch_spread_ready, b + 1)
                    pe.matmul(misc[:, 4:4 + KT], mean8[:, :], gn[:, 4, :], start=True, stop=True).then_inc(group_var_ready, 1)
                    pe.wait_ge(affine_ready, b + 1)
                    for h in range(NH):
                        for k in range(KT):
                            pe.matmul(misc[:, 8 + h:9 + h], wqkv[:, k, h * 2 * DH:(h + 1) * 2 * DH], gn[:, 6, k:k + 1],
                                      start=(k == 0), stop=(k == KT - 1))
                    for m in range(KT):
                        for k in range(KT):
                            last = pe.matmul(misc[:, 16 + m:17 + m], wqkv[:, k, V_COL + m * P:V_COL + (m + 1) * P],
                                             gn[:, 6, k:k + 1], start=(k == 0), stop=(k == KT - 1))
                    last.then_inc(bias_ready, 1)
                    pe.wait_ge(bv_ready, b + 1)
                    for m in range(KT):
                        for k in range(KT):
                            last = pe.matmul(misc[:, 24 + m:25 + m], wproj[:, k, m * P:(m + 1) * P], b_v[:, k:k + 1],
                                             start=(k == 0), stop=(k == KT - 1))
                    last.then_inc(out_bias_ready, 1)

                def prepare(b, hh):
                    pe.wait_ge(head_w_ready, hh + 1)
                    pe.wait_ge(o_copied, hh * NTB + 1)
                    for i in range(NTB + 1):
                        if i < NTB:
                            if i >= 4:
                                pe.wait_ge(lo_done, (hh * NTB + (i - 3)) * 2)
                            for k in range(KT):
                                last = pe.matmul(st[i // 2 % 2][:, i % 2, :], w_head[:, k, 0:2 * DH],
                                                 X[:, b, k, i * TB:(i + 1) * TB], start=(k == 0), stop=(k == KT - 1))
                            last.then_inc(qk_ready, 1)
                            if i > 0:
                                pe.wait_ge(v_copied, hh * NTB + i)
                            for s in range(SUBS):
                                tok = (i * SUBS + s) * P
                                for k in range(KT):
                                    last = pe.matmul(pvo[:, s * DH:(s + 1) * DH], X[:, b, k, tok:tok + P],
                                                     w_head[:, k, 2 * DH:QKV], start=(k == 0), stop=(k == KT - 1))
                            last.then_inc(v_ready, 1)
                        if i > 0:
                            pe.wait_ge(hi_done, (hh * NTB + i) * PARTS)
                            pe.wait_ge(lo_done, (hh * NTB + i) * 2)
                            for u in range((i - 1) * SUBS, i * SUBS):
                                unit(hh * NTB, 0, u)
                    pe.wait_ge(v_copied, hh * NTB + NTB)

                def unit(g, tb, u):
                    pe.wait_ge(mx_free, g * UNITS + (u + 1))
                    keys = slice(u // SUBS * TB, (u // SUBS + 1) * TB)
                    pe.matmul(mx[u % 2][:, :], q_hh[:, ds(tb * TB + u % SUBS * P, P)], k_hl[:, keys],
                              start=True, stop=True).then_inc(mx_ready, 1)

                def turn_max(g):
                    pe.wait_ge(max_cols_ready, g + 1)
                    for s in range(SUBS):
                        last = pe.matmul(misc[0:LO_ROW + 1, s * P:(s + 1) * P], max_cols[:, s, :], ident_bf[:, :],
                                         start=True, stop=True)
                    last.then_inc(max_turned, 1)

                def scores(g, tb, j):
                    cols = ds(tb * TB, TB)
                    for c in range(2):
                        keys = slice((2 * j + c) * P, (2 * j + c + 1) * P)
                        pe.matmul(st[j % 2][:, c, :], k_hl[:, keys], q_hh[:, cols], start=True, stop=False)
                        last = pe.matmul(st[j % 2][:, c, :], k_h1[:, keys], q_lm[:, cols], start=False, stop=True)
                    last.then_inc(st_ready, 1)

                def weighted_values(g, j):
                    pe.wait_ge(exp_done, exps(g, j))
                    for c in range(2):
                        last = pe.matmul(pvo[c * DH:(c + 1) * DH, :], v_sb[:, 2 * j + c, :], prob[:, j % NBUF, c, :],
                                         start=(j == 0), stop=(j == NPAIR - 1))
                    last.then_inc(pv_done, 1)

                def turn_total(g):
                    pe.wait_ge(total_ready, g + 1)
                    for s in range(SUBS):
                        last = pe.matmul(misc[:, s:s + 1], total[:, s * P:(s + 1) * P], ones[:, 0:1], start=True, stop=True)
                    last.then_inc(total_turned, 1)

                def spread_inverse(g):
                    pe.wait_ge(inv_ready, g + 1)
                    for s in range(SUBS):
                        last = pe.matmul(misc[:, s * P:(s + 1) * P], inv_cols[:, s:s + 1].broadcast_to([P, P]), ident[:, :],
                                         start=True, stop=True)
                    last.then_inc(inv_spread, 1)

                def project(g, m):
                    pe.wait_ge(o_norm_ready, g + 1)
                    if m:
                        pe.wait_ge(y_added, g * KT + (m + KT))
                    pe.matmul(misc[:, :], wp_head[:, m * P:(m + 1) * P], o_norm[:, :],
                              start=True, stop=True).then_inc(proj_ready, 1)

                def step(g, tb, tail, turn):
                    pe.wait_ge(max_row_ready, g + 1)
                    for j in range(NPAIR):
                        units = SLOTS[j] if turn else []
                        for u in units[0:1]:
                            unit(g + 1, tb + 1, u)
                        scores(g, tb, j)
                        for u in units[1:2]:
                            unit(g + 1, tb + 1, u)
                        if j == 0 and tail:
                            weighted_values(g + (-1), NPAIR - 1)
                        if j == 1:
                            pe.wait_ge(o_copied, g + 1)
                        if j >= 1:
                            weighted_values(g, j - 1)
                        for u in units[2:]:
                            unit(g + 1, tb + 1, u)
                        if tail and j == SUM_SLOT:
                            turn_total(g + (-1))
                        if tail and j == INV_SLOT:
                            spread_inverse(g + (-1))
                        if tail and j in PROJ_SLOTS:
                            project(g + (-1), PROJ_SLOTS.index(j))
                        if turn and j == TURN_SLOT:
                            if tail:
                                pe.wait_ge(y_added, g * KT + KT)
                            turn_max(g + 1)

                def tail_alone(g):
                    weighted_values(g, NPAIR - 1)
                    turn_total(g)
                    spread_inverse(g)
                    for m in range(KT):
                        project(g, m)
                    pe.wait_ge(y_added, g * KT + 2 * KT)

                for b in range(B):
                    group_norm(b)
                    with pe.Fori(0, NH) as h:
                        hh = h + b * NH
                        prepare(b, hh)
                        turn_max(hh * NTB)
                        pe.wait_ge(head_wp_ready, hh + 1)
                        step(hh * NTB, 0, tail=False, turn=True)
                        with pe.Fori(1, NTB - 1) as tb:
                            step(hh * NTB + tb, tb, tail=True, turn=True)
                        step(hh * NTB + (NTB - 1), NTB - 1, tail=True, turn=False)
                        tail_alone(hh * NTB + (NTB - 1))

            def later_layers():
                def taps(n, name_i, i):
                    for k in range(KT):
                        pe.wait_ge(conv_taken, convs(n, i) + (k + 1))
                        for t in range(PE_TAPS):
                            dy, dx = TAPS[t]
                            last = pe.matmul(bank[k][:, :], diag[:, name_i, k, t, :],
                                             H[:, k, ds(i * ROWS + dy, ROWS), dx:dx + IMG],
                                             start=(t == 0), stop=(t == PE_TAPS - 1))
                        last.then_inc(conv_part, 1)

                def keys(b):
                    pe.wait_ge(zi_ready, b + 1)
                    for j in range(JT):
                        for k in range(KT):
                            last = pe.matmul(bank[4 + j][:, :], z_rev[:, k, j * P:(j + 1) * P], w1[:, k, C:3 * C], start=(k == 0), stop=(k == KT - 1))
                        last.then_inc(kv_ready, 1)
                    pe.wait_ge(kn_ready, (b + 1) * JT)
                    for m in range(KT):
                        for j in range(JT):
                            last = pe.matmul(bank[6][:, m * P:(m + 1) * P], kn[:, j, m * P:(m + 1) * P],
                                             vv[:, j, m * P:(m + 1) * P], start=(j == 0), stop=(j == JT - 1))
                    last.then_inc(kk_ready, KT)
                    pe.wait_ge(kvm_ready, (b + 1) * KT)
                    for m in range(KT):
                        last = pe.matmul(bank[7][:, m:m + 1], kv[:, m, :], col("nq_b", m), start=True, stop=True)
                    last.then_inc(kvc_ready, 1)
                    pe.wait_ge(table_loaded, 16 * (P // RS))
                    for m in range(KT):
                        for h4 in range(P // D1):
                            h = m * (P // D1) + h4
                            for j in range(JT):
                                start = j * (P // RS) * TABLE
                                rhs = table[:, h, start:start + RS * TABLE].rearrange("p (r c) -> p r c", c=TABLE)[:, :, 0:RS]
                                last = pe.matmul(bank[4 + m][h4 * D1:(h4 + 1) * D1, 0:NKEY], vv[:, j, h * D1:(h + 1) * D1],
                                                 rhs, start=(j == 0), stop=(j == JT - 1), tile_position=(0, h4 * D1))
                        last.then_inc(bias_part, 1)
                    pe.wait_ge(bias_v_ready, (b + 1) * KT)

                def queries(b):
                    with pe.Fori(0, NTB) as i:
                        n = (i + b * NTB) * KT
                        pe.wait_ge(q_n_ready, n + KT)
                        for m in range(KT):
                            for k in range(KT):
                                last = pe.matmul(bank[m][:, :], w1[:, k, m * P:(m + 1) * P], Z[:, k, ds(i * TB, TB)],
                                                 start=(k == 0), stop=(k == KT - 1))
                            last.then_inc(q_ready, 1)
                        for m in range(KT):
                            pe.wait_ge(q_sq_ready, n + (m + 1))
                            pe.matmul(bank[2 + m][:, :], mean32[:, :], q_sq[:, m, :], start=True, stop=True)\
                                .then_inc(q_var_ready, 1)
                        for m in range(KT):
                            pe.wait_ge(q_n_ready, n + (m + 1 + KT))
                            pe.wait_ge(o_placed, n + (m + 1))
                            pe.matmul(bank[4 + m][:, :], kvg[:, m, :], q_n[:, m, :], start=True, stop=True)\
                                .then_inc(o_ready, 1)

                def pointwise(b, i):
                    n = (i + b * NTB) * KT
                    pe.wait_ge(conv_step, conv_steps(2 * b + 1, i) + KT * (DVE_TAPS - 1))
                    for m in range(KT):
                        pe.wait_ge(x_added, n + (m + 1))
                        for k in range(KT):
                            last = pe.matmul(bank[2 + m][:, :], w_out[:, k, m * P:(m + 1) * P], Z[:, k, ds(i * TB, TB)],
                                             start=(k == 0), stop=(k == KT - 1))
                        last.then_inc(pw_ready, 1)

                def layer1():
                    pe.sem_inc(mlp_ready, KT)
                    pe.wait_ge(diag_ready, 2 * KT * PE_TAPS + 1)
                    pe.wait_ge(wq1_ready, KT)
                    for b in range(B):
                        pe.wait_ge(h_ready, (b + 1) * KT)
                        with pe.Fori(0, NTB) as i:
                            taps(2 * b, 0, i)
                        keys(b)
                        queries(b)
                        pe.wait_ge(o_placed, (b + 1) * NTB * KT + KT)
                        taps(2 * b + 1, 1, 0)
                        with pe.Fori(1, NTB) as i:
                            taps(2 * b + 1, 1, i)
                            pointwise(b, i + (-1))
                        pointwise(b, NTB - 1)

                def layer2_weights():
                    for k in range(KT):
                        pe.matmul(bank[6][:, k:k + 1], w2q[:, 0, k * P:(k + 1) * P], col("wq_c"), start=True, stop=False)
                        last = pe.matmul(bank[6][:, k:k + 1], w2q[:, 1, k * P:(k + 1) * P], col("wk_c"),
                                         start=False, stop=True)
                    last.then_inc(l2_a, 1)
                    pe.wait_ge(l2_b, 1)
                    pe.matmul(bank[6][:, 7:8], b2all[:, 0, :], col("wq_c"), start=True, stop=False)
                    pe.matmul(bank[6][:, 7:8], b2all[:, 1, :], col("wk_c"), start=False, stop=True)
                    for k in range(KT):
                        last = pe.matmul(bank[6][:, 8:9], u_all[:, k, :], col("bexp", k), start=(k == 0), stop=(k == KT - 1))
                    last.then_inc(l2_a, 1)

                def mlp(b):
                    with pe.Fori(0, NTB) as i:
                        n = (i + b * NTB) * KT
                        pe.wait_ge(mlp_in, n + KT)
                        for m in range(KT):
                            pe.wait_ge(mlp_added, n + (m + 1))
                            for k in range(KT):
                                last = pe.matmul(bank[4 + m][:, :], w_mlp[:, k, m * P:(m + 1) * P], relu_h[:, k, :],
                                                 start=(k == 0), stop=(k == KT - 1))
                            last.then_inc(mlp_ready, 1)

                def mixing(b):
                    pe.wait_ge(mix_a, 2 * b + 1)
                    for k in range(KT):
                        last = pe.matmul(bank[7][:, 0:1], w2v[:, k, :], xs[:, b, k:k + 1], start=(k == 0), stop=(k == KT - 1))
                    last.then_inc(mix_b, 1)
                    pe.wait_ge(mix_a, 2 * b + 2)
                    for m in range(KT):
                        last = pe.matmul(bank[7][:, 4 + m:5 + m], w2e[:, m * P:(m + 1) * P], v_sum[:, b:b + 1],
                                         start=True, stop=True)
                    last.then_inc(mix_b, 1)

                def gates(b, i):
                    n = b * NTB + i
                    if n >= 2:
                        pe.wait_ge(s_relu_ready, n - 1)
                    for k in range(KT):
                        last = pe.matmul(bank[n % 2][:, :], u_all[:, k, :], X[:, b, k, i * TB:(i + 1) * TB],
                                         start=(k == 0), stop=(k == KT - 1))
                    last.then_inc(gate_ready, 1)

                def turn(n):
                    b, c = n // (HW // P), n % (HW // P)
                    if n >= 2:
                        pe.wait_ge(xt_ready, n - 1)
                    for k in range(KT):
                        last = pe.transpose(bank[2 + n % 2][:, k * P:(k + 1) * P], X[:, b, k, c * P:(c + 1) * P], ident[:, :])
                    last.then_inc(turned3, 1)

                def gram(n):
                    b, c = n // (HW // P), n % (HW // P)
                    pe.wait_ge(xt_ready, n + 1)
                    for m in range(KT):
                        last = pe.matmul(bank[4 + m][:, 0:C], xt[:, n % 4, m * P:(m + 1) * P], xt[:, n % 4, :],
                                         start=(c == 0), stop=(c == HW // P - 1))
                    if c == HW // P - 1:
                        last.then_inc(gram_ready, 1)

                def layer3():
                    pe.wait_ge(x3_ready, B * NTB * KT)
                    chunks = HW // P
                    turn(0)
                    for n in range(B * chunks):
                        if n + 1 < B * chunks:
                            turn(n + 1)
                        gram(n)
                        if n % chunks == chunks - 1:
                            b = n // chunks
                            pe.wait_ge(gram_scaled, b + 1)
                            if b > 0:
                                pe.wait_ge(cos_added, b)
                            for m in range(KT):
                                for k in range(KT):
                                    last = pe.transpose(bank[6 + m][:, k * P:(k + 1) * P], gram_s[:, k, m * P:(m + 1) * P],
                                                        ident[:, :])
                            last.then_inc(gram_turned, 1)
                    pe.wait_ge(pick_ready, 1)
                    for d in range(KT):
                        for m in range(KT):
                            last = pe.transpose(bank[d][:, m * P:(m + 1) * P], pick[:, m, d * P:(d + 1) * P], ident[:, :])
                        last.then_inc(pick_turned, 1)
                    pe.wait_ge(pick_t_ready, KT)
                    for m in range(KT):
                        for d in range(KT):
                            last = pe.matmul(bank[2][:, m * 4:m * 4 + 4], pick_t[:, d, m * P:(m + 1) * P],
                                             tot3[:, d, :, :].rearrange("p q b -> p (q b)"), start=(d == 0), stop=(d == KT - 1))
                    last.then_inc(group_sums, 1)

                layer1()
                pe.wait_ge(weights1_loaded, 16 * 7)
                layer2_weights()
                for b in range(B):
                    mlp(b)
                for b in range(B):
                    mixing(b)
                    for i in range(NTB):
                        gates(b, i)
                layer3()

            attention_layer()
            later_layers()



def kernel(**inputs):
    import numpy as _np
    import concourse.bacc as _bacc
    from concourse import mybir as _mybir
    from concourse.bass_utils import run_bass_kernel_spmd as _run

    def columns(v):
        return _np.asarray(v).reshape(-1, P).T

    def taps(w):
        return _np.asarray(w).reshape(KT, P, 9).transpose(1, 0, 2).reshape(P, KT * 9)

    by_head = _np.arange(C).reshape(D1, HEADS1).T.reshape(-1)
    g = {k: _np.asarray(v) for k, v in inputs.items()}
    w_qkv = g["L0_conv_w_qkv"].reshape(NH, 3, DH, C)
    w_qkv = _np.concatenate([w_qkv[:, 0:2].reshape(V_COL, C), w_qkv[:, 2].reshape(C, C)])
    b_qkv = g["L0_conv_b_qkv"].reshape(NH, 3, DH)
    parts = {
        "gn_scale": columns(g["L0_conv_gn_scale"]), "gn_bias": columns(g["L0_conv_gn_bias"]),
        "b_qk": b_qkv[:, 0:2].reshape(NH, P).T, "b_v": columns(b_qkv[:, 2].reshape(-1)),
        "b_proj": columns(g["L0_conv_b_proj"]),
        "bn1_g": columns(g["L1_conv_bn1_g"]), "bn1_b": columns(g["L1_conv_bn1_b"]),
        "dw1": taps(g["L1_conv_qkv_dw"]), "dw2": taps(g["L1_conv_out_dw"][by_head]),
        "nq_g": columns(g["L1_conv_nq_g"].reshape(-1)), "nq_b": columns(g["L1_conv_nq_b"].reshape(-1)),
        "bn2_g": columns(g["L1_conv_bn2_g"]), "bn2_b": columns(g["L1_conv_bn2_b"]),
        "bexp": columns(g["L2_conv_bexp"]), "bq": columns(g["L2_conv_bq"]), "bk": columns(g["L2_conv_bk"]),
        "bv": columns(g["L2_conv_bv"]), "wq_c": columns(g["L2_conv_Wcat"][0, :E2]),
        "wk_c": columns(g["L2_conv_Wcat"][0, E2:]), "gamma": columns(g["L3_conv_gamma"]),
        "beta": columns(g["L3_conv_beta"]),
    }
    w1 = g["L1_conv_qkv_pw"].reshape(3, C, C)[:, by_head].reshape(3 * C, C)
    k_norm = _np.stack([g["L1_conv_nk_g"].reshape(-1), g["L1_conv_nk_b"].reshape(-1)])
    arrays = {
        "x": g["x"],
        "w_qkv_t": w_qkv.T, "w_proj_t": g["L0_conv_w_proj"].T,
        "vectors": _np.concatenate([parts[n] for n in VEC_NAMES], axis=1),
        "w1_t": w1.T, "w_out_t": g["L1_conv_out_pw"][:, by_head].T, "mlp_t": g["L1_conv_mlp_w"].T,
        "k_norm": _np.broadcast_to(k_norm, (P, 2, C)),
        "rel_table": g["L1_conv_rel_table"].T,
        "w2_qk": _np.stack([g["L2_conv_Wq"], g["L2_conv_Wk"]], axis=1),
        "w2_v_t": g["L2_conv_Wv"].T, "w2_exp_t": g["L2_conv_Wexp"].T,
    }
    arrays = {n: _np.ascontiguousarray(a) for n, a in arrays.items()}
    nc = _bacc.Bacc("TRN2", target_bir_lowering=False, num_devices=1)
    args = [nc.dram_tensor(f"in_{n}", a.shape, _mybir.dt.from_np(a.dtype), kind="ExternalInput").ap()
            for n, a in arrays.items()]
    result = nc.dram_tensor("out_0", (B, C, IMG, IMG), F32, kind="ExternalOutput").ap()
    build(nc, *args, result)
    r = _run(nc, [{f"in_{n}": a for n, a in arrays.items()}], core_ids=[0])
    return r.results[0]["out_0"]
```

```python
from contextlib import ExitStack

import concourse.bass as bass
from concourse import mybir

F32 = mybir.dt.float32
BF16 = mybir.dt.bfloat16
U32 = mybir.dt.uint32
ALU = mybir.AluOpType
ACT = mybir.ActivationFunctionType
AX = mybir.AxisListType
ds = bass.ds

P = 128
B, C, IMG = 2, 256, 64
HW = IMG * IMG
KT = C // P
TB = 512
NTB = HW // TB

NH, DH = 4, 64
QKV = 3 * DH
V_COL = 2 * DH * NH
EPS_GN = 1e-5
GROUP0 = C // 32
SCALE0 = 1.0 / DH ** 0.5
NPAIR = HW // (2 * P)
POOL_PAIRS = 12
DVE_PAIRS = NPAIR - POOL_PAIRS
NBUF = 4
SUBS = TB // P
UNITS = SUBS * NTB
PER_SLOT = 3


def unit_slots():
    slots, u = [[] for _ in range(NPAIR)], 0
    for j in range(1, NPAIR):
        while u < UNITS and len(slots[j]) < PER_SLOT:
            slots[j].append(u)
            u += 1
    return slots


SLOTS = unit_slots()
LAST_UNIT_SLOT = max(j for j in range(NPAIR) if SLOTS[j])
assert SLOTS[LAST_UNIT_SLOT][-1] == UNITS - 1 and LAST_UNIT_SLOT + 2 < NPAIR
TURN_SLOT = LAST_UNIT_SLOT + 2
assert TURN_SLOT <= NPAIR - 2

SUM_SLOT, INV_SLOT = 2, 3
PROJ_SLOTS = (5, 7)
LO_ROW = 32
PARTS = 4
CONSTS = 6
LAG = 2
TAIL_STAGES = 4
assert max(PROJ_SLOTS) < TURN_SLOT

HEADS1, RS = 8, 16
D1 = C // HEADS1
NKEY = RS * RS
JT = NKEY // P
REP = IMG // RS
TABLE = 2 * RS - 1
ROWS = TB // IMG
PAD = IMG + 2
TAPS = [(dy, dx) for dy in range(3) for dx in range(3)]
PE_TAPS = (4, 3)
VAR_ROWS = 64
TILE_HEADS = P // D1
assert NTB * TILE_HEADS <= VAR_ROWS
KV_AT = 4
EPS_BN = 1e-5
EPS_LN = 1e-6
RATIO = (IMG - 1) / (RS - 1)
PERIOD = 5
PERIOD_ROWS = int(PERIOD * RATIO)
GROUPS = RS // PERIOD
assert PERIOD_ROWS == PERIOD * RATIO and GROUPS * PERIOD + 1 == RS and GROUPS * PERIOD_ROWS + 1 == IMG
E2 = C // 2
NSEL = C // 32
EPS_L3 = 1e-5
BIAS_RUN = (RS - 1) * TABLE + RS + (P // RS) * TABLE


VEC_NAMES = {"gn_scale": KT, "gn_bias": KT, "b_qk": NH, "b_v": KT, "b_proj": KT,
             "bn1_g": KT, "bn1_b": KT, "dw1": KT * 9, "dw2": KT * 9, "nq_g": KT, "nq_b": KT, "bn2_g": KT,
             "bn2_b": KT, "bexp": KT, "bq": 1, "bk": 1, "bv": 1, "wq_c": 1, "wk_c": 1, "gamma": KT, "beta": KT}
VEC, NVEC = {}, 0
for _name, _n in VEC_NAMES.items():
    VEC[_name] = NVEC
    NVEC += _n


ARENA_WORDS = 36128


def np_f32(v):
    import numpy as np
    return float(np.float32(v))


def build(nc, x, w_qkv_t, w_proj_t, vectors, w1_t, w_out_t, mlp_t, k_norm, rel_table, w2_qk, w2_v_t, w2_exp_t, out):
    ctx = ExitStack()
    with ctx:
        def sb(name, shape, dt=F32):
            return ctx.enter_context(nc.sbuf_tensor(name, shape, dt))

        def sem(name):
            return ctx.enter_context(nc.semaphore(name))

        X = sb("X", [P, B, KT, HW])
        vec = sb("vec", [P, NVEC])
        ident = sb("ident", [P, P])
        ones = sb("ones", [P, P])
        mean8 = sb("mean8", [P, P])
        mean32 = sb("mean32", [P, P])
        first_stats = sb("first_stats", [P, KT, NTB, 6])
        eps = sb("eps", [P, 2])

        def col(name, k=0, n=1):
            return vec[:, VEC[name] + k:VEC[name] + k + n]

        arena = sb("arena", [P, ARENA_WORDS])

        def carver(start, end):
            at = [start]

            def take(shape, dt=F32):
                n = 1
                for d in shape[1:]:
                    n *= d
                words = (n + 1) // 2 if dt == BF16 else n
                assert at[0] + words <= end, (at, words, end)
                tile = arena[0:shape[0], at[0]:at[0] + words]
                at[0] += words
                if dt != F32:
                    tile = tile.bitcast(dt)[:, 0:n]
                if len(shape) > 2:
                    names = " ".join("abcdef"[:len(shape) - 1])
                    tile = tile.rearrange(f"p ({names}) -> p {names}",
                                          **{c: d for c, d in zip("abcdef", shape[1:])})
                return tile
            return take

        early = carver(0, ARENA_WORDS)
        late = carver(0, ARENA_WORDS)

        Y = early([P, KT, HW])
        q_hh = early([P, HW], BF16)
        k_hl = early([P, HW], BF16)
        q_lm = early([P, HW], BF16)
        k_h1 = early([P, HW], BF16)
        v_sb = early([P, HW // P, DH])
        prob = early([P, NBUF, 2, TB])
        acc_pool = early([P, 2, TB])
        acc_dve = early([P, 2, TB])
        pool_total = early([P, TB])
        total = early([P, TB])
        inv_cols = early([P, SUBS])
        o_raw = early([P, TB])
        o_norm = early([P, TB])
        wqkv = early([P, KT, NH * QKV])
        wproj = early([P, KT, C])
        wproj2 = early([P, NH, C])
        w_head = early([P, KT, QKV])
        wp_head = early([P, C])
        b_head = early([P, 1])
        stats = early([P, KT, NTB, 6])
        mv = early([P, KT, 2])
        gn = early([P, 8, KT])
        b_qk = early([P, NH])
        b_v = early([P, KT])
        b_out = early([P, KT])
        part_max = early([P, SUBS, NTB])
        neg_max = early([P, SUBS])
        max_cols = early([P, SUBS, LO_ROW + 1], BF16)
        ident_bf = early([P, P], BF16)

        H = late([P, KT, PAD, PAD])
        Z = late([P, KT, HW])
        w1 = late([P, KT, 3 * C])
        w_out = late([P, KT, C])
        k_gb = late([P, 2, C])
        table = late([P, HEADS1, BIAS_RUN + TABLE - RS])
        diag = [late([P, KT, taps, P]) for taps in PE_TAPS]
        stats1 = late([P, KT, B, NTB, 6])
        mv1 = late([P, KT, 2])
        bn = late([P, 4, KT])
        q_mean = late([P, KT, HEADS1])
        rows_n, part_n = KT * RS * IMG, KT * (PERIOD - 1) * GROUPS * IMG
        shared = late([P, rows_n + part_n])
        rows_i = shared[:, 0:rows_n].rearrange("p (k r c) -> p k r c", k=KT, r=RS)
        part_i = shared[:, rows_n:].rearrange("p (k r c) -> p k r c", k=KT, r=PERIOD - 1)
        zi = late([P, KT, NKEY])
        z_rev = shared[:, 0:KT * NKEY].rearrange("p (k n) -> p k n", k=KT)
        kn = shared[:, KT * NKEY:KT * NKEY + JT * C].rearrange("p (j c) -> p j c", j=JT)
        k_sq = shared[:, KT * NKEY + JT * C:KT * NKEY + 2 * JT * C].rearrange("p (j c) -> p j c", j=JT)
        o_part = shared[:, 0:2 * KT * TB].rearrange("p (a k n) -> p a k n", a=2, k=KT)
        q_rs = shared[:, 2 * KT * TB:2 * KT * TB + TB]
        q_sd = shared[:, 2 * KT * TB + TB:2 * KT * TB + 2 * TB]
        vv = late([P, JT, C])
        k_st = late([P, 4, JT, HEADS1])
        kv = late([P, KT, P])
        kvg = late([P, KT, P])
        kv_c = late([P, KT])
        bias_v = late([P, KT, NKEY])
        q_sq = late([P, KT, TB])
        var_cols = late([P, (NTB - 1) * TILE_HEADS + VAR_ROWS])
        head_of = late([P, NTB * P])

        spare, used = Z[:, :, :].rearrange("p k n -> p (k n)"), [0]

        def carve(n, *names, **sizes):
            used[0] += n
            part = spare[:, used[0] - n:used[0]]
            return part.rearrange(f"p ({' '.join(names)}) -> p {' '.join(names)}", **sizes) if names else part

        table_words = table[:, :, :].rearrange("p h n -> p (h n)")
        w_mlp = table_words[:, 0:KT * C].rearrange("p (k c) -> p k c", k=KT)
        w2q = table_words[:, KT * C:(KT + 2) * C].rearrange("p (k c) -> p k c", k=2)
        w2v = table_words[:, (KT + 2) * C:(KT + 3) * C].rearrange("p (k c) -> p k c", k=KT)
        w2e = table_words[:, (KT + 3) * C:(KT + 4) * C]
        u_all = carve(KT * P, "k", "c", k=KT)
        u_col = late([P, KT])
        b2all = carve(2 * P, "k", "c", k=2)
        c2 = late([P, 4])
        relu_h = carve(KT * TB, "k", "n", k=KT)
        xsum = late([P, B, KT, NTB])
        xs = late([P, B, KT])
        v_sum = late([P, B])
        mixed = late([P, B, KT])
        s_relu = carve(TB)
        sums3 = late([P, 2, B, KT, NTB])
        tot3 = late([P, KT, 2, B])
        junk = carve(TB)
        xt = carve(4 * C, "r", "c", r=4)
        inv3 = late([P, B, KT])
        gram_s = carve(KT * C, "k", "c", k=KT)
        cos = carve(KT * C, "k", "c", k=KT)
        top = late([P, KT, 8])
        top_i = late([P, KT, 8], U32)
        top_f = late([P, KT, 8])
        count = late([P, C])
        pick = carve(KT * C, "k", "c", k=KT)
        pick_t = carve(KT * C, "k", "c", k=KT)
        g3 = late([P, KT, 2, B])
        st3 = late([P, 6, KT, B])

        st = [ctx.enter_context(nc.psum_tensor(f"st{i}", [P, 2, TB], F32)) for i in range(2)]
        mx = [ctx.enter_context(nc.psum_tensor(f"mx{i}", [P, TB], F32)) for i in range(2)]
        pvo = ctx.enter_context(nc.psum_tensor("pvo", [P, TB], F32))
        misc = ctx.enter_context(nc.psum_tensor("misc", [P, TB], F32))
        bank = [st[0][:, 0, :], st[0][:, 1, :], st[1][:, 0, :], st[1][:, 1, :], mx[0][:, :], mx[1][:, :],
                pvo[:, :], misc[:, :]]

        consts_ready = sem("consts_ready")
        ident_ready = sem("ident_ready")
        x_loaded = [sem(f"x_loaded{b}") for b in range(B)]
        weights_loaded = sem("weights_loaded")
        pool_chain = sem("pool_chain")
        dve_chain = sem("dve_chain")
        ch_mean_ready = sem("ch_mean_ready")
        group_mean_ready = sem("group_mean_ready")
        ch_spread_ready = sem("ch_spread_ready")
        group_var_ready = sem("group_var_ready")
        sd_ready = sem("sd_ready")
        affine_ready = sem("affine_ready")
        bias_ready = sem("bias_ready")
        bv_ready = sem("bv_ready")
        out_bias_ready = sem("out_bias_ready")
        b_out_ready = sem("b_out_ready")
        y_init = sem("y_init")
        head_w_ready = sem("head_w_ready")
        head_wp_ready = sem("head_wp_ready")
        qk_ready = sem("qk_ready")
        hi_done = sem("hi_done")
        lo_done = sem("lo_done")
        v_ready = sem("v_ready")
        v_copied = sem("v_copied")
        mx_ready = sem("mx_ready")
        mx_free = sem("mx_free")
        neg_max_ready = sem("neg_max_ready")
        max_turned = sem("max_turned")
        max_hi_ready = sem("max_hi_ready")
        max_cols_ready = sem("max_cols_ready")
        max_row_ready = sem("max_row_ready")
        st_ready = sem("st_ready")
        exp_done = sem("exp_done")
        pv_done = sem("pv_done")
        pool_sums = sem("pool_sums")
        dve_sums = sem("dve_sums")
        pool_total_ready = sem("pool_total_ready")
        dve_folded = sem("dve_folded")
        total_ready = sem("total_ready")
        total_turned = sem("total_turned")
        inv_ready = sem("inv_ready")
        inv_spread = sem("inv_spread")
        o_copied = sem("o_copied")
        o_norm_ready = sem("o_norm_ready")
        proj_ready = sem("proj_ready")
        y_added = sem("y_added")
        layer0_done = sem("layer0_done")
        early_stats = sem("early_stats")

        weights1_loaded = sem("weights1_loaded")
        weights2_loaded = sem("weights2_loaded")
        table_loaded = sem("table_loaded")
        pool1_chain = sem("pool1_chain")
        dve1_chain = sem("dve1_chain")
        var1_ready = sem("var1_ready")
        sd1_ready = sem("sd1_ready")
        affine1_ready = sem("affine1_ready")
        border_ready = sem("border_ready")
        diag_ready = sem("diag_ready")
        wq1_ready = sem("wq1_ready")
        h_ready = sem("h_ready")
        conv_part = sem("conv_part")
        conv_taken = sem("conv_taken")
        conv_step = sem("conv_step")
        zi_ready = sem("zi_ready")
        kv_ready = sem("kv_ready")
        v_got = sem("v_got")
        k_var_ready = sem("k_var_ready")
        k_sd_ready = sem("k_sd_ready")
        kn_ready = sem("kn_ready")
        kk_ready = sem("kk_ready")
        kvm_ready = sem("kvm_ready")
        kvc_ready = sem("kvc_ready")
        bias_part = sem("bias_part")
        bias_v_ready = sem("bias_v_ready")
        q_ready = sem("q_ready")
        q_kept = sem("q_kept")
        q_sq_ready = sem("q_sq_ready")
        q_var_part = sem("q_var_part")
        q_sd_ready = sem("q_sd_ready")
        q_rs_ready = sem("q_rs_ready")
        q_rs_spread = sem("q_rs_spread")
        q_rs_copied = sem("q_rs_copied")
        o_scaled = sem("o_scaled")
        o_ready = sem("o_ready")
        o_placed = sem("o_placed")
        pw_ready = sem("pw_ready")
        x_added = sem("x_added")
        mlp_in = sem("mlp_in")
        mlp_ready = sem("mlp_ready")
        mlp_added = sem("mlp_added")
        l2_a = sem("l2_a")
        l2_b = sem("l2_b")
        mix_a = sem("mix_a")
        mix_b = sem("mix_b")
        gate_ready = sem("gate_ready")
        s_relu_ready = sem("s_relu_ready")
        x3_ready = sem("x3_ready")
        sq3_ready = sem("sq3_ready")
        turned3 = sem("turned3")
        xt_ready = sem("xt_ready")
        gram_ready = sem("gram_ready")
        norm3_ready = sem("norm3_ready")
        nrm3_ready = sem("nrm3_ready")
        gram_scaled = sem("gram_scaled")
        gram_turned = sem("gram_turned")
        cos_added = sem("cos_added")
        pick_ready = sem("pick_ready")
        pick_turned = sem("pick_turned")
        pick_t_ready = sem("pick_t_ready")
        group_sums = sem("group_sums")
        var3_ready = sem("var3_ready")
        sd3_ready = sem("sd3_ready")
        affine3_ready = sem("affine3_ready")
        out_ready = [sem(f"out_ready{k}") for k in range(KT)]
        stored = sem("stored")

        def exps(g, j):
            return g * NPAIR + (j + 1)

        def pvs(g, j):
            return g * NPAIR + (j + 1 + NBUF)

        def pool_summed(g, j):
            return g * POOL_PAIRS + (POOL_PAIRS + j + 1)

        def dve_summed(g, j):
            return g * DVE_PAIRS + (DVE_PAIRS + j + 1)

        CONSTS1 = KT * sum(PE_TAPS) + TILE_HEADS + KT + 1

        def convs(n, i):
            return (i + n * NTB) * KT

        def dve_steps(n):
            return KT * (len(TAPS) - PE_TAPS[n % 2] - 1)

        def conv_steps(n, i):
            return i * dve_steps(n) + NTB * sum(dve_steps(c) for c in range(n))

        x_t = x.rearrange("b (k p) h w -> b p k (h w)", p=P)
        out_t = out.rearrange("b (k p) h w -> b p k (h w)", p=P)
        block = ctx.enter_context(nc.Block())

        @block.sync
        def _(sp):
            sp.dma_start(vec[:, :], vectors).then_inc(weights_loaded, 16)
            for b in range(B):
                for k in range(KT):
                    sp.dma_start(X[:, b, k, :], x_t[b, :, k, :]).then_inc(x_loaded[b], 16)
                if b == 0:
                    sp.dma_start(wqkv[:, :, :], w_qkv_t.rearrange("(k p) o -> p k o", p=P)).then_inc(weights_loaded, 16)
                    sp.dma_start(wproj[:, :, :], w_proj_t.rearrange("(k p) o -> p k o", p=P)).then_inc(weights_loaded, 16)
                    for half in range(2):
                        sp.dma_start(wproj2[half * DH:(half + 1) * DH, :, :],
                                     w_proj_t.rearrange("(h d) o -> d h o", d=DH)).then_inc(weights_loaded, 16)

            def load_weights():
                for dst, src in ((w1, w1_t), (w_out, w_out_t)):
                    sp.dma_start(dst[:, :, :], src.rearrange("(k p) o -> p k o", p=P)).then_inc(weights1_loaded, 16)
                sp.dma_start(k_gb[:, :, :], k_norm).then_inc(weights1_loaded, 16)

            def load_late_weights():
                sp.wait_ge(bias_part, B * KT)
                for dst, src in ((w_mlp, mlp_t), (w2v, w2_v_t)):
                    sp.dma_start(dst[:, :, :], src.rearrange("(k p) o -> p k o", p=P)).then_inc(weights2_loaded, 16)
                sp.dma_start(w2q[:, :, :], w2_qk).then_inc(weights2_loaded, 16)
                sp.dma_start(w2e[:, :], w2_exp_t).then_inc(weights2_loaded, 16)

            def load_table():
                for r in range(P // RS):
                    first = rel_table[:, r * TABLE:r * TABLE + BIAS_RUN]
                    src = bass.AP(first.tensor, first.offset, [[1, RS], [TABLE * TABLE, HEADS1], [1, BIAS_RUN]])
                    sp.dma_start(table[r * RS:(r + 1) * RS, :, 0:BIAS_RUN], src).then_inc(table_loaded, 16)

            def store_out():
                for b in range(B):
                    for k in range(KT):
                        sp.wait_ge(out_ready[k], b + 1)
                        sp.dma_start(out_t[b, :, k, :], X[:, b, k, :]).then_inc(stored, 16)
                sp.wait_ge(stored, 16 * B * KT)

            sp.wait_ge(layer0_done, B)
            load_weights()
            load_table()
            load_late_weights()
            store_out()

        @block.gpsimd
        def _(pool):
            pool.memset(eps[:, 0:1], EPS_BN).then_inc(consts_ready, 1)
            pool.memset(eps[:, 1:2], EPS_LN).then_inc(consts_ready, 1)
            pool.memset(ones[:, :], 1.0).then_inc(consts_ready, 1)
            pool.memset(ident[:, :], 0.0).then_inc(pool_chain, 1)
            pool.memset(mean8[:, :], 1.0 / GROUP0).then_inc(pool_chain, 1)
            pool.memset(mean32[:, :], 1.0 / 32).then_inc(pool_chain, 1)
            pool.wait_ge(pool_chain, 3)
            pool.affine_select(out=ident[:, :], in_=ident[:, :], compare_op=ALU.not_equal, fill=1.0,
                               base=0, pattern=[[-1, P]], channel_multiplier=1).then_inc(ident_ready, 1)
            chain = 3
            for m, n in ((mean8, GROUP0), (mean32, 32)):
                blocks = m[:, :].rearrange("p (a c) -> p a c", c=n)
                pool.affine_select(out=blocks, in_=blocks, compare_op=ALU.is_ge, fill=0.0, base=0,
                                   pattern=[[-n, P // n], [0, n]], channel_multiplier=1).then_inc(pool_chain, 1)
                chain += 1
                pool.wait_ge(pool_chain, chain)
                pool.affine_select(out=blocks, in_=blocks, compare_op=ALU.is_ge, fill=0.0, base=n - 1,
                                   pattern=[[n, P // n], [0, n]], channel_multiplier=-1).then_inc(consts_ready, 1)

            def later_constants():
                pool.wait_ge(consts_ready, CONSTS)
                for n, name in enumerate(("dw1", "dw2")):
                    for k in range(KT):
                        for t in range(PE_TAPS[n]):
                            pool.tensor_scalar(diag[n][:, k, t, :], ident[:, :], col(name, k * 9 + t), 0.0,
                                               ALU.mult, ALU.add).then_inc(diag_ready, 1)
                pool.iota(count[:, :], pattern=[[1, C]], base=0, channel_multiplier=0,
                          allow_small_or_imprecise_dtypes=True).then_inc(diag_ready, 1)
                row0 = (NTB - 1) * TILE_HEADS
                pool.memset(var_cols[:, :], 0.0).then_inc(pool1_chain, 1)
                pool.memset(head_of[:, :], 1.0).then_inc(pool1_chain, 1)
                pool.wait_ge(pool1_chain, 2)
                for h in range(TILE_HEADS):
                    pool.tensor_copy(var_cols[:, row0 + h:row0 + h + 1], mean32[:, h * D1:h * D1 + 1])\
                        .then_inc(diag_ready, 1)
                for half in range(KT):
                    rows = head_of[half * VAR_ROWS:(half + 1) * VAR_ROWS, :]
                    pool.affine_select(out=rows, in_=rows, compare_op=ALU.is_ge, fill=0.0, base=0,
                                       pattern=[[1, NTB * P]], channel_multiplier=-D1).then_inc(pool1_chain, 1)
                    pool.wait_ge(pool1_chain, 3 + half)
                    pool.affine_select(out=rows, in_=rows, compare_op=ALU.is_ge, fill=0.0, base=D1 - 1,
                                       pattern=[[-1, NTB * P]], channel_multiplier=D1).then_inc(diag_ready, 1)

            pool.sem_inc(pool_sums, POOL_PAIRS)
            pool.sem_inc(pool_total_ready, 1)

            def sums(g):
                for j in range(1, POOL_PAIRS):
                    pool.wait_ge(exp_done, exps(g, j))
                    if j == 1:
                        pool.wait_ge(pool_total_ready, g + 1)
                        pool.tensor_tensor(acc_pool[:, :, :], prob[:, 0, :, :], prob[:, 1, :, :],
                                           ALU.add).then_inc(pool_sums, 2)
                    else:
                        pool.wait_ge(pool_sums, pool_summed(g, j - 1))
                        pool.tensor_tensor(acc_pool[:, :, :], acc_pool[:, :, :], prob[:, j % NBUF, :, :],
                                           ALU.add).then_inc(pool_sums, 1)
                pool.wait_ge(pool_sums, pool_summed(g, POOL_PAIRS - 1))
                pool.tensor_tensor(pool_total[:, :], acc_pool[:, 0, :], acc_pool[:, 1, :],
                                   ALU.add).then_inc(pool_total_ready, 1)

            for b in range(B):
                pool.wait_ge(b_out_ready, b + 1)
                for k in range(KT):
                    last = pool.tensor_scalar(Y[:, k, :], X[:, b, k, :], 1.0, b_out[:, k:k + 1], ALU.mult, ALU.add)
                last.then_inc(y_init, 1)
                with pool.Fori(0, NH) as h:
                    hh = h + b * NH
                    pool.wait_ge(y_added, hh * (NTB * KT) + KT)
                    pool.wait_ge(weights_loaded, 16 * 5)
                    pool.tensor_copy(wp_head[:, :], wproj2[:, ds(h, 1), :].rearrange("p a o -> p (a o)"))\
                        .then_inc(head_wp_ready, 1)
                    with pool.Fori(0, NTB) as tb:
                        sums(hh * NTB + tb)
            pool.wait_ge(layer0_done, B)
            pool.memset(H[:, :, :, :], 0.0).then_inc(border_ready, 1)
            later_constants()

        @block.scalar
        def _(act):
            def attention_layer():
                def prepare(hh, tail):
                    if tail:
                        copy_out(hh * NTB + (-1))
                    act.wait_ge(head_w_ready, hh + 1)
                    q, k = slice(0, DH), slice(DH, P)
                    for i in range(NTB):
                        cols = slice(i * TB, (i + 1) * TB)
                        act.wait_ge(qk_ready, hh * NTB + (i + 1))
                        for dst, half in ((q_hh[q, cols], q), (k_hl[k, cols], k)):
                            act.activation(dst, st[i // 2 % 2][half, i % 2, :], ACT.Identity,
                                           bias=b_head[half, 0:1]).then_inc(hi_done, 1)
                        act.wait_ge(hi_done, (hh * NTB + i) * PARTS + 2)
                        for dst, src in ((q_hh[k, cols], q_hh[q, cols]), (k_h1[k, cols], k_hl[k, cols])):
                            act.activation(dst, src, ACT.Copy).then_inc(hi_done, 1)
                        act.wait_ge(v_ready, hh * NTB + (i + 1))
                        act.activation(v_sb[:, SUBS * i:SUBS * (i + 1), :],
                                       pvo[:, 0:SUBS * DH].rearrange("p (s d) -> p s d", d=DH),
                                       ACT.Copy).then_inc(v_copied, 1)

                def max_row(g, tb):
                    act.wait_ge(max_turned, g + 1)
                    act.activation(q_lm[0:LO_ROW + 1, ds(tb * TB, TB)], misc[0:LO_ROW + 1, :], ACT.Copy)\
                        .then_inc(max_row_ready, 1)

                def copy_out(g):
                    act.wait_ge(pv_done, pvs(g, NPAIR - 1))
                    act.activation(o_raw[:, :], pvo[:, :], ACT.Copy).then_inc(o_copied, 1)

                def step(g, tb, tail, turn):
                    for j in range(NPAIR):
                        act.wait_ge(st_ready, exps(g, j))
                        act.wait_ge(pv_done, g * NPAIR + (j + 1))
                        if j >= NBUF:
                            act.wait_ge(pool_sums, pool_summed(g, j - NBUF))
                        else:
                            act.wait_ge(dve_sums, g * DVE_PAIRS + (j + 1))
                        act.activation(prob[:, j % NBUF, :, :], st[j % 2][:, :, :], ACT.Exp,
                                       scale=SCALE0).then_inc(exp_done, 1)
                        if j == 0 and tail:
                            copy_out(g + (-1))
                        if turn and j == TURN_SLOT:
                            max_row(g + 1, tb + 1)

                def steps(hh):
                    max_row(hh * NTB, 0)
                    step(hh * NTB, 0, tail=False, turn=True)
                    with act.Fori(1, NTB - 1) as tb:
                        step(hh * NTB + tb, tb, tail=True, turn=True)
                    step(hh * NTB + (NTB - 1), NTB - 1, tail=True, turn=False)

                act.wait_ge(consts_ready, CONSTS)
                act.sem_inc(o_copied, 1)
                for b in range(B):
                    act.wait_ge(group_var_ready, b + 1)
                    act.activation(gn[:, 3, :], misc[:, 4:4 + KT], ACT.Sqrt, bias=eps[:, 0:1]).then_inc(sd_ready, 1)
                    prepare(b * NH, tail=False)
                    with act.Fori(0, NH - 1) as h:
                        steps(h + b * NH)
                        prepare(h + (b * NH + 1), tail=True)
                    steps(b * NH + NH - 1)
                    copy_out((b + 1) * NH * NTB - 1)

            def later_layers():
                def sqrt_of(dst, src, e):
                    return act.activation(dst, src, ACT.Sqrt, bias=eps[:, e:e + 1])

                def fill_h(b):
                    if b > 0:
                        act.wait_ge(conv_step, conv_steps(2 * b, 0))
                        act.wait_ge(conv_part, convs(2 * b, 0))
                    for k in range(KT):
                        act.activation(H[:, k, 1:1 + IMG, 1:1 + IMG],
                                       X[:, b, k, :].rearrange("p (r c) -> p r c", c=IMG), ACT.Identity,
                                       scale=bn[:, 2, k:k + 1], bias=bn[:, 3, k:k + 1]).then_inc(h_ready, 1)

                def keys_and_queries(b):
                    act.wait_ge(conv_step, conv_steps(2 * b + 1, 0))
                    for i in range(NTB):
                        n = (b * NTB + i) * KT
                        for m in range(KT):
                            act.wait_ge(q_ready, n + m + 1)
                            q_bank = bank[i % 2 * 2 + m][:, :]
                            act.activation(H[:, m, 1 + i * ROWS:1 + (i + 1) * ROWS, 1:1 + IMG],
                                           q_bank.rearrange("p (r c) -> p r c", c=IMG), ACT.Copy).then_inc(q_kept, 1)
                            if i > 0:
                                act.wait_ge(q_var_part, n - KT + m + 1)
                            act.activation(q_sq[:, m, :], q_bank, ACT.Square).then_inc(q_sq_ready, 1)
                        if i == KV_AT:
                            for j in range(JT):
                                act.wait_ge(kv_ready, b * JT + j + 1)
                                act.activation(vv[:, j, :], bank[4 + j][:, C:2 * C], ACT.Copy).then_inc(v_got, 1)
                    act.wait_ge(k_var_ready, b + 1)
                    sqrt_of(k_st[:, 2, :, :], k_st[:, 1, :, :], 1).then_inc(k_sd_ready, 1)
                    act.wait_ge(q_var_part, (b + 1) * NTB * KT)
                    sqrt_of(q_sd[:, :], bank[7][:, :], 1).then_inc(q_sd_ready, 1)

                def outputs(b):
                    for i in range(NTB):
                        n = (b * NTB + i) * KT
                        for m in range(KT):
                            act.wait_ge(q_rs_spread, n + m + 1)
                            if i >= 2:
                                act.wait_ge(o_placed, n - KT + m + 1)
                            act.activation(o_part[:, i % 2, m, :], bank[m][:, :], ACT.Copy).then_inc(q_rs_copied, 1)

                def layer1():
                    act.wait_ge(var1_ready, 1)
                    sqrt_of(bn[:, 0, :], mv1[:, :, 1], 0).then_inc(sd1_ready, 1)
                    act.wait_ge(affine1_ready, 1)
                    act.wait_ge(border_ready, 1)
                    for b in range(B):
                        fill_h(b)
                        keys_and_queries(b)
                        outputs(b)
                    act.wait_ge(var1_ready, 2)
                    sqrt_of(bn[:, 0, :], mv1[:, :, 1], 0).then_inc(sd1_ready, 1)

                def mlp(b):
                    with act.Fori(0, NTB) as i:
                        n = (i + b * NTB) * KT
                        act.wait_ge(mlp_ready, n + KT)
                        for k in range(KT):
                            act.activation(relu_h[:, k, :], X[:, b, k, ds(i * TB, TB)], ACT.Relu,
                                           scale=bn[:, 2, k:k + 1], bias=bn[:, 3, k:k + 1]).then_inc(mlp_in, 1)

                def gates(b):
                    for i in range(NTB):
                        n = b * NTB + i
                        act.wait_ge(gate_ready, n + 1)
                        if n > 0:
                            act.wait_ge(x3_ready, n * KT)
                        act.activation(s_relu[:, :], bank[n % 2][:, :], ACT.Relu, bias=c2[:, 1:2]).then_inc(s_relu_ready, 1)
                        for k in range(KT):
                            act.wait_ge(x3_ready, n * KT + k + 1)
                            if n * KT + k > 0:
                                act.wait_ge(sq3_ready, n * KT + k)
                            act.activation(junk[:, :], X[:, b, k, i * TB:(i + 1) * TB], ACT.Square,
                                           accum_out=sums3[:, 1, b, k, i:i + 1]).then_inc(sq3_ready, 1)

                def layer23():
                    act.wait_ge(affine1_ready, 2)
                    for b in range(B):
                        mlp(b)
                    for b in range(B):
                        gates(b)
                    act.wait_ge(norm3_ready, 1)
                    act.activation(st3[:, 0, :, :], tot3[:, :, 1, :], ACT.Sqrt).then_inc(nrm3_ready, 1)
                    act.wait_ge(var3_ready, 1)
                    sqrt_of(st3[:, 3, :, :], st3[:, 2, :, :], 0).then_inc(sd3_ready, 1)
                    act.wait_ge(affine3_ready, 1)
                    for b in range(B):
                        act.activation(X[:, b, 0, :], X[:, b, 0, :], ACT.Identity, scale=st3[:, 4, 0, b:b + 1],
                                       bias=st3[:, 5, 0, b:b + 1]).then_inc(out_ready[0], 1)

                layer1()
                layer23()

            attention_layer()
            later_layers()

        @block.vector
        def _(dve):
            def attention_layer():
                chain = [0]

                def link(ins):
                    chain[0] += 1
                    ins.then_inc(dve_chain, 1)
                    dve.wait_ge(dve_chain, chain[0])

                dve.sem_inc(mx_free, 2)
                dve.sem_inc(dve_sums, DVE_PAIRS)
                dve.sem_inc(y_added, KT)
                dve.memset(q_lm[0:DH, :], 0.0)
                dve.memset(max_cols[:, :, :], 0.0)
                link(dve.memset(k_h1[0:DH, :], 0.0))
                dve.memset(k_h1[0:1, :], 1.0)
                link(dve.memset(k_h1[LO_ROW:LO_ROW + 1, :], 1.0))
                dve.wait_ge(ident_ready, 1)
                dve.tensor_copy(ident_bf[:, :], ident[:, :]).then_inc(consts_ready, 1)

                def group_norm(b):
                    dve.wait_ge(x_loaded[b], 16 * KT)
                    if b == 0:
                        for k in range(KT):
                            for i in range(NTB):
                                last = dve.bn_stats(stats[:, k, i, :], X[:, b, k, i * TB:(i + 1) * TB])
                            link(last)
                    else:
                        dve.wait_ge(early_stats, KT * NTB)
                    for k in range(KT):
                        last = dve.bn_aggr(mv[:, k, :], stats[:, k, :, :].rearrange("p i s -> p (i s)"))
                    link(last)
                    link(dve.tensor_copy(gn[:, 0, :], mv[:, :, 0]))
                    dve.tensor_copy(gn[:, 1, :], mv[:, :, 1]).then_inc(ch_mean_ready, 1)
                    dve.wait_ge(ch_mean_ready, b + 1)
                    dve.wait_ge(group_mean_ready, b + 1)
                    link(dve.tensor_copy(gn[:, 2, :], misc[:, 0:KT]))
                    link(dve.tensor_tensor(gn[:, 4, :], gn[:, 0, :], gn[:, 2, :], ALU.subtract))
                    link(dve.tensor_tensor(gn[:, 4, :], gn[:, 4, :], gn[:, 4, :], ALU.mult))
                    dve.tensor_tensor(gn[:, 4, :], gn[:, 4, :], gn[:, 1, :], ALU.add).then_inc(ch_spread_ready, 1)
                    dve.wait_ge(sd_ready, b + 1)
                    link(dve.reciprocal(gn[:, 5, :], gn[:, 3, :]))
                    link(dve.tensor_tensor(gn[:, 5, :], gn[:, 5, :], col("gn_scale", 0, KT), ALU.mult))
                    link(dve.tensor_tensor(gn[:, 6, :], gn[:, 2, :], gn[:, 5, :], ALU.mult))
                    dve.tensor_tensor(gn[:, 6, :], col("gn_bias", 0, KT), gn[:, 6, :], ALU.subtract)\
                        .then_inc(affine_ready, 1)
                    dve.wait_ge(bias_ready, b + 1)
                    link(dve.tensor_tensor(b_qk[:, :], misc[:, 8:8 + NH], col("b_qk", 0, NH), ALU.add))
                    dve.tensor_tensor(b_v[:, :], misc[:, 16:16 + KT], col("b_v", 0, KT), ALU.add).then_inc(bv_ready, 1)
                    dve.wait_ge(out_bias_ready, b + 1)
                    dve.tensor_tensor(b_out[:, :], misc[:, 24:24 + KT], col("b_proj", 0, KT), ALU.add).then_inc(b_out_ready, 1)
                    dve.wait_ge(b_out_ready, b + 1)

                def prepare(hh, h, tail):
                    dve.tensor_copy(b_head[:, :], b_qk[:, ds(h, 1)])
                    for k in range(KT):
                        dve.tensor_scalar(w_head[:, k, 0:2 * DH], wqkv[:, k, ds(h * (2 * DH), 2 * DH)],
                                          gn[:, 5, k:k + 1], None, ALU.mult)
                        last = dve.tensor_scalar(w_head[:, k, 2 * DH:QKV], wqkv[:, k, ds(h * DH + V_COL, DH)],
                                                 gn[:, 5, k:k + 1], None, ALU.mult)
                    last.then_inc(head_w_ready, 1)
                    dve.wait_ge(head_w_ready, hh + 1)
                    q, k = slice(0, DH), slice(DH, P)
                    g_last = hh * NTB + (-1)
                    if tail:
                        all_sums(g_last)
                    for i in range(NTB + LAG):
                        units = range((i - LAG) * SUBS, (i - LAG + 1) * SUBS) if i >= LAG else ()
                        for u in units:
                            unit_max(hh * NTB, u)
                        if i < NTB:
                            cols = slice(i * TB, (i + 1) * TB)
                            for dst, half, hi in ((q_lm[k, cols], q, q_hh[q, cols]), (k_hl[q, cols], k, k_hl[k, cols])):
                                dve.wait_ge(hi_done, (hh * NTB + i) * PARTS + 2)
                                dve.scalar_tensor_tensor(dst, st[i // 2 % 2][half, i % 2, :], b_head[half, 0:1], hi,
                                                         ALU.add, ALU.subtract).then_inc(lo_done, 1)
                        if tail and i == 0:
                            invert(g_last)
                        if tail and i == 1:
                            normalise(g_last)
                        if tail and 2 <= i < TAIL_STAGES:
                            add_out(g_last, NTB - 1, i - 2, Y)
                    row_max(hh * NTB)

                def unit_max(g, u):
                    dve.wait_ge(mx_ready, g * UNITS + (u + 1))
                    dve.tensor_reduce(part_max[:, u % SUBS, u // SUBS:u // SUBS + 1], mx[u % 2][:, :], AX.X,
                                      ALU.max).then_inc(mx_free, 1)

                def row_max(g):
                    dve.wait_ge(mx_free, g * UNITS + (UNITS + 2))
                    dve.tensor_reduce(neg_max[:, :], part_max[:, :, :], AX.X, ALU.max, negate=True)\
                        .then_inc(neg_max_ready, 1)
                    dve.wait_ge(neg_max_ready, g + 1)
                    dve.tensor_copy(max_cols[:, :, 0], neg_max[:, :]).then_inc(max_hi_ready, 1)
                    dve.wait_ge(max_hi_ready, g + 1)
                    dve.tensor_tensor(max_cols[:, :, LO_ROW], neg_max[:, :], max_cols[:, :, 0], ALU.subtract)\
                        .then_inc(max_cols_ready, 1)

                def pair_sum(g, i):
                    j = POOL_PAIRS + i
                    dve.wait_ge(exp_done, exps(g, j))
                    if i == 0:
                        dve.tensor_copy(acc_dve[:, :, :], prob[:, j % NBUF, :, :]).then_inc(dve_sums, 1)
                    else:
                        dve.wait_ge(dve_sums, dve_summed(g, i - 1))
                        dve.tensor_tensor(acc_dve[:, :, :], acc_dve[:, :, :], prob[:, j % NBUF, :, :],
                                          ALU.add).then_inc(dve_sums, 1)

                def all_sums(g):
                    pair_sum(g, DVE_PAIRS - 1)
                    dve.wait_ge(dve_sums, dve_summed(g, DVE_PAIRS - 1))
                    dve.tensor_tensor(total[:, :], acc_dve[:, 0, :], acc_dve[:, 1, :], ALU.add).then_inc(dve_folded, 1)
                    dve.wait_ge(dve_folded, g + 1)
                    dve.wait_ge(pool_total_ready, g + 2)
                    dve.tensor_tensor(total[:, :], total[:, :], pool_total[:, :], ALU.add).then_inc(total_ready, 1)

                def invert(g):
                    dve.wait_ge(total_turned, g + 1)
                    dve.reciprocal(inv_cols[:, :], misc[:, 0:SUBS]).then_inc(inv_ready, 1)

                def normalise(g):
                    dve.wait_ge(o_copied, g + 2)
                    dve.wait_ge(inv_spread, g + 1)
                    dve.tensor_tensor(o_norm[:, :], o_raw[:, :], misc[:, :], ALU.mult).then_inc(o_norm_ready, 1)

                def add_out(g, tb, m, to):
                    dve.wait_ge(proj_ready, g * KT + (m + 1))
                    y = Y[:, m, ds(tb * TB, TB)]
                    dve.tensor_tensor(to[:, m, ds(tb * TB, TB)], misc[:, :], y, ALU.add).then_inc(y_added, 1)

                def step(g, tb, tail, turn, to, spare=None):
                    if tail:
                        all_sums(g + (-1))
                    for j in range(NPAIR):
                        if turn:
                            for u in SLOTS[j]:
                                unit_max(g + 1, u)
                        if tail and j == SUM_SLOT:
                            invert(g + (-1))
                        if tail and j == INV_SLOT:
                            normalise(g + (-1))
                        if tail and j in PROJ_SLOTS:
                            add_out(g + (-1), tb + (-1), PROJ_SLOTS.index(j), to)
                        if turn and j == LAST_UNIT_SLOT:
                            row_max(g + 1)
                        if j > POOL_PAIRS:
                            pair_sum(g, j - 1 - POOL_PAIRS)
                        elif spare:
                            spare(j)

                def steps(hh, to, spare=None):
                    step(hh * NTB, 0, tail=False, turn=True, to=to)
                    with dve.Fori(1, NTB - 1) as tb:
                        step(hh * NTB + tb, tb, tail=True, turn=True, to=to)
                    step(hh * NTB + (NTB - 1), NTB - 1, tail=True, turn=False, to=to, spare=spare)

                def tail_alone(g, tb, to):
                    all_sums(g)
                    invert(g)
                    normalise(g)
                    for m in range(KT):
                        add_out(g, tb, m, to)

                def next_stats(b):
                    def f(j):
                        if 1 <= j <= NTB:
                            for k in range(KT):
                                if b == 0:
                                    dve.wait_ge(x_loaded[1], 16 * KT)
                                    dve.bn_stats(stats[:, k, j - 1, :], X[:, 1, k, (j - 1) * TB:j * TB])\
                                        .then_inc(early_stats, 1)
                                else:
                                    dve.wait_ge(layer0_done, 1)
                                    dve.bn_stats(first_stats[:, k, j - 1, :], X[:, 0, k, (j - 1) * TB:j * TB])\
                                        .then_inc(early_stats, 1)
                    return f

                for b in range(B):
                    if b == 0:
                        dve.wait_ge(weights_loaded, 16 * 5)
                    group_norm(b)
                    prepare(b * NH, 0, tail=False)
                    dve.wait_ge(y_init, b + 1)
                    with dve.Fori(0, NH - 1) as h:
                        steps(h + b * NH, Y)
                        prepare(h + (b * NH + 1), h + 1, tail=True)
                    steps(b * NH + NH - 1, X[:, b, :, :], next_stats(b))
                    tail_alone((b + 1) * NH * NTB - 1, NTB - 1, X[:, b, :, :])
                    dve.wait_ge(y_added, (b + 1) * NH * NTB * KT + KT)
                    dve.sem_inc(layer0_done, 1)
                    dve.wait_ge(layer0_done, b + 1)

            def later_layers():
                chain1 = [0]

                def link1(ins):
                    chain1[0] += 1
                    ins.then_inc(dve1_chain, 1)
                    dve.wait_ge(dve1_chain, chain1[0])

                def batch_stats(g, beta, n):
                    for k in range(KT):
                        for b in range(B):
                            for i in range(NTB):
                                if b > 0 or n > 1:
                                    last = dve.bn_stats(stats1[:, k, b, i, :], X[:, b, k, i * TB:(i + 1) * TB])
                        if n == 1:
                            dve.wait_ge(early_stats, 2 * KT * NTB)
                            last = dve.tensor_copy(stats1[:, k, 0, :, :], first_stats[:, k, :, :])
                        link1(last)
                    for k in range(KT):
                        last = dve.bn_aggr(mv1[:, k, :], stats1[:, k, :, :, :].rearrange("p b i s -> p (b i s)"))
                    last.then_inc(var1_ready, 1)
                    dve.wait_ge(var1_ready, n)
                    dve.wait_ge(sd1_ready, n)
                    link1(dve.reciprocal(bn[:, 1, :], bn[:, 0, :]))
                    link1(dve.tensor_tensor(bn[:, 2, :], bn[:, 1, :], col(g, 0, KT), ALU.mult))
                    link1(dve.tensor_tensor(bn[:, 1, :], mv1[:, :, 0], bn[:, 2, :], ALU.mult))
                    dve.tensor_tensor(bn[:, 3, :], col(beta, 0, KT), bn[:, 1, :], ALU.subtract).then_inc(affine1_ready, 1)

                def centre_wq():
                    for k in range(KT):
                        w = w1[:, k, 0:C].rearrange("p (h d) -> p h d", d=D1)
                        link1(dve.tensor_reduce(q_mean[:, k, :], w, AX.X, ALU.add))
                        link1(dve.tensor_scalar(q_mean[:, k, :], q_mean[:, k, :], 1.0 / D1, None, ALU.mult))
                        dve.tensor_tensor(w, w, q_mean[:, k, :].unsqueeze(2).broadcast_to([P, HEADS1, D1]),
                                          ALU.subtract).then_inc(wq1_ready, 1)

                def convolve(n, name, after=None):
                    out_of = Z

                    def blk(i):
                        steps = conv_steps(n, i)
                        first = PE_TAPS[n % 2]
                        for t in range(first, 9):
                            dy, dx = TAPS[t]
                            for k in range(KT):
                                src = H[:, k, ds(i * ROWS + dy, ROWS), dx:dx + IMG]
                                dst = out_of[:, k, ds(i * TB, TB)].rearrange("p (r c) -> p r c", c=IMG)
                                w = col(name, k * 9 + t)
                                if t == first:
                                    dve.wait_ge(conv_part, convs(n, i) + (k + 1))
                                    part = bank[k][:, :].rearrange("p (r c) -> p r c", c=IMG)
                                    dve.scalar_tensor_tensor(dst, src, w, part, ALU.mult, ALU.add)\
                                        .then_inc(conv_taken, 1)
                                else:
                                    if t == first + 1:
                                        dve.wait_ge(conv_taken, convs(n, i) + (k + 1 + KT))
                                    else:
                                        dve.wait_ge(conv_step, steps + ((t - first - 2) * KT + k + 1))
                                    dve.scalar_tensor_tensor(dst, src, w, dst, ALU.mult, ALU.add).then_inc(conv_step, 1)

                    if after is None:
                        with dve.Fori(0, NTB) as i:
                            blk(i)
                    else:
                        blk(0)
                        with dve.Fori(1, NTB) as i:
                            blk(i)
                            after(i + (-1))
                        after(NTB - 1)

                def downsample(b):
                    dve.wait_ge(conv_step, conv_steps(2 * b + 1, 0))
                    if b > 0:
                        dve.wait_ge(kv_ready, b * JT)
                    weights = []
                    for r in range(1, PERIOD):
                        f = np_f32(r * RATIO - int(r * RATIO))
                        weights.append((np_f32(1.0 - f), f, int(r * RATIO)))
                    for k in range(KT):
                        src = Z[:, k, :].rearrange("p (r c) -> p r c", c=IMG)
                        dst = rows_i[:, k, :, :]
                        last = dve.tensor_copy(dst[:, 0:RS:PERIOD, :], src[:, 0:IMG:PERIOD_ROWS, :])
                        for r, (_, f, i0) in enumerate(weights):
                            tmp = part_i[:, k, r, :].rearrange("p (g c) -> p g c", c=IMG)
                            last = dve.tensor_scalar(tmp, src[:, i0 + 1:i0 + 2 + (GROUPS - 1) * PERIOD_ROWS:PERIOD_ROWS, :],
                                                     f, None, ALU.mult)
                    link1(last)
                    for k in range(KT):
                        src = Z[:, k, :].rearrange("p (r c) -> p r c", c=IMG)
                        dst = rows_i[:, k, :, :]
                        for r, (w0, _, i0) in enumerate(weights):
                            tmp = part_i[:, k, r, :].rearrange("p (g c) -> p g c", c=IMG)
                            last = dve.scalar_tensor_tensor(
                                dst[:, r + 1:r + 2 + (GROUPS - 1) * PERIOD:PERIOD, :],
                                src[:, i0:i0 + 1 + (GROUPS - 1) * PERIOD_ROWS:PERIOD_ROWS, :], w0, tmp, ALU.mult, ALU.add)
                    link1(last)
                    for k in range(KT):
                        src = rows_i[:, k, :, :]
                        dst = zi[:, k, :].rearrange("p (r c) -> p r c", c=RS)
                        last = dve.tensor_copy(dst[:, :, 0:RS:PERIOD], src[:, :, 0:IMG:PERIOD_ROWS])
                        for r, (_, f, i0) in enumerate(weights):
                            tmp = part_i[:, k, r, 0:RS * GROUPS].rearrange("p (r g) -> p r g", g=GROUPS)
                            last = dve.tensor_scalar(tmp, src[:, :, i0 + 1:i0 + 2 + (GROUPS - 1) * PERIOD_ROWS:PERIOD_ROWS],
                                                     f, None, ALU.mult)
                    link1(last)
                    for k in range(KT):
                        src = rows_i[:, k, :, :]
                        dst = zi[:, k, :].rearrange("p (r c) -> p r c", c=RS)
                        for r, (w0, _, i0) in enumerate(weights):
                            tmp = part_i[:, k, r, 0:RS * GROUPS].rearrange("p (r g) -> p r g", g=GROUPS)
                            last = dve.scalar_tensor_tensor(
                                dst[:, :, r + 1:r + 2 + (GROUPS - 1) * PERIOD:PERIOD],
                                src[:, :, i0:i0 + 1 + (GROUPS - 1) * PERIOD_ROWS:PERIOD_ROWS], w0, tmp, ALU.mult, ALU.add)
                    link1(last)
                    for k in range(KT):
                        last = dve.tensor_copy(z_rev[:, k, :], zi[:, k, ::-1])
                    last.then_inc(zi_ready, 1)

                def keys(b):
                    def per_head(a):
                        return a.rearrange("p (h d) -> p h d", d=D1)

                    def spread(a):
                        return a.unsqueeze(2).broadcast_to([P, HEADS1, D1])

                    heads = "p j (h d) -> p j h d"
                    dve.wait_ge(v_got, (b + 1) * JT)
                    for j in range(JT):
                        last = dve.tensor_reduce(k_st[:, 0, j, :], per_head(bank[4 + j][:, 0:C]), AX.X, ALU.add)
                    link1(last)
                    link1(dve.tensor_scalar(k_st[:, 0, :, :], k_st[:, 0, :, :], 1.0 / D1, None, ALU.mult))
                    for j in range(JT):
                        last = dve.tensor_tensor(per_head(kn[:, j, :]), per_head(bank[4 + j][:, 0:C]), spread(k_st[:, 0, j, :]),
                                                 ALU.subtract)
                    link1(last)
                    link1(dve.tensor_tensor(k_sq[:, :, :], kn[:, :, :], kn[:, :, :], ALU.mult))
                    link1(dve.tensor_reduce(k_st[:, 1, :, :], k_sq[:, :, :].rearrange(heads, d=D1), AX.X, ALU.add))
                    dve.tensor_scalar(k_st[:, 1, :, :], k_st[:, 1, :, :], 1.0 / D1, None, ALU.mult).then_inc(k_var_ready, 1)
                    dve.wait_ge(k_sd_ready, b + 1)
                    link1(dve.reciprocal(k_st[:, 3, :, :], k_st[:, 2, :, :]))
                    for j in range(JT):
                        last = dve.tensor_tensor(per_head(kn[:, j, :]), per_head(kn[:, j, :]), spread(k_st[:, 3, j, :]), ALU.mult)
                    link1(last)
                    for j in range(JT):
                        last = dve.tensor_tensor(kn[:, j, :], kn[:, j, :], k_gb[:, 0, :], ALU.mult)
                    link1(last)
                    for j in range(JT):
                        last = dve.tensor_tensor(kn[:, j, :], kn[:, j, :], k_gb[:, 1, :], ALU.add)
                    last.then_inc(kn_ready, 1)
                    for m in range(KT):
                        dve.wait_ge(kk_ready, b * KT + m + 1)
                        link1(dve.tensor_tensor(kv[:, m, :], bank[6][:, m * P:(m + 1) * P], mean32[:, :], ALU.mult))
                        dve.tensor_scalar(kvg[:, m, :], kv[:, m, :], col("nq_g", m), None, ALU.mult).then_inc(kvm_ready, 1)
                    dve.wait_ge(q_sd_ready, b + 1)
                    dve.reciprocal(q_rs[:, :], q_sd[:, :]).then_inc(q_rs_ready, 1)
                    dve.wait_ge(kvc_ready, b + 1)
                    link1(dve.tensor_copy(kv_c[:, :], bank[6][:, C:C + KT]))
                    for m in range(KT):
                        dve.wait_ge(bias_part, b * KT + m + 1)
                        dve.tensor_scalar(bias_v[:, m, :], bank[4 + m][:, 0:NKEY], 1.0 / D1, kv_c[:, m:m + 1],
                                          ALU.mult, ALU.add).then_inc(bias_v_ready, 1)
                    dve.wait_ge(bias_v_ready, (b + 1) * KT)

                def outputs(b):
                    for i in range(NTB):
                        n = (b * NTB + i) * KT
                        for m in range(KT):
                            dve.wait_ge(q_rs_copied, n + m + 1)
                            dve.wait_ge(o_ready, n + m + 1)
                            dve.tensor_tensor(o_part[:, i % 2, m, :], bank[4 + i % 2 * 2 + m][:, :], o_part[:, i % 2, m, :],
                                              ALU.mult).then_inc(o_scaled, 1)
                        for m in range(KT):
                            dve.wait_ge(o_scaled, n + m + 1)
                            for r in range(ROWS // REP):
                                cell = (i * (ROWS // REP) + r) * RS
                                row = 1 + i * ROWS + r * REP
                                last = dve.tensor_tensor(
                                    H[:, m, row:row + REP, 1:1 + IMG].rearrange("p r (a c) -> p r a c", c=REP),
                                    o_part[:, i % 2, m, r * REP * IMG:(r + 1) * REP * IMG]
                                    .rearrange("p (r a c) -> p r a c", a=RS, c=REP),
                                    bias_v[:, m, cell:cell + RS].unsqueeze(1).unsqueeze(3).broadcast_to([P, REP, RS, REP]),
                                    ALU.add)
                            last.then_inc(o_placed, 1)

                def add_attention(b):
                    def f(i):
                        n = (i + b * NTB) * KT
                        for m in range(KT):
                            dve.wait_ge(pw_ready, n + (m + 1))
                            xx = X[:, b, m, ds(i * TB, TB)]
                            dve.tensor_tensor(xx, bank[2 + m][:, :], xx, ALU.add).then_inc(x_added, 1)
                    return f

                def layer1():
                    dve.sem_inc(conv_taken, KT)
                    dve.sem_inc(mlp_added, KT)
                    dve.sem_inc(x_added, KT)
                    dve.sem_inc(o_placed, KT)
                    batch_stats("bn1_g", "bn1_b", 1)
                    dve.wait_ge(weights1_loaded, 16 * 3)
                    centre_wq()
                    for b in range(B):
                        dve.wait_ge(h_ready, (b + 1) * KT)
                        convolve(2 * b, "dw1")
                        downsample(b)
                        keys(b)
                        outputs(b)
                        dve.wait_ge(o_placed, (b + 1) * NTB * KT + KT)
                        convolve(2 * b + 1, "dw2", add_attention(b))
                    dve.wait_ge(x_added, B * NTB * KT + KT)
                    batch_stats("bn2_g", "bn2_b", 2)

                def layer2_weights():
                    dve.wait_ge(l2_a, 1)
                    link1(dve.tensor_copy(u_col[:, :], bank[6][:, 0:KT]))
                    for k in range(KT):
                        dve.tensor_scalar(u_all[:, k, :], ones[:, :], u_col[:, k:k + 1], None, ALU.mult)
                    dve.tensor_scalar(b2all[:, 0, :], ones[:, :], col("bq"), None, ALU.mult)
                    dve.tensor_scalar(b2all[:, 1, :], ones[:, :], col("bk"), None, ALU.mult).then_inc(l2_b, 1)
                    dve.wait_ge(l2_a, 2)
                    link1(dve.tensor_copy(c2[:, 2:3], bank[6][:, 8:9]))
                    link1(dve.tensor_tensor(c2[:, 1:2], bank[6][:, 7:8], c2[:, 2:3], ALU.subtract))
                    dve.tensor_scalar(c2[:, 0:1], col("bv"), float(HW), None, ALU.mult).then_inc(l2_b, 1)
                    dve.wait_ge(l2_b, 2)

                def mlp(b):
                    with dve.Fori(0, NTB) as i:
                        n = (i + b * NTB) * KT
                        for m in range(KT):
                            dve.wait_ge(mlp_ready, n + (m + 1 + KT))
                            xx = X[:, b, m, ds(i * TB, TB)]
                            dve.scalar_tensor_tensor(xx, bank[4 + m][:, :], col("bexp", m), xx, ALU.add, ALU.add)\
                                .then_inc(mlp_added, 1)

                def mixing(b):
                    for k in range(KT):
                        last = dve.tensor_reduce(xs[:, b, k:k + 1], X[:, b, k, :], AX.X, ALU.add)
                    link1(last)
                    for k in range(KT):
                        last = dve.scalar_tensor_tensor(xs[:, b, k:k + 1], col("bexp", k), -float(HW), xs[:, b, k:k + 1],
                                                        ALU.mult, ALU.add)
                    last.then_inc(mix_a, 1)
                    dve.wait_ge(mix_b, 2 * b + 1)
                    dve.tensor_tensor(v_sum[:, b:b + 1], bank[7][:, 0:1], c2[:, 0:1], ALU.add).then_inc(mix_a, 1)
                    dve.wait_ge(mix_b, 2 * b + 2)
                    link1(dve.tensor_scalar(mixed[:, b, :], bank[7][:, 4:4 + KT], 1.0 / HW, None, ALU.mult))

                def apply_gates(b):
                    for i in range(NTB):
                        n = b * NTB + i
                        dve.wait_ge(s_relu_ready, n + 1)
                        for k in range(KT):
                            xx = X[:, b, k, i * TB:(i + 1) * TB]
                            dve.scalar_tensor_tensor(xx, s_relu[:, :], mixed[:, b, k:k + 1], xx, ALU.mult, ALU.add,
                                                     accum_out=sums3[:, 0, b, k, i:i + 1]).then_inc(x3_ready, 1)

                def evacuate_turned(b):
                    for c in range(HW // P):
                        n = b * (HW // P) + c
                        dve.wait_ge(turned3, n + 1)
                        dve.tensor_copy(xt[:, n % 4, :], bank[2 + n % 2][:, 0:C]).then_inc(xt_ready, 1)

                def layer3():
                    dve.wait_ge(x3_ready, B * NTB * KT)
                    dve.wait_ge(sq3_ready, B * NTB * KT)
                    for q in range(2):
                        for b in range(B):
                            last = dve.tensor_reduce(tot3[:, :, q, b], sums3[:, q, b, :, :], AX.X, ALU.add)
                    last.then_inc(norm3_ready, 1)
                    dve.wait_ge(nrm3_ready, 1)
                    link1(dve.tensor_scalar(st3[:, 1, :, :], st3[:, 0, :, :], 1e-12, None, ALU.max))
                    link1(dve.reciprocal(st3[:, 0, :, :], st3[:, 1, :, :]))
                    for b in range(B):
                        evacuate_turned(b)
                        dve.wait_ge(gram_ready, b + 1)
                        for m in range(KT):
                            last = dve.tensor_scalar(gram_s[:, m, :], bank[4 + m][:, 0:C], st3[:, 0, m, b:b + 1], None,
                                                     ALU.mult)
                        last.then_inc(gram_scaled, 1)
                        dve.wait_ge(gram_turned, b + 1)
                        for m in range(KT):
                            if b == 0:
                                last = dve.tensor_scalar(cos[:, m, :], bank[6 + m][:, 0:C], st3[:, 0, m, b:b + 1], None,
                                                         ALU.mult)
                            else:
                                last = dve.scalar_tensor_tensor(cos[:, m, :], bank[6 + m][:, 0:C], st3[:, 0, m, b:b + 1],
                                                                cos[:, m, :], ALU.mult, ALU.add)
                        last.then_inc(cos_added, 1)
                        dve.wait_ge(cos_added, b + 1)
                    for m in range(KT):
                        last = dve.tensor_scalar(gram_s[:, m, :], cos[:, m, :], 1.0 / B, None, ALU.mult)
                    link1(last)
                    for m in range(KT):
                        last = dve.scalar_tensor_tensor(cos[:, m, :], gram_s[:, m, :], -1.0, gram_s[:, m, :],
                                                        ALU.mult, ALU.min)
                    link1(last)
                    dve.wait_ge(diag_ready, CONSTS1)
                    for m in range(KT):
                        last = dve.max(top[:, m, :], cos[:, m, :])
                    link1(last)
                    for m in range(KT):
                        last = dve.max_index(top_i[:, m, :], top[:, m, :], cos[:, m, :])
                    link1(last)
                    link1(dve.tensor_copy(top_f[:, :, :], top_i[:, :, :]))
                    for n in range(1, NSEL):
                        for m in range(KT):
                            one = top_f[:, m, n:n + 1]
                            if n == 1:
                                last = dve.tensor_scalar(pick[:, m, :], count[:, :], one, None, ALU.is_equal)
                            else:
                                last = dve.scalar_tensor_tensor(pick[:, m, :], count[:, :], one, pick[:, m, :],
                                                                ALU.is_equal, ALU.add)
                        if n < NSEL - 1:
                            link1(last)
                    last.then_inc(pick_ready, 1)
                    for d in range(KT):
                        dve.wait_ge(pick_turned, d + 1)
                        dve.tensor_copy(pick_t[:, d, :], bank[d][:, 0:C]).then_inc(pick_t_ready, 1)
                    dve.wait_ge(group_sums, 1)
                    for m in range(KT):
                        last = dve.tensor_tensor(g3[:, m, :, :].rearrange("p q b -> p (q b)"), bank[2][:, m * 4:m * 4 + 4],
                                                 tot3[:, m, :, :].rearrange("p q b -> p (q b)"), ALU.add)
                    link1(last)
                    count3 = 1.0 / (NSEL * HW)
                    mean, sq = g3[:, :, 0, :], g3[:, :, 1, :]
                    link1(dve.tensor_scalar(g3[:, :, :, :], g3[:, :, :, :], count3, None, ALU.mult))
                    link1(dve.tensor_tensor(st3[:, 5, :, :], mean, mean, ALU.mult))
                    dve.tensor_tensor(st3[:, 2, :, :], sq, st3[:, 5, :, :], ALU.subtract).then_inc(var3_ready, 1)
                    dve.wait_ge(sd3_ready, 1)
                    link1(dve.reciprocal(st3[:, 1, :, :], st3[:, 3, :, :]))
                    for k in range(KT):
                        last = dve.tensor_scalar(st3[:, 4, k, :], st3[:, 1, k, :], col("gamma", k), None, ALU.mult)
                    link1(last)
                    link1(dve.tensor_tensor(st3[:, 2, :, :], mean, st3[:, 4, :, :], ALU.mult))
                    for k in range(KT):
                        last = dve.tensor_scalar(st3[:, 5, k, :], st3[:, 2, k, :], -1.0, col("beta", k), ALU.mult, ALU.add)
                    last.then_inc(affine3_ready, 1)
                    dve.wait_ge(affine3_ready, 1)
                    for b in range(B):
                        dve.tensor_scalar(X[:, b, 1, :], X[:, b, 1, :], st3[:, 4, 1, b:b + 1], st3[:, 5, 1, b:b + 1],
                                          ALU.mult, ALU.add).then_inc(out_ready[1], 1)

                layer1()
                layer2_weights()
                for b in range(B):
                    mlp(b)
                dve.wait_ge(mlp_added, B * NTB * KT + KT)
                for b in range(B):
                    mixing(b)
                    apply_gates(b)
                layer3()

            attention_layer()
            later_layers()

        @block.tensor
        def _(pe):
            def attention_layer():
                pe.wait_ge(consts_ready, CONSTS)
                pe.wait_ge(weights_loaded, 16 * 5)
                pe.sem_inc(pv_done, NBUF)

                def group_norm(b):
                    pe.wait_ge(ch_mean_ready, b + 1)
                    pe.matmul(misc[:, 0:KT], mean8[:, :], gn[:, 0, :], start=True, stop=True).then_inc(group_mean_ready, 1)
                    pe.wait_ge(ch_spread_ready, b + 1)
                    pe.matmul(misc[:, 4:4 + KT], mean8[:, :], gn[:, 4, :], start=True, stop=True).then_inc(group_var_ready, 1)
                    pe.wait_ge(affine_ready, b + 1)
                    for h in range(NH):
                        for k in range(KT):
                            pe.matmul(misc[:, 8 + h:9 + h], wqkv[:, k, h * 2 * DH:(h + 1) * 2 * DH], gn[:, 6, k:k + 1],
                                      start=(k == 0), stop=(k == KT - 1))
                    for m in range(KT):
                        for k in range(KT):
                            last = pe.matmul(misc[:, 16 + m:17 + m], wqkv[:, k, V_COL + m * P:V_COL + (m + 1) * P],
                                             gn[:, 6, k:k + 1], start=(k == 0), stop=(k == KT - 1))
                    last.then_inc(bias_ready, 1)
                    pe.wait_ge(bv_ready, b + 1)
                    for m in range(KT):
                        for k in range(KT):
                            last = pe.matmul(misc[:, 24 + m:25 + m], wproj[:, k, m * P:(m + 1) * P], b_v[:, k:k + 1],
                                             start=(k == 0), stop=(k == KT - 1))
                    last.then_inc(out_bias_ready, 1)

                def prepare(b, hh, tail):
                    g_last = hh * NTB + (-1)
                    pe.wait_ge(head_w_ready, hh + 1)
                    if tail:
                        weighted_values(g_last, NPAIR - 1)
                    for i in range(NTB + LAG):
                        units = range((i - LAG) * SUBS, (i - LAG + 1) * SUBS) if i >= LAG else ()
                        if units:
                            pe.wait_ge(hi_done, (hh * NTB + (i - LAG + 1)) * PARTS)
                            pe.wait_ge(lo_done, (hh * NTB + (i - LAG + 1)) * 2)
                            unit(hh * NTB, 0, units[0])
                        if i < NTB:
                            if i >= 4:
                                pe.wait_ge(lo_done, (hh * NTB + (i - 3)) * 2)
                            for k in range(KT):
                                last = pe.matmul(st[i // 2 % 2][:, i % 2, :], w_head[:, k, 0:2 * DH],
                                                 X[:, b, k, i * TB:(i + 1) * TB], start=(k == 0), stop=(k == KT - 1))
                            last.then_inc(qk_ready, 1)
                        if units:
                            unit(hh * NTB, 0, units[1])
                        if i < NTB:
                            if i > 0:
                                pe.wait_ge(v_copied, hh * NTB + i)
                            else:
                                pe.wait_ge(o_copied, hh * NTB + 1)
                            for s in range(SUBS):
                                if units and s == 2:
                                    unit(hh * NTB, 0, units[2])
                                tok = (i * SUBS + s) * P
                                for k in range(KT):
                                    last = pe.matmul(pvo[:, s * DH:(s + 1) * DH], X[:, b, k, tok:tok + P],
                                                     w_head[:, k, 2 * DH:QKV], start=(k == 0), stop=(k == KT - 1))
                            last.then_inc(v_ready, 1)
                        for u in units[2 if i >= NTB else 3:]:
                            unit(hh * NTB, 0, u)
                        if tail and i == 0:
                            turn_total(g_last)
                        if tail and i == 1:
                            spread_inverse(g_last)
                        if tail and 2 <= i < TAIL_STAGES:
                            project(g_last, i - 2)
                    pe.wait_ge(v_copied, hh * NTB + NTB)
                    pe.wait_ge(y_added, hh * NTB * KT + KT)
                    turn_max(hh * NTB)

                def unit(g, tb, u):
                    pe.wait_ge(mx_free, g * UNITS + (u + 1))
                    keys = slice(u // SUBS * TB, (u // SUBS + 1) * TB)
                    pe.matmul(mx[u % 2][:, :], q_hh[:, ds(tb * TB + u % SUBS * P, P)], k_hl[:, keys],
                              start=True, stop=True).then_inc(mx_ready, 1)

                def turn_max(g):
                    pe.wait_ge(max_cols_ready, g + 1)
                    for s in range(SUBS):
                        last = pe.matmul(misc[0:LO_ROW + 1, s * P:(s + 1) * P], max_cols[:, s, :], ident_bf[:, :],
                                         start=True, stop=True)
                    last.then_inc(max_turned, 1)

                def scores(g, tb, j):
                    cols = ds(tb * TB, TB)
                    for c in range(2):
                        keys = slice((2 * j + c) * P, (2 * j + c + 1) * P)
                        pe.matmul(st[j % 2][:, c, :], k_hl[:, keys], q_hh[:, cols], start=True, stop=False)
                        last = pe.matmul(st[j % 2][:, c, :], k_h1[:, keys], q_lm[:, cols], start=False, stop=True)
                    last.then_inc(st_ready, 1)

                def weighted_values(g, j):
                    pe.wait_ge(exp_done, exps(g, j))
                    for c in range(2):
                        last = pe.matmul(pvo[c * DH:(c + 1) * DH, :], v_sb[:, 2 * j + c, :], prob[:, j % NBUF, c, :],
                                         start=(j == 0), stop=(j == NPAIR - 1))
                    last.then_inc(pv_done, 1)

                def turn_total(g):
                    pe.wait_ge(total_ready, g + 1)
                    for s in range(SUBS):
                        last = pe.matmul(misc[:, s:s + 1], total[:, s * P:(s + 1) * P], ones[:, 0:1], start=True, stop=True)
                    last.then_inc(total_turned, 1)

                def spread_inverse(g):
                    pe.wait_ge(inv_ready, g + 1)
                    for s in range(SUBS):
                        last = pe.matmul(misc[:, s * P:(s + 1) * P], inv_cols[:, s:s + 1].broadcast_to([P, P]), ident[:, :],
                                         start=True, stop=True)
                    last.then_inc(inv_spread, 1)

                def project(g, m):
                    pe.wait_ge(o_norm_ready, g + 1)
                    if m:
                        pe.wait_ge(y_added, g * KT + (m + KT))
                    pe.matmul(misc[:, :], wp_head[:, m * P:(m + 1) * P], o_norm[:, :],
                              start=True, stop=True).then_inc(proj_ready, 1)

                def step(g, tb, tail, turn):
                    pe.wait_ge(max_row_ready, g + 1)
                    for j in range(NPAIR):
                        units = SLOTS[j] if turn else []
                        for u in units[0:1]:
                            unit(g + 1, tb + 1, u)
                        scores(g, tb, j)
                        for u in units[1:2]:
                            unit(g + 1, tb + 1, u)
                        if j == 0 and tail:
                            weighted_values(g + (-1), NPAIR - 1)
                        if j == 1:
                            pe.wait_ge(o_copied, g + 1)
                        if j >= 1:
                            weighted_values(g, j - 1)
                        for u in units[2:]:
                            unit(g + 1, tb + 1, u)
                        if tail and j == SUM_SLOT:
                            turn_total(g + (-1))
                        if tail and j == INV_SLOT:
                            spread_inverse(g + (-1))
                        if tail and j in PROJ_SLOTS:
                            project(g + (-1), PROJ_SLOTS.index(j))
                        if turn and j == TURN_SLOT:
                            if tail:
                                pe.wait_ge(y_added, g * KT + KT)
                            turn_max(g + 1)

                def steps(hh):
                    pe.wait_ge(head_wp_ready, hh + 1)
                    step(hh * NTB, 0, tail=False, turn=True)
                    with pe.Fori(1, NTB - 1) as tb:
                        step(hh * NTB + tb, tb, tail=True, turn=True)
                    step(hh * NTB + (NTB - 1), NTB - 1, tail=True, turn=False)

                def tail_alone(g):
                    weighted_values(g, NPAIR - 1)
                    turn_total(g)
                    spread_inverse(g)
                    for m in range(KT):
                        project(g, m)
                    pe.wait_ge(y_added, g * KT + 2 * KT)

                for b in range(B):
                    group_norm(b)
                    prepare(b, b * NH, tail=False)
                    with pe.Fori(0, NH - 1) as h:
                        steps(h + b * NH)
                        prepare(b, h + (b * NH + 1), tail=True)
                    steps(b * NH + NH - 1)
                    tail_alone((b + 1) * NH * NTB - 1)

            def later_layers():
                def taps(n, name_i, i):
                    for k in range(KT):
                        pe.wait_ge(conv_taken, convs(n, i) + (k + 1))
                        for t in range(PE_TAPS[name_i]):
                            dy, dx = TAPS[t]
                            last = pe.matmul(bank[k][:, :], diag[name_i][:, k, t, :],
                                             H[:, k, ds(i * ROWS + dy, ROWS), dx:dx + IMG],
                                             start=(t == 0), stop=(t == PE_TAPS[name_i] - 1))
                        last.then_inc(conv_part, 1)

                def queries(b):
                    pe.wait_ge(conv_step, conv_steps(2 * b + 1, 0))
                    for i in range(NTB + 1):
                        n = (b * NTB + i) * KT
                        if i < NTB:
                            if i >= 2:
                                pe.wait_ge(q_sq_ready, n - KT)
                            for m in range(KT):
                                for k in range(KT):
                                    last = pe.matmul(bank[i % 2 * 2 + m][:, :], w1[:, k, m * P:(m + 1) * P],
                                                     Z[:, k, i * TB:(i + 1) * TB], start=(k == 0), stop=(k == KT - 1))
                                last.then_inc(q_ready, 1)
                        if i == KV_AT:
                            pe.wait_ge(zi_ready, b + 1)
                            for j in range(JT):
                                for k in range(KT):
                                    last = pe.matmul(bank[4 + j][:, :], z_rev[:, k, j * P:(j + 1) * P], w1[:, k, C:3 * C],
                                                     start=(k == 0), stop=(k == KT - 1))
                                last.then_inc(kv_ready, 1)
                        if i > 0:
                            pe.wait_ge(q_sq_ready, n)
                            first = (NTB - i) * TILE_HEADS
                            for m in range(KT):
                                last = pe.matmul(bank[7][m * VAR_ROWS:(m + 1) * VAR_ROWS, :], var_cols[:, first:first + VAR_ROWS],
                                                 q_sq[:, m, :], start=(i == 1), stop=(i == NTB))
                                last.then_inc(q_var_part, 1)

                def keys(b):
                    pe.wait_ge(kn_ready, b + 1)
                    for m in range(KT):
                        for j in range(JT):
                            last = pe.matmul(bank[6][:, m * P:(m + 1) * P], kn[:, j, m * P:(m + 1) * P],
                                             vv[:, j, m * P:(m + 1) * P], start=(j == 0), stop=(j == JT - 1))
                    last.then_inc(kk_ready, KT)
                    pe.wait_ge(kvm_ready, (b + 1) * KT)
                    for m in range(KT):
                        last = pe.matmul(bank[6][:, C + m:C + m + 1], kv[:, m, :], col("nq_b", m), start=True, stop=True)
                    last.then_inc(kvc_ready, 1)
                    pe.wait_ge(table_loaded, 16 * (P // RS))
                    for m in range(KT):
                        for h4 in range(P // D1):
                            h = m * (P // D1) + h4
                            for j in range(JT):
                                start = j * (P // RS) * TABLE
                                rhs = table[:, h, start:start + RS * TABLE].rearrange("p (r c) -> p r c", c=TABLE)[:, :, 0:RS]
                                last = pe.matmul(bank[4 + m][h4 * D1:(h4 + 1) * D1, 0:NKEY], vv[:, j, h * D1:(h + 1) * D1],
                                                 rhs, start=(j == 0), stop=(j == JT - 1), tile_position=(0, h4 * D1))
                        last.then_inc(bias_part, 1)
                    pe.wait_ge(bias_v_ready, (b + 1) * KT)

                def outputs(b):
                    pe.wait_ge(q_rs_ready, b + 1)
                    for i in range(NTB):
                        n = (b * NTB + i) * KT
                        for m in range(KT):
                            half = slice(m * VAR_ROWS, (m + 1) * VAR_ROWS)
                            if i > 0:
                                pe.wait_ge(q_rs_copied, n - KT + m + 1)
                            pe.matmul(bank[m][:, :], head_of[half, i * P:(i + 1) * P], q_rs[half, :],
                                      start=True, stop=True).then_inc(q_rs_spread, 1)
                        if i >= 2:
                            pe.wait_ge(o_scaled, n - KT)
                        for m in range(KT):
                            pe.matmul(bank[4 + i % 2 * 2 + m][:, :], kvg[:, m, :],
                                      H[:, m, 1 + i * ROWS:1 + (i + 1) * ROWS, 1:1 + IMG],
                                      start=True, stop=True).then_inc(o_ready, 1)

                def pointwise(b, i):
                    n = (i + b * NTB) * KT
                    pe.wait_ge(conv_step, conv_steps(2 * b + 1, i) + dve_steps(1))
                    for m in range(KT):
                        pe.wait_ge(x_added, n + (m + 1))
                        for k in range(KT):
                            last = pe.matmul(bank[2 + m][:, :], w_out[:, k, m * P:(m + 1) * P], Z[:, k, ds(i * TB, TB)],
                                             start=(k == 0), stop=(k == KT - 1))
                        last.then_inc(pw_ready, 1)

                def layer1():
                    pe.sem_inc(mlp_ready, KT)
                    pe.wait_ge(diag_ready, CONSTS1)
                    pe.wait_ge(wq1_ready, KT)
                    for b in range(B):
                        pe.wait_ge(h_ready, (b + 1) * KT)
                        with pe.Fori(0, NTB) as i:
                            taps(2 * b, 0, i)
                        queries(b)
                        keys(b)
                        pe.wait_ge(q_kept, (b + 1) * NTB * KT)
                        outputs(b)
                        pe.wait_ge(o_placed, (b + 1) * NTB * KT + KT)
                        taps(2 * b + 1, 1, 0)
                        with pe.Fori(1, NTB) as i:
                            taps(2 * b + 1, 1, i)
                            pointwise(b, i + (-1))
                        pointwise(b, NTB - 1)

                def layer2_weights():
                    for k in range(KT):
                        pe.matmul(bank[6][:, k:k + 1], w2q[:, 0, k * P:(k + 1) * P], col("wq_c"), start=True, stop=False)
                        last = pe.matmul(bank[6][:, k:k + 1], w2q[:, 1, k * P:(k + 1) * P], col("wk_c"),
                                         start=False, stop=True)
                    last.then_inc(l2_a, 1)
                    pe.wait_ge(l2_b, 1)
                    pe.matmul(bank[6][:, 7:8], b2all[:, 0, :], col("wq_c"), start=True, stop=False)
                    pe.matmul(bank[6][:, 7:8], b2all[:, 1, :], col("wk_c"), start=False, stop=True)
                    for k in range(KT):
                        last = pe.matmul(bank[6][:, 8:9], u_all[:, k, :], col("bexp", k), start=(k == 0), stop=(k == KT - 1))
                    last.then_inc(l2_a, 1)

                def mlp(b):
                    with pe.Fori(0, NTB) as i:
                        n = (i + b * NTB) * KT
                        pe.wait_ge(mlp_in, n + KT)
                        for m in range(KT):
                            pe.wait_ge(mlp_added, n + (m + 1))
                            for k in range(KT):
                                last = pe.matmul(bank[4 + m][:, :], w_mlp[:, k, m * P:(m + 1) * P], relu_h[:, k, :],
                                                 start=(k == 0), stop=(k == KT - 1))
                            last.then_inc(mlp_ready, 1)

                def mixing(b):
                    pe.wait_ge(mix_a, 2 * b + 1)
                    for k in range(KT):
                        last = pe.matmul(bank[7][:, 0:1], w2v[:, k, :], xs[:, b, k:k + 1], start=(k == 0), stop=(k == KT - 1))
                    last.then_inc(mix_b, 1)
                    pe.wait_ge(mix_a, 2 * b + 2)
                    for m in range(KT):
                        last = pe.matmul(bank[7][:, 4 + m:5 + m], w2e[:, m * P:(m + 1) * P], v_sum[:, b:b + 1],
                                         start=True, stop=True)
                    last.then_inc(mix_b, 1)

                def gates(b, i):
                    n = b * NTB + i
                    if n >= 2:
                        pe.wait_ge(s_relu_ready, n - 1)
                    for k in range(KT):
                        last = pe.matmul(bank[n % 2][:, :], u_all[:, k, :], X[:, b, k, i * TB:(i + 1) * TB],
                                         start=(k == 0), stop=(k == KT - 1))
                    last.then_inc(gate_ready, 1)

                def turn(n):
                    b, c = n // (HW // P), n % (HW // P)
                    if n >= 2:
                        pe.wait_ge(xt_ready, n - 1)
                    for k in range(KT):
                        last = pe.transpose(bank[2 + n % 2][:, k * P:(k + 1) * P], X[:, b, k, c * P:(c + 1) * P], ident[:, :])
                    last.then_inc(turned3, 1)

                def gram(n):
                    b, c = n // (HW // P), n % (HW // P)
                    pe.wait_ge(xt_ready, n + 1)
                    for m in range(KT):
                        last = pe.matmul(bank[4 + m][:, 0:C], xt[:, n % 4, m * P:(m + 1) * P], xt[:, n % 4, :],
                                         start=(c == 0), stop=(c == HW // P - 1))
                    if c == HW // P - 1:
                        last.then_inc(gram_ready, 1)

                def layer3():
                    pe.wait_ge(x3_ready, B * NTB * KT)
                    chunks = HW // P
                    turn(0)
                    for n in range(B * chunks):
                        if n + 1 < B * chunks:
                            turn(n + 1)
                        gram(n)
                        if n % chunks == chunks - 1:
                            b = n // chunks
                            pe.wait_ge(gram_scaled, b + 1)
                            if b > 0:
                                pe.wait_ge(cos_added, b)
                            for m in range(KT):
                                for k in range(KT):
                                    last = pe.transpose(bank[6 + m][:, k * P:(k + 1) * P], gram_s[:, k, m * P:(m + 1) * P],
                                                        ident[:, :])
                            last.then_inc(gram_turned, 1)
                    pe.wait_ge(pick_ready, 1)
                    for d in range(KT):
                        for m in range(KT):
                            last = pe.transpose(bank[d][:, m * P:(m + 1) * P], pick[:, m, d * P:(d + 1) * P], ident[:, :])
                        last.then_inc(pick_turned, 1)
                    pe.wait_ge(pick_t_ready, KT)
                    for m in range(KT):
                        for d in range(KT):
                            last = pe.matmul(bank[2][:, m * 4:m * 4 + 4], pick_t[:, d, m * P:(m + 1) * P],
                                             tot3[:, d, :, :].rearrange("p q b -> p (q b)"), start=(d == 0), stop=(d == KT - 1))
                    last.then_inc(group_sums, 1)

                layer1()
                pe.wait_ge(weights2_loaded, 16 * 4)
                layer2_weights()
                for b in range(B):
                    mlp(b)
                for b in range(B):
                    mixing(b)
                    for i in range(NTB):
                        gates(b, i)
                layer3()

            attention_layer()
            later_layers()



def kernel(**inputs):
    import numpy as _np
    import concourse.bacc as _bacc
    from concourse import mybir as _mybir
    from concourse.bass_utils import run_bass_kernel_spmd as _run

    def columns(v):
        return _np.asarray(v).reshape(-1, P).T

    def taps(w):
        return _np.asarray(w).reshape(KT, P, 9).transpose(1, 0, 2).reshape(P, KT * 9)

    by_head = _np.arange(C).reshape(D1, HEADS1).T.reshape(-1)
    g = {k: _np.asarray(v) for k, v in inputs.items()}
    w_qkv = g["L0_conv_w_qkv"].reshape(NH, 3, DH, C)
    w_qkv = _np.concatenate([w_qkv[:, 0:2].reshape(V_COL, C), w_qkv[:, 2].reshape(C, C)])
    b_qkv = g["L0_conv_b_qkv"].reshape(NH, 3, DH)
    parts = {
        "gn_scale": columns(g["L0_conv_gn_scale"]), "gn_bias": columns(g["L0_conv_gn_bias"]),
        "b_qk": b_qkv[:, 0:2].reshape(NH, P).T, "b_v": columns(b_qkv[:, 2].reshape(-1)),
        "b_proj": columns(g["L0_conv_b_proj"]),
        "bn1_g": columns(g["L1_conv_bn1_g"]), "bn1_b": columns(g["L1_conv_bn1_b"]),
        "dw1": taps(g["L1_conv_qkv_dw"]), "dw2": taps(g["L1_conv_out_dw"][by_head]),
        "nq_g": columns(g["L1_conv_nq_g"].reshape(-1)), "nq_b": columns(g["L1_conv_nq_b"].reshape(-1)),
        "bn2_g": columns(g["L1_conv_bn2_g"]), "bn2_b": columns(g["L1_conv_bn2_b"]),
        "bexp": columns(g["L2_conv_bexp"]), "bq": columns(g["L2_conv_bq"]), "bk": columns(g["L2_conv_bk"]),
        "bv": columns(g["L2_conv_bv"]), "wq_c": columns(g["L2_conv_Wcat"][0, :E2]),
        "wk_c": columns(g["L2_conv_Wcat"][0, E2:]), "gamma": columns(g["L3_conv_gamma"]),
        "beta": columns(g["L3_conv_beta"]),
    }
    w1 = g["L1_conv_qkv_pw"].reshape(3, C, C)[:, by_head].reshape(3 * C, C)
    k_norm = _np.stack([g["L1_conv_nk_g"].reshape(-1), g["L1_conv_nk_b"].reshape(-1)])
    arrays = {
        "x": g["x"],
        "w_qkv_t": w_qkv.T, "w_proj_t": g["L0_conv_w_proj"].T,
        "vectors": _np.concatenate([parts[n] for n in VEC_NAMES], axis=1),
        "w1_t": w1.T, "w_out_t": g["L1_conv_out_pw"][:, by_head].T, "mlp_t": g["L1_conv_mlp_w"].T,
        "k_norm": _np.broadcast_to(k_norm, (P, 2, C)),
        "rel_table": g["L1_conv_rel_table"].T,
        "w2_qk": _np.stack([g["L2_conv_Wq"], g["L2_conv_Wk"]], axis=1),
        "w2_v_t": g["L2_conv_Wv"].T, "w2_exp_t": g["L2_conv_Wexp"].T,
    }
    arrays = {n: _np.ascontiguousarray(a) for n, a in arrays.items()}
    nc = _bacc.Bacc("TRN2", target_bir_lowering=False, num_devices=1)
    args = [nc.dram_tensor(f"in_{n}", a.shape, _mybir.dt.from_np(a.dtype), kind="ExternalInput").ap()
            for n, a in arrays.items()]
    result = nc.dram_tensor("out_0", (B, C, IMG, IMG), F32, kind="ExternalOutput").ap()
    build(nc, *args, result)
    r = _run(nc, [{f"in_{n}": a for n, a in arrays.items()}], core_ids=[0])
    return r.results[0]["out_0"]
```

```python
from contextlib import ExitStack

import concourse.bass as bass
from concourse import mybir

F32 = mybir.dt.float32
BF16 = mybir.dt.bfloat16
U32 = mybir.dt.uint32
ALU = mybir.AluOpType
ACT = mybir.ActivationFunctionType
AX = mybir.AxisListType
ds = bass.ds

P = 128
B, C, IMG = 2, 256, 64
HW = IMG * IMG
KT = C // P
TB = 512
NTB = HW // TB

NH, DH = 4, 64
QKV = 3 * DH
V_COL = 2 * DH * NH
EPS_GN = 1e-5
GROUP0 = C // 32
SCALE0 = 1.0 / DH ** 0.5
NPAIR = HW // (2 * P)
POOL_PAIRS = 12
DVE_PAIRS = NPAIR - POOL_PAIRS
NBUF = 4
SUBS = TB // P
UNITS = SUBS * NTB
PER_SLOT = 3


def unit_slots():
    slots, u = [[] for _ in range(NPAIR)], 0
    for j in range(1, NPAIR):
        while u < UNITS and len(slots[j]) < PER_SLOT:
            slots[j].append(u)
            u += 1
    return slots


SLOTS = unit_slots()
LAST_UNIT_SLOT = max(j for j in range(NPAIR) if SLOTS[j])
assert SLOTS[LAST_UNIT_SLOT][-1] == UNITS - 1 and LAST_UNIT_SLOT + 2 < NPAIR
TURN_SLOT = LAST_UNIT_SLOT + 2
assert TURN_SLOT <= NPAIR - 2

SUM_SLOT, INV_SLOT = 2, 3
PROJ_SLOTS = (5, 7)
LO_ROW = 32
PARTS = 4
CONSTS = 6
PE_NORM_SLOTS = (9, 11, 13, 15)
ACT_NORM_SLOT = 12
DVE_NORM_SLOTS = (8, 10, 12, 14, 15)
X_PIECES = 2
LAG = 2
V_LAG = 1
TAIL_AT = 1
assert max(PROJ_SLOTS) < TURN_SLOT

HEADS1, RS = 8, 16
D1 = C // HEADS1
NKEY = RS * RS
JT = NKEY // P
REP = IMG // RS
TABLE = 2 * RS - 1
ROWS = TB // IMG
PAD = IMG + 2
TAPS = [(dy, dx) for dy in range(3) for dx in range(3)]
PE_TAPS = (3, 2)
SIDE_TAPS = 3
VAR_ROWS = 64
TILE_HEADS = P // D1
assert NTB * TILE_HEADS <= VAR_ROWS
KV_AT, K_SD_AT = 3, 5
EPS_BN = 1e-5
EPS_LN = 1e-6
RATIO = (IMG - 1) / (RS - 1)
PERIOD = 5
PERIOD_ROWS = int(PERIOD * RATIO)
GROUPS = RS // PERIOD
assert PERIOD_ROWS == PERIOD * RATIO and GROUPS * PERIOD + 1 == RS and GROUPS * PERIOD_ROWS + 1 == IMG
E2 = C // 2
NSEL = C // 32
EPS_L3 = 1e-5
BIAS_RUN = (RS - 1) * TABLE + RS + (P // RS) * TABLE


VEC_NAMES = {"gn_scale": KT, "gn_bias": KT, "b_qk": NH, "b_v": KT, "b_proj": KT,
             "bn1_g": KT, "bn1_b": KT, "dw1": KT * 9, "dw2": KT * 9, "nq_g": KT, "nq_b": KT, "bn2_g": KT,
             "bn2_b": KT, "bexp": KT, "bq": 1, "bk": 1, "bv": 1, "wq_c": 1, "wk_c": 1, "gamma": KT, "beta": KT}
VEC, NVEC = {}, 0
for _name, _n in VEC_NAMES.items():
    VEC[_name] = NVEC
    NVEC += _n


ARENA_WORDS = 36032


def np_f32(v):
    import numpy as np
    return float(np.float32(v))


def build(nc, x, w_qkv_t, w_proj_t, vectors, w1_t, w_out_t, mlp_t, k_norm, rel_table, w2_qk, w2_v_t, w2_exp_t, out):
    ctx = ExitStack()
    with ctx:
        def sb(name, shape, dt=F32):
            return ctx.enter_context(nc.sbuf_tensor(name, shape, dt))

        def sem(name):
            return ctx.enter_context(nc.semaphore(name))

        X = sb("X", [P, B, KT, HW])
        vec = sb("vec", [P, NVEC])
        ident = sb("ident", [P, P])
        ones = sb("ones", [P, P])
        mean8 = sb("mean8", [P, P])
        mean32 = sb("mean32", [P, P])
        stats1 = sb("stats1", [P, KT, B, NTB, 6])
        eps = sb("eps", [P, 2])

        def col(name, k=0, n=1):
            return vec[:, VEC[name] + k:VEC[name] + k + n]

        arena = sb("arena", [P, ARENA_WORDS])

        def carver(start, end):
            at = [start]

            def take(shape, dt=F32):
                n = 1
                for d in shape[1:]:
                    n *= d
                words = (n + 1) // 2 if dt == BF16 else n
                assert at[0] + words <= end, (at, words, end)
                tile = arena[0:shape[0], at[0]:at[0] + words]
                at[0] += words
                if dt != F32:
                    tile = tile.bitcast(dt)[:, 0:n]
                if len(shape) > 2:
                    names = " ".join("abcdef"[:len(shape) - 1])
                    tile = tile.rearrange(f"p ({names}) -> p {names}",
                                          **{c: d for c, d in zip("abcdef", shape[1:])})
                return tile
            return take

        early = carver(0, ARENA_WORDS)
        late = carver(0, ARENA_WORDS)

        Y = early([P, KT, HW])
        q_hh = early([P, HW], BF16)
        k_hl = early([P, HW], BF16)
        q_lm = early([P, HW], BF16)
        k_h1 = early([P, HW], BF16)
        v_sb = early([P, HW // P, DH])
        prob = early([P, NBUF, 2, TB])
        acc_pool = early([P, 2, TB])
        acc_dve = early([P, 2, TB])
        pool_total = early([P, TB])
        total = early([P, TB])
        inv_cols = early([P, SUBS])
        o_raw = early([P, TB])
        o_norm = early([P, TB])
        wqkv = early([P, KT, NH * QKV])
        wproj = early([P, KT, C])
        wproj2 = early([P, NH, C])
        w_head = early([P, KT, QKV])
        wp_head = early([P, C])
        b_head = early([P, 1])
        stats = early([P, KT, NTB, 6])
        mv = early([P, KT, 2])
        gn = early([P, 8, KT])
        b_qk = early([P, NH])
        b_v = early([P, KT])
        b_out = early([P, KT])
        part_max = early([P, SUBS, NTB])
        neg_max = early([P, SUBS])
        max_cols = early([P, SUBS, LO_ROW + 1], BF16)
        ident_bf = early([P, P], BF16)

        H = late([P, KT, PAD, PAD])
        Z = late([P, KT, HW])
        w1 = late([P, KT, 3 * C])
        w_out = late([P, KT, C])
        k_gb = late([P, 2, C])
        table = late([P, HEADS1, BIAS_RUN + TABLE - RS])
        diag = [late([P, KT, taps, P]) for taps in PE_TAPS]
        mv1 = late([P, KT, 2])
        bn = late([P, 4, KT])
        q_mean = late([P, KT, HEADS1])
        rows_n, part_n = KT * RS * IMG, KT * (PERIOD - 1) * GROUPS * IMG
        shared = late([P, rows_n + part_n])
        rows_i = shared[:, 0:rows_n].rearrange("p (k r c) -> p k r c", k=KT, r=RS)
        part_i = shared[:, rows_n:].rearrange("p (k r c) -> p k r c", k=KT, r=PERIOD - 1)
        zi = late([P, KT, NKEY])
        z_rev = shared[:, 0:KT * NKEY].rearrange("p (k n) -> p k n", k=KT)
        kn = shared[:, KT * NKEY:KT * NKEY + JT * C].rearrange("p (j c) -> p j c", j=JT)
        k_sq = shared[:, KT * NKEY + JT * C:KT * NKEY + 2 * JT * C].rearrange("p (j c) -> p j c", j=JT)
        o_part = shared[:, 0:2 * KT * TB].rearrange("p (a k n) -> p a k n", a=2, k=KT)
        q_rs = shared[:, 2 * KT * TB:2 * KT * TB + TB]
        q_sd = shared[:, 2 * KT * TB + TB:2 * KT * TB + 2 * TB]
        vv = late([P, JT, C])
        k_st = late([P, 4, JT, HEADS1])
        kv = late([P, KT, P])
        kvg = late([P, KT, P])
        kv_c = late([P, KT])
        bias_v = late([P, KT, NKEY])
        q_sq = late([P, KT, TB])
        var_cols = late([P, (NTB - 1) * TILE_HEADS + VAR_ROWS])
        head_of = late([P, NTB * P])

        spare, used = Z[:, :, :].rearrange("p k n -> p (k n)"), [0]

        def carve(n, *names, **sizes):
            used[0] += n
            part = spare[:, used[0] - n:used[0]]
            return part.rearrange(f"p ({' '.join(names)}) -> p {' '.join(names)}", **sizes) if names else part

        table_words = table[:, :, :].rearrange("p h n -> p (h n)")
        w_mlp = table_words[:, 0:KT * C].rearrange("p (k c) -> p k c", k=KT)
        w2q = table_words[:, KT * C:(KT + 2) * C].rearrange("p (k c) -> p k c", k=2)
        w2v = table_words[:, (KT + 2) * C:(KT + 3) * C].rearrange("p (k c) -> p k c", k=KT)
        w2e = table_words[:, (KT + 3) * C:(KT + 4) * C]
        u_all = carve(KT * P, "k", "c", k=KT)
        u_col = late([P, KT])
        b2all = carve(2 * P, "k", "c", k=2)
        c2 = late([P, 4])
        relu_h = carve(2 * KT * TB, "a", "k", "n", a=2, k=KT)
        xsum = late([P, B, KT, NTB])
        xs = late([P, B, KT])
        v_sum = late([P, B])
        mixed = late([P, B, KT])
        s_relu = carve(2 * TB, "a", "n", a=2)
        sums3 = late([P, 2, B, KT, NTB])
        tot3 = late([P, KT, 2, B])
        junk = carve(TB)
        xt = carve(4 * C, "r", "c", r=4)
        gram_s = carve(KT * C, "k", "c", k=KT)
        gram_01 = carve(P)
        cos = carve(KT * C, "k", "c", k=KT)
        top = late([P, KT, 8])
        top_i = late([P, KT, 8], U32)
        top_f = late([P, KT, 8])
        count = late([P, C])
        pick = carve(KT * C, "k", "c", k=KT)
        pick_t = carve(KT * C, "k", "c", k=KT)
        g3 = late([P, KT, 2, B])
        st3 = late([P, 6, KT, B])

        side = shared[:, 0:SIDE_TAPS * KT * TB].rearrange("p (s k n) -> p s k n", s=SIDE_TAPS, k=KT)

        st = [ctx.enter_context(nc.psum_tensor(f"st{i}", [P, 2, TB], F32)) for i in range(2)]
        mx = [ctx.enter_context(nc.psum_tensor(f"mx{i}", [P, TB], F32)) for i in range(2)]
        pvo = ctx.enter_context(nc.psum_tensor("pvo", [P, TB], F32))
        misc = ctx.enter_context(nc.psum_tensor("misc", [P, TB], F32))
        bank = [st[0][:, 0, :], st[0][:, 1, :], st[1][:, 0, :], st[1][:, 1, :], mx[0][:, :], mx[1][:, :],
                pvo[:, :], misc[:, :]]

        consts_ready = sem("consts_ready")
        ident_ready = sem("ident_ready")
        x_loaded = [[[sem(f"x{b}_{k}_{piece}_loaded") for piece in range(X_PIECES)] for k in range(KT)] for b in range(B)]
        weights_loaded = sem("weights_loaded")
        pool_chain = sem("pool_chain")
        dve_chain = sem("dve_chain")
        ch_mean_ready = sem("ch_mean_ready")
        group_mean_ready = sem("group_mean_ready")
        ch_spread_ready = sem("ch_spread_ready")
        group_var_ready = sem("group_var_ready")
        sd_ready = sem("sd_ready")
        affine_ready = sem("affine_ready")
        bias_ready = sem("bias_ready")
        bv_ready = sem("bv_ready")
        out_bias_ready = sem("out_bias_ready")
        b_out_ready = sem("b_out_ready")
        y_init = sem("y_init")
        head_w_ready = sem("head_w_ready")
        head_wp_ready = sem("head_wp_ready")
        qk_ready = sem("qk_ready")
        hi_done = sem("hi_done")
        lo_done = sem("lo_done")
        v_ready = sem("v_ready")
        v_copied = sem("v_copied")
        mx_ready = sem("mx_ready")
        mx_free = sem("mx_free")
        neg_max_ready = sem("neg_max_ready")
        max_turned = sem("max_turned")
        max_hi_ready = sem("max_hi_ready")
        max_cols_ready = sem("max_cols_ready")
        max_row_ready = sem("max_row_ready")
        st_ready = sem("st_ready")
        exp_done = sem("exp_done")
        pv_done = sem("pv_done")
        pool_sums = sem("pool_sums")
        dve_sums = sem("dve_sums")
        pool_total_ready = sem("pool_total_ready")
        dve_folded = sem("dve_folded")
        total_ready = sem("total_ready")
        total_turned = sem("total_turned")
        inv_ready = sem("inv_ready")
        inv_spread = sem("inv_spread")
        o_copied = sem("o_copied")
        o_norm_ready = sem("o_norm_ready")
        proj_ready = sem("proj_ready")
        y_added = sem("y_added")
        layer0_done = sem("layer0_done")
        early_stats = sem("early_stats")

        weights1_loaded = sem("weights1_loaded")
        weights2_loaded = sem("weights2_loaded")
        table_loaded = sem("table_loaded")
        pool1_chain = sem("pool1_chain")
        dve1_chain = sem("dve1_chain")
        var1_ready = sem("var1_ready")
        sd1_ready = sem("sd1_ready")
        affine1_ready = sem("affine1_ready")
        border_ready = sem("border_ready")
        diag_ready = sem("diag_ready")
        wq1_ready = sem("wq1_ready")
        h_ready = sem("h_ready")
        conv_part = sem("conv_part")
        conv_taken = sem("conv_taken")
        conv_step = sem("conv_step")
        side_made = sem("side_made")
        side_taps = sem("side_taps")
        zi_ready = sem("zi_ready")
        kv_ready = sem("kv_ready")
        v_got = sem("v_got")
        k_var_ready = sem("k_var_ready")
        k_sd_ready = sem("k_sd_ready")
        kn_ready = sem("kn_ready")
        kk_ready = sem("kk_ready")
        kvm_ready = sem("kvm_ready")
        kvc_ready = sem("kvc_ready")
        bias_part = sem("bias_part")
        bias_v_ready = sem("bias_v_ready")
        q_ready = sem("q_ready")
        q_kept = sem("q_kept")
        q_sq_ready = sem("q_sq_ready")
        q_var_part = sem("q_var_part")
        q_sd_ready = sem("q_sd_ready")
        q_rs_ready = sem("q_rs_ready")
        q_rs_spread = sem("q_rs_spread")
        q_rs_copied = sem("q_rs_copied")
        o_scaled = sem("o_scaled")
        o_ready = sem("o_ready")
        o_placed = sem("o_placed")
        pw_ready = sem("pw_ready")
        x_added = sem("x_added")
        mlp_in = sem("mlp_in")
        mlp_ready = sem("mlp_ready")
        mlp_added = sem("mlp_added")
        l2_a = sem("l2_a")
        l2_b = sem("l2_b")
        mix_a = sem("mix_a")
        mix_b = sem("mix_b")
        gate_ready = sem("gate_ready")
        s_relu_ready = sem("s_relu_ready")
        x3_ready = sem("x3_ready")
        sq3_ready = sem("sq3_ready")
        turned3 = sem("turned3")
        xt_ready = sem("xt_ready")
        gram_ready = sem("gram_ready")
        norm3_ready = sem("norm3_ready")
        nrm3_ready = sem("nrm3_ready")
        gram_copied = sem("gram_copied")
        gram_whole = sem("gram_whole")
        gram_scaled = sem("gram_scaled")
        gram_turned = sem("gram_turned")
        cos_added = sem("cos_added")
        pick_ready = sem("pick_ready")
        pick_turned = sem("pick_turned")
        pick_t_ready = sem("pick_t_ready")
        group_sums = sem("group_sums")
        var3_ready = sem("var3_ready")
        sd3_ready = sem("sd3_ready")
        affine3_ready = sem("affine3_ready")
        out_ready = [sem(f"out_ready{k}") for k in range(KT)]
        stored = sem("stored")

        def exps(g, j):
            return g * NPAIR + (j + 1)

        def pvs(g, j):
            return g * NPAIR + (j + 1 + NBUF)

        def pool_summed(g, j):
            return g * POOL_PAIRS + (POOL_PAIRS + j + 1)

        def dve_summed(g, j):
            return g * DVE_PAIRS + (DVE_PAIRS + j + 1)

        CONSTS1 = KT * sum(PE_TAPS) + TILE_HEADS + KT + 1

        def convs(n, i):
            return (i + n * NTB) * KT

        def dve_steps(n):
            return KT * (len(TAPS) - PE_TAPS[n % 2] - SIDE_TAPS)

        def conv_steps(n, i):
            return i * dve_steps(n) + (KT + NTB * sum(dve_steps(c) for c in range(n)))

        def side_added(n, i):
            return (i + n * NTB) * (KT * (SIDE_TAPS - 1))

        x_t = x.rearrange("b (k p) h w -> b p k (h w)", p=P)
        out_t = out.rearrange("b (k p) h w -> b p k (h w)", p=P)
        block = ctx.enter_context(nc.Block())

        @block.sync
        def _(sp):
            for b in range(B):
                for k in range(KT):
                    for piece in range(X_PIECES):
                        cols = slice(piece * HW // X_PIECES, (piece + 1) * HW // X_PIECES)
                        sp.dma_start(X[:, b, k, cols], x_t[b, :, k, cols]).then_inc(x_loaded[b][k][piece], 16)
                if b == 0:
                    sp.dma_start(vec[:, :], vectors).then_inc(weights_loaded, 16)
                    sp.dma_start(wqkv[:, :, :], w_qkv_t.rearrange("(k p) o -> p k o", p=P)).then_inc(weights_loaded, 16)
                    sp.dma_start(wproj[:, :, :], w_proj_t.rearrange("(k p) o -> p k o", p=P)).then_inc(weights_loaded, 16)
                    for half in range(2):
                        sp.dma_start(wproj2[half * DH:(half + 1) * DH, :, :],
                                     w_proj_t.rearrange("(h d) o -> d h o", d=DH)).then_inc(weights_loaded, 16)

            def load_weights():
                for dst, src in ((w1, w1_t), (w_out, w_out_t)):
                    sp.dma_start(dst[:, :, :], src.rearrange("(k p) o -> p k o", p=P)).then_inc(weights1_loaded, 16)
                sp.dma_start(k_gb[:, :, :], k_norm).then_inc(weights1_loaded, 16)

            def load_late_weights():
                sp.wait_ge(bias_part, B * KT)
                for dst, src in ((w_mlp, mlp_t), (w2v, w2_v_t)):
                    sp.dma_start(dst[:, :, :], src.rearrange("(k p) o -> p k o", p=P)).then_inc(weights2_loaded, 16)
                sp.dma_start(w2q[:, :, :], w2_qk).then_inc(weights2_loaded, 16)
                sp.dma_start(w2e[:, :], w2_exp_t).then_inc(weights2_loaded, 16)

            def load_table():
                for r in range(P // RS):
                    first = rel_table[:, r * TABLE:r * TABLE + BIAS_RUN]
                    src = bass.AP(first.tensor, first.offset, [[1, RS], [TABLE * TABLE, HEADS1], [1, BIAS_RUN]])
                    sp.dma_start(table[r * RS:(r + 1) * RS, :, 0:BIAS_RUN], src).then_inc(table_loaded, 16)

            def store_out():
                for b in range(B):
                    for k in range(KT):
                        for half in range(2):
                            cols = slice(half * HW // 2, (half + 1) * HW // 2)
                            sp.wait_ge(out_ready[k], 2 * b + half + 1)
                            sp.dma_start(out_t[b, :, k, cols], X[:, b, k, cols]).then_inc(stored, 16)
                sp.wait_ge(stored, 16 * B * KT * 2)

            sp.wait_ge(layer0_done, B)
            load_weights()
            load_table()
            load_late_weights()
            store_out()

        @block.gpsimd
        def _(pool):
            pool.memset(eps[:, 0:1], EPS_BN).then_inc(consts_ready, 1)
            pool.memset(eps[:, 1:2], EPS_LN).then_inc(consts_ready, 1)
            pool.memset(ones[:, :], 1.0).then_inc(consts_ready, 1)
            pool.memset(ident[:, :], 0.0).then_inc(pool_chain, 1)
            pool.memset(mean8[:, :], 1.0 / GROUP0).then_inc(pool_chain, 1)
            pool.memset(mean32[:, :], 1.0 / 32).then_inc(pool_chain, 1)
            pool.wait_ge(pool_chain, 3)
            pool.affine_select(out=ident[:, :], in_=ident[:, :], compare_op=ALU.not_equal, fill=1.0,
                               base=0, pattern=[[-1, P]], channel_multiplier=1).then_inc(ident_ready, 1)
            chain = 3
            for m, n in ((mean8, GROUP0), (mean32, 32)):
                blocks = m[:, :].rearrange("p (a c) -> p a c", c=n)
                pool.affine_select(out=blocks, in_=blocks, compare_op=ALU.is_ge, fill=0.0, base=0,
                                   pattern=[[-n, P // n], [0, n]], channel_multiplier=1).then_inc(pool_chain, 1)
                chain += 1
                pool.wait_ge(pool_chain, chain)
                pool.affine_select(out=blocks, in_=blocks, compare_op=ALU.is_ge, fill=0.0, base=n - 1,
                                   pattern=[[n, P // n], [0, n]], channel_multiplier=-1).then_inc(consts_ready, 1)

            def later_constants():
                pool.wait_ge(consts_ready, CONSTS)
                for n, name in enumerate(("dw1", "dw2")):
                    for k in range(KT):
                        for t in range(PE_TAPS[n]):
                            pool.tensor_scalar(diag[n][:, k, t, :], ident[:, :], col(name, k * 9 + t), 0.0,
                                               ALU.mult, ALU.add).then_inc(diag_ready, 1)
                pool.iota(count[:, :], pattern=[[1, C]], base=0, channel_multiplier=0,
                          allow_small_or_imprecise_dtypes=True).then_inc(diag_ready, 1)
                row0 = (NTB - 1) * TILE_HEADS
                pool.memset(var_cols[:, :], 0.0).then_inc(pool1_chain, 1)
                pool.memset(head_of[:, :], 1.0).then_inc(pool1_chain, 1)
                pool.wait_ge(pool1_chain, 2)
                for h in range(TILE_HEADS):
                    pool.tensor_copy(var_cols[:, row0 + h:row0 + h + 1], mean32[:, h * D1:h * D1 + 1])\
                        .then_inc(diag_ready, 1)
                for half in range(KT):
                    rows = head_of[half * VAR_ROWS:(half + 1) * VAR_ROWS, :]
                    pool.affine_select(out=rows, in_=rows, compare_op=ALU.is_ge, fill=0.0, base=0,
                                       pattern=[[1, NTB * P]], channel_multiplier=-D1).then_inc(pool1_chain, 1)
                    pool.wait_ge(pool1_chain, 3 + half)
                    pool.affine_select(out=rows, in_=rows, compare_op=ALU.is_ge, fill=0.0, base=D1 - 1,
                                       pattern=[[-1, NTB * P]], channel_multiplier=D1).then_inc(diag_ready, 1)

            def side_sums(n):
                with pool.Fori(0, NTB) as i:
                    for k in range(KT):
                        for t in range(1, SIDE_TAPS):
                            if t > 1:
                                pool.wait_ge(side_taps, side_added(n, i) + (k * (SIDE_TAPS - 1) + t - 1))
                            pool.wait_ge(side_made, convs(n, i) * SIDE_TAPS + (k * SIDE_TAPS + t + 1))
                            pool.tensor_tensor(side[:, 0, k, :], side[:, 0, k, :], side[:, t, k, :], ALU.add)\
                                .then_inc(side_taps, 1)

            pool.sem_inc(pool_sums, POOL_PAIRS)
            pool.sem_inc(pool_total_ready, 1)

            def sums(g):
                for j in range(1, POOL_PAIRS):
                    pool.wait_ge(exp_done, exps(g, j))
                    if j == 1:
                        pool.wait_ge(pool_total_ready, g + 1)
                        pool.tensor_tensor(acc_pool[:, :, :], prob[:, 0, :, :], prob[:, 1, :, :],
                                           ALU.add).then_inc(pool_sums, 2)
                    else:
                        pool.wait_ge(pool_sums, pool_summed(g, j - 1))
                        pool.tensor_tensor(acc_pool[:, :, :], acc_pool[:, :, :], prob[:, j % NBUF, :, :],
                                           ALU.add).then_inc(pool_sums, 1)
                pool.wait_ge(pool_sums, pool_summed(g, POOL_PAIRS - 1))
                pool.tensor_tensor(pool_total[:, :], acc_pool[:, 0, :], acc_pool[:, 1, :],
                                   ALU.add).then_inc(pool_total_ready, 1)

            for b in range(B):
                pool.wait_ge(b_out_ready, b + 1)
                pool.wait_ge(y_added, b * NH * NTB * KT + KT)
                for k in range(KT):
                    last = pool.tensor_scalar(Y[:, k, :], X[:, b, k, :], 1.0, b_out[:, k:k + 1], ALU.mult, ALU.add)
                last.then_inc(y_init, 1)
                with pool.Fori(0, NH) as h:
                    hh = h + b * NH
                    pool.wait_ge(y_added, hh * (NTB * KT) + KT)
                    pool.wait_ge(weights_loaded, 16 * 5)
                    pool.tensor_copy(wp_head[:, :], wproj2[:, ds(h, 1), :].rearrange("p a o -> p (a o)"))\
                        .then_inc(head_wp_ready, 1)
                    with pool.Fori(0, NTB) as tb:
                        sums(hh * NTB + tb)
            pool.wait_ge(layer0_done, B)
            for edge in (0, PAD - 1):
                pool.memset(H[:, :, edge, :], 0.0).then_inc(border_ready, 1)
                pool.memset(H[:, :, 1:1 + IMG, edge:edge + 1], 0.0).then_inc(border_ready, 1)
            later_constants()
            pool.wait_ge(diag_ready, CONSTS1)
            for b in range(B):
                side_sums(2 * b)
                side_sums(2 * b + 1)

        @block.scalar
        def _(act):
            def attention_layer():
                def high_parts(hh, i):
                    q, k = slice(0, DH), slice(DH, P)
                    cols = slice(i * TB, (i + 1) * TB)
                    act.wait_ge(qk_ready, hh * NTB + (i + 1))
                    for dst, half in ((q_hh[q, cols], q), (k_hl[k, cols], k)):
                        act.activation(dst, st[i // 2 % 2][half, i % 2, :], ACT.Identity,
                                       bias=b_head[half, 0:1]).then_inc(hi_done, 1)
                    act.wait_ge(hi_done, (hh * NTB + i) * PARTS + 2)
                    for dst, src in ((q_hh[k, cols], q_hh[q, cols]), (k_h1[k, cols], k_hl[k, cols])):
                        act.activation(dst, src, ACT.Copy).then_inc(hi_done, 1)

                def prepare(hh, tail):
                    if tail:
                        copy_out(hh * NTB + (-1))
                    act.wait_ge(head_w_ready, hh + 1)
                    for i in range(NTB + V_LAG):
                        if i < NTB:
                            high_parts(hh, i)
                        if i >= V_LAG:
                            i_v = i - V_LAG
                            act.wait_ge(v_ready, hh * NTB + (i_v + 1))
                            act.activation(v_sb[:, SUBS * i_v:SUBS * (i_v + 1), :],
                                           pvo[:, 0:SUBS * DH].rearrange("p (s d) -> p s d", d=DH),
                                           ACT.Copy).then_inc(v_copied, 1)

                def max_row(g, tb):
                    act.wait_ge(max_turned, g + 1)
                    act.activation(q_lm[0:LO_ROW + 1, ds(tb * TB, TB)], misc[0:LO_ROW + 1, :], ACT.Copy)\
                        .then_inc(max_row_ready, 1)

                def copy_out(g):
                    act.wait_ge(pv_done, pvs(g, NPAIR - 1))
                    act.activation(o_raw[:, :], pvo[:, :], ACT.Copy).then_inc(o_copied, 1)

                def step(g, tb, tail, turn, norm=False):
                    for j in range(NPAIR):
                        act.wait_ge(st_ready, exps(g, j))
                        act.wait_ge(pv_done, g * NPAIR + (j + 1))
                        if j >= NBUF:
                            act.wait_ge(pool_sums, pool_summed(g, j - NBUF))
                        else:
                            act.wait_ge(dve_sums, g * DVE_PAIRS + (j + 1))
                        act.activation(prob[:, j % NBUF, :, :], st[j % 2][:, :, :], ACT.Exp,
                                       scale=SCALE0).then_inc(exp_done, 1)
                        if j == 0 and tail:
                            copy_out(g + (-1))
                        if turn and j == TURN_SLOT:
                            max_row(g + 1, tb + 1)
                        if norm and j == ACT_NORM_SLOT:
                            group_sd(1)

                def group_sd(b):
                    act.wait_ge(group_var_ready, b + 1)
                    act.activation(gn[:, 3, :], misc[:, 4:4 + KT], ACT.Sqrt, bias=eps[:, 0:1]).then_inc(sd_ready, 1)

                def steps(hh, norm=False):
                    max_row(hh * NTB, 0)
                    step(hh * NTB, 0, tail=False, turn=True)
                    with act.Fori(1, NTB - 1) as tb:
                        step(hh * NTB + tb, tb, tail=True, turn=True)
                    step(hh * NTB + (NTB - 1), NTB - 1, tail=True, turn=False, norm=norm)

                act.wait_ge(consts_ready, CONSTS)
                act.sem_inc(o_copied, 1)
                group_sd(0)
                for b in range(B):
                    prepare(b * NH, tail=b > 0)
                    with act.Fori(0, NH - 1) as h:
                        steps(h + b * NH)
                        prepare(h + (b * NH + 1), tail=True)
                    steps(b * NH + NH - 1, norm=b == 0)
                copy_out(B * NH * NTB - 1)

            def later_layers():
                def sqrt_of(dst, src, e):
                    return act.activation(dst, src, ACT.Sqrt, bias=eps[:, e:e + 1])

                def fill_h(b):
                    last = (NTB - 1, KT - 1)
                    for i in range(NTB):
                        if b > 0:
                            act.wait_ge(conv_step, conv_steps(2 * b - 1, min(i + 2, NTB)))
                            act.wait_ge(conv_part, convs(2 * b - 1, min(i + 2, NTB)))
                        for k in range(KT):
                            act.activation(H[:, k, 1 + i * ROWS:1 + (i + 1) * ROWS, 1:1 + IMG],
                                           X[:, b, k, i * TB:(i + 1) * TB].rearrange("p (r c) -> p r c", c=IMG), ACT.Identity,
                                           scale=bn[:, 2, k:k + 1], bias=bn[:, 3, k:k + 1])\
                                .then_inc(h_ready, 1 + KT if (i, k) == last else 1)

                def keys_and_queries(b):
                    act.wait_ge(conv_step, conv_steps(2 * b + 1, 0))
                    for i in range(NTB):
                        n = (b * NTB + i) * KT
                        for m in range(KT):
                            act.wait_ge(q_ready, n + m + 1)
                            q_bank = bank[i % 2 * 2 + m][:, :]
                            act.activation(H[:, m, 1 + i * ROWS:1 + (i + 1) * ROWS, 1:1 + IMG],
                                           q_bank.rearrange("p (r c) -> p r c", c=IMG), ACT.Copy).then_inc(q_kept, 1)
                            if i > 0:
                                act.wait_ge(q_var_part, n - KT + m + 1)
                            act.activation(q_sq[:, m, :], q_bank, ACT.Square).then_inc(q_sq_ready, 1)
                        if i == KV_AT:
                            for j in range(JT):
                                act.wait_ge(kv_ready, b * JT + j + 1)
                                act.activation(vv[:, j, :], bank[4 + j][:, C:2 * C], ACT.Copy).then_inc(v_got, 1)
                        if i == K_SD_AT:
                            act.wait_ge(k_var_ready, b + 1)
                            sqrt_of(k_st[:, 2, :, :], k_st[:, 1, :, :], 1).then_inc(k_sd_ready, 1)
                    act.wait_ge(q_var_part, (b + 1) * NTB * KT)
                    sqrt_of(q_sd[:, :], bank[7][:, :], 1).then_inc(q_sd_ready, 1)

                def outputs(b):
                    for i in range(NTB):
                        n = (b * NTB + i) * KT
                        for m in range(KT):
                            act.wait_ge(q_rs_spread, n + m + 1)
                            if i >= 2:
                                act.wait_ge(o_placed, n - KT + m + 1)
                            act.activation(o_part[:, i % 2, m, :], bank[m][:, :], ACT.Copy).then_inc(q_rs_copied, 1)

                def side_products(n, name):
                    with act.Fori(0, NTB) as i:
                        for k in range(KT):
                            act.wait_ge(conv_step, conv_steps(n, i) + (k + 1 - KT))
                            for t in range(SIDE_TAPS):
                                tap = len(TAPS) - SIDE_TAPS + t
                                dy, dx = TAPS[tap]
                                act.activation(side[:, t, k, :].rearrange("p (r c) -> p r c", c=IMG),
                                               H[:, k, ds(i * ROWS + dy, ROWS), dx:dx + IMG], ACT.Copy,
                                               scale=col(name, k * 9 + tap)).then_inc(side_made, 1)

                def layer1():
                    act.wait_ge(var1_ready, 1)
                    sqrt_of(bn[:, 0, :], mv1[:, :, 1], 0).then_inc(sd1_ready, 1)
                    act.wait_ge(affine1_ready, 1)
                    for b in range(B):
                        fill_h(b)
                        act.wait_ge(border_ready, 4)
                        act.wait_ge(h_ready, (b + 1) * (NTB + 1) * KT)
                        side_products(2 * b, "dw1")
                        keys_and_queries(b)
                        outputs(b)
                        act.wait_ge(o_placed, (b + 1) * NTB * KT + KT)
                        side_products(2 * b + 1, "dw2")
                    act.wait_ge(var1_ready, 2)
                    sqrt_of(bn[:, 0, :], mv1[:, :, 1], 0).then_inc(sd1_ready, 1)

                def mlp(b):
                    for i in range(NTB):
                        n = b * NTB + i
                        if n >= 2:
                            act.wait_ge(mlp_ready, (n - 1) * KT)
                        for k in range(KT):
                            act.activation(relu_h[:, n % 2, k, :], X[:, b, k, i * TB:(i + 1) * TB], ACT.Relu,
                                           scale=bn[:, 2, k:k + 1], bias=bn[:, 3, k:k + 1]).then_inc(mlp_in, 1)

                def gates():
                    for n in range(B * NTB + 1):
                        if n < B * NTB:
                            act.wait_ge(gate_ready, n + 1)
                            if n >= 2:
                                act.wait_ge(x3_ready, (n - 1) * KT)
                            act.activation(s_relu[:, n % 2, :], bank[n % 2][:, :], ACT.Relu, bias=c2[:, 1:2])\
                                .then_inc(s_relu_ready, 1)
                        if n > 0:
                            b, i = (n - 1) // NTB, (n - 1) % NTB
                            for k in range(KT):
                                act.wait_ge(x3_ready, (n - 1) * KT + k + 1)
                                if n > 1 or k > 0:
                                    act.wait_ge(sq3_ready, (n - 1) * KT + k)
                                act.activation(junk[:, :], X[:, b, k, i * TB:(i + 1) * TB], ACT.Square,
                                               accum_out=sums3[:, 1, b, k, i:i + 1]).then_inc(sq3_ready, 1)

                def layer23():
                    act.wait_ge(affine1_ready, 2)
                    for b in range(B):
                        mlp(b)
                    gates()
                    act.wait_ge(norm3_ready, 1)
                    act.activation(st3[:, 0, :, :], tot3[:, :, 1, :], ACT.Sqrt).then_inc(nrm3_ready, 1)
                    act.wait_ge(var3_ready, 1)
                    sqrt_of(st3[:, 3, :, :], st3[:, 2, :, :], 0).then_inc(sd3_ready, 1)
                    act.wait_ge(affine3_ready, 1)
                    for b in range(B):
                        for half in range(2):
                            xx = X[:, b, 0, half * HW // 2:(half + 1) * HW // 2]
                            act.activation(xx, xx, ACT.Identity, scale=st3[:, 4, 0, b:b + 1],
                                           bias=st3[:, 5, 0, b:b + 1]).then_inc(out_ready[0], 1)

                layer1()
                layer23()

            attention_layer()
            later_layers()

        @block.vector
        def _(dve):
            def attention_layer():
                chain = [0]

                def link(ins):
                    chain[0] += 1
                    ins.then_inc(dve_chain, 1)
                    dve.wait_ge(dve_chain, chain[0])

                dve.sem_inc(mx_free, 2)
                dve.sem_inc(dve_sums, DVE_PAIRS)
                dve.sem_inc(y_added, KT)
                dve.memset(q_lm[0:DH, :], 0.0)
                dve.memset(max_cols[:, :, :], 0.0)
                link(dve.memset(k_h1[0:DH, :], 0.0))
                dve.memset(k_h1[0:1, :], 1.0)
                link(dve.memset(k_h1[LO_ROW:LO_ROW + 1, :], 1.0))
                dve.wait_ge(ident_ready, 1)
                dve.tensor_copy(ident_bf[:, :], ident[:, :]).then_inc(consts_ready, 1)

                def group_norm(b, stage):
                    (channel_means, variance, scale_and_shift, biases, out_bias)[stage](b)

                def channel_means(b):
                    if b == 0:
                        for k in range(KT):
                            for i in range(NTB):
                                if i % (NTB // X_PIECES) == 0:
                                    dve.wait_ge(x_loaded[b][k][i // (NTB // X_PIECES)], 16)
                                last = dve.bn_stats(stats[:, k, i, :], X[:, b, k, i * TB:(i + 1) * TB])
                            link(last)
                    else:
                        dve.wait_ge(early_stats, KT * NTB)
                    for k in range(KT):
                        last = dve.bn_aggr(mv[:, k, :], stats[:, k, :, :].rearrange("p i s -> p (i s)"))
                    link(last)
                    link(dve.tensor_copy(gn[:, 0, :], mv[:, :, 0]))
                    dve.tensor_copy(gn[:, 1, :], mv[:, :, 1]).then_inc(ch_mean_ready, 1)
                    dve.wait_ge(ch_mean_ready, b + 1)

                def variance(b):
                    dve.wait_ge(group_mean_ready, b + 1)
                    link(dve.tensor_copy(gn[:, 2, :], misc[:, 0:KT]))
                    link(dve.tensor_tensor(gn[:, 4, :], gn[:, 0, :], gn[:, 2, :], ALU.subtract))
                    link(dve.tensor_tensor(gn[:, 4, :], gn[:, 4, :], gn[:, 4, :], ALU.mult))
                    dve.tensor_tensor(gn[:, 4, :], gn[:, 4, :], gn[:, 1, :], ALU.add).then_inc(ch_spread_ready, 1)

                def scale_and_shift(b):
                    dve.wait_ge(sd_ready, b + 1)
                    link(dve.reciprocal(gn[:, 5, :], gn[:, 3, :]))
                    link(dve.tensor_tensor(gn[:, 5, :], gn[:, 5, :], col("gn_scale", 0, KT), ALU.mult))
                    link(dve.tensor_tensor(gn[:, 6, :], gn[:, 2, :], gn[:, 5, :], ALU.mult))
                    dve.tensor_tensor(gn[:, 6, :], col("gn_bias", 0, KT), gn[:, 6, :], ALU.subtract)\
                        .then_inc(affine_ready, 1)

                def biases(b):
                    dve.wait_ge(bias_ready, b + 1)
                    link(dve.tensor_tensor(b_qk[:, :], misc[:, 8:8 + NH], col("b_qk", 0, NH), ALU.add))
                    dve.tensor_tensor(b_v[:, :], misc[:, 16:16 + KT], col("b_v", 0, KT), ALU.add).then_inc(bv_ready, 1)

                def out_bias(b):
                    dve.wait_ge(out_bias_ready, b + 1)
                    dve.tensor_tensor(b_out[:, :], misc[:, 24:24 + KT], col("b_proj", 0, KT), ALU.add).then_inc(b_out_ready, 1)
                    dve.wait_ge(b_out_ready, b + 1)

                def prepare(hh, h, tail, to):
                    dve.tensor_copy(b_head[:, :], b_qk[:, ds(h, 1)])
                    for k in range(KT):
                        dve.tensor_scalar(w_head[:, k, 0:2 * DH], wqkv[:, k, ds(h * (2 * DH), 2 * DH)],
                                          gn[:, 5, k:k + 1], None, ALU.mult)
                        last = dve.tensor_scalar(w_head[:, k, 2 * DH:QKV], wqkv[:, k, ds(h * DH + V_COL, DH)],
                                                 gn[:, 5, k:k + 1], None, ALU.mult)
                    last.then_inc(head_w_ready, 1)
                    dve.wait_ge(head_w_ready, hh + 1)
                    q, k = slice(0, DH), slice(DH, P)
                    g_last = hh * NTB + (-1)
                    if tail:
                        all_sums(g_last)
                    for i in range(NTB + LAG):
                        units = range((i - LAG) * SUBS, (i - LAG + 1) * SUBS) if i >= LAG else ()
                        for u in units:
                            unit_max(hh * NTB, u)
                        if i < NTB:
                            cols = slice(i * TB, (i + 1) * TB)
                            for dst, half, hi in ((q_lm[k, cols], q, q_hh[q, cols]), (k_hl[q, cols], k, k_hl[k, cols])):
                                dve.wait_ge(hi_done, (hh * NTB + i) * PARTS + 2)
                                dve.scalar_tensor_tensor(dst, st[i // 2 % 2][half, i % 2, :], b_head[half, 0:1], hi,
                                                         ALU.add, ALU.subtract).then_inc(lo_done, 1)
                        if tail and i == TAIL_AT:
                            invert(g_last)
                        if tail and i == TAIL_AT + 1:
                            normalise(g_last)
                        if tail and 0 <= i - TAIL_AT - 2 < KT:
                            add_out(g_last, NTB - 1, i - TAIL_AT - 2, to)
                    row_max(hh * NTB)

                def unit_max(g, u):
                    dve.wait_ge(mx_ready, g * UNITS + (u + 1))
                    dve.tensor_reduce(part_max[:, u % SUBS, u // SUBS:u // SUBS + 1], mx[u % 2][:, :], AX.X,
                                      ALU.max).then_inc(mx_free, 1)

                def row_max(g):
                    dve.wait_ge(mx_free, g * UNITS + (UNITS + 2))
                    dve.tensor_reduce(neg_max[:, :], part_max[:, :, :], AX.X, ALU.max, negate=True)\
                        .then_inc(neg_max_ready, 1)
                    dve.wait_ge(neg_max_ready, g + 1)
                    dve.tensor_copy(max_cols[:, :, 0], neg_max[:, :]).then_inc(max_hi_ready, 1)
                    dve.wait_ge(max_hi_ready, g + 1)
                    dve.tensor_tensor(max_cols[:, :, LO_ROW], neg_max[:, :], max_cols[:, :, 0], ALU.subtract)\
                        .then_inc(max_cols_ready, 1)

                def pair_sum(g, i):
                    j = POOL_PAIRS + i
                    dve.wait_ge(exp_done, exps(g, j))
                    if i == 0:
                        dve.tensor_copy(acc_dve[:, :, :], prob[:, j % NBUF, :, :]).then_inc(dve_sums, 1)
                    else:
                        dve.wait_ge(dve_sums, dve_summed(g, i - 1))
                        dve.tensor_tensor(acc_dve[:, :, :], acc_dve[:, :, :], prob[:, j % NBUF, :, :],
                                          ALU.add).then_inc(dve_sums, 1)

                def all_sums(g):
                    pair_sum(g, DVE_PAIRS - 1)
                    dve.wait_ge(dve_sums, dve_summed(g, DVE_PAIRS - 1))
                    dve.tensor_tensor(total[:, :], acc_dve[:, 0, :], acc_dve[:, 1, :], ALU.add).then_inc(dve_folded, 1)
                    dve.wait_ge(dve_folded, g + 1)
                    dve.wait_ge(pool_total_ready, g + 2)
                    dve.tensor_tensor(total[:, :], total[:, :], pool_total[:, :], ALU.add).then_inc(total_ready, 1)

                def invert(g):
                    dve.wait_ge(total_turned, g + 1)
                    dve.reciprocal(inv_cols[:, :], misc[:, 0:SUBS]).then_inc(inv_ready, 1)

                def normalise(g):
                    dve.wait_ge(o_copied, g + 2)
                    dve.wait_ge(inv_spread, g + 1)
                    dve.tensor_tensor(o_norm[:, :], o_raw[:, :], misc[:, :], ALU.mult).then_inc(o_norm_ready, 1)

                def add_out(g, tb, m, to):
                    dve.wait_ge(proj_ready, g * KT + (m + 1))
                    y = Y[:, m, ds(tb * TB, TB)]
                    dve.tensor_tensor(to[:, m, ds(tb * TB, TB)], misc[:, :], y, ALU.add).then_inc(y_added, 1)

                def step(g, tb, tail, turn, to, spare=None):
                    if tail:
                        all_sums(g + (-1))
                    for j in range(NPAIR):
                        if turn:
                            for u in SLOTS[j]:
                                unit_max(g + 1, u)
                        if tail and j == SUM_SLOT:
                            invert(g + (-1))
                        if tail and j == INV_SLOT:
                            normalise(g + (-1))
                        if tail and j in PROJ_SLOTS:
                            add_out(g + (-1), tb + (-1), PROJ_SLOTS.index(j), to)
                        if turn and j == LAST_UNIT_SLOT:
                            row_max(g + 1)
                        if j > POOL_PAIRS:
                            pair_sum(g, j - 1 - POOL_PAIRS)
                        if spare:
                            spare(j)

                def steps(hh, to, spare=None):
                    step(hh * NTB, 0, tail=False, turn=True, to=to)
                    with dve.Fori(1, NTB - 1) as tb:
                        step(hh * NTB + tb, tb, tail=True, turn=True, to=to)
                    step(hh * NTB + (NTB - 1), NTB - 1, tail=True, turn=False, to=to, spare=spare)

                def tail_alone(g, tb, to):
                    all_sums(g)
                    invert(g)
                    normalise(g)
                    for m in range(KT):
                        add_out(g, tb, m, to)

                def next_stats(b):
                    def f(j):
                        for k in range(KT):
                            if b == 0 and 1 <= j <= NTB:
                                dve.wait_ge(x_loaded[1][k][(j - 1) // (NTB // X_PIECES)], 16)
                                dve.bn_stats(stats[:, k, j - 1, :], X[:, 1, k, (j - 1) * TB:j * TB]).then_inc(early_stats, 1)
                            if b > 0 and 1 <= j <= NTB:
                                dve.wait_ge(layer0_done, 1)
                                dve.bn_stats(stats1[:, k, 0, j - 1, :], X[:, 0, k, (j - 1) * TB:j * TB])\
                                    .then_inc(early_stats, 1)
                            if b > 0 and NTB < j < 2 * NTB:
                                i = j - NTB - 1
                                dve.wait_ge(y_added, (B * NH * NTB - 1) * KT + KT)
                                dve.bn_stats(stats1[:, k, 1, i, :], X[:, 1, k, i * TB:(i + 1) * TB])\
                                    .then_inc(early_stats, 1)
                        if b == 0:
                            for stage, slot in enumerate(DVE_NORM_SLOTS):
                                if j == slot:
                                    group_norm(1, stage)
                    return f

                def layer0_image(b):
                    dve.wait_ge(y_added, (b + 1) * NH * NTB * KT + KT)
                    dve.sem_inc(layer0_done, 1)
                    dve.wait_ge(layer0_done, b + 1)

                for b in range(B):
                    if b == 0:
                        dve.wait_ge(weights_loaded, 16 * 5)
                        for stage in range(len(DVE_NORM_SLOTS)):
                            group_norm(0, stage)
                    prepare(b * NH, 0, tail=b > 0, to=X[:, 0, :, :])
                    if b > 0:
                        layer0_image(0)
                    dve.wait_ge(y_init, b + 1)
                    with dve.Fori(0, NH - 1) as h:
                        steps(h + b * NH, Y)
                        prepare(h + (b * NH + 1), h + 1, tail=True, to=Y)
                    steps(b * NH + NH - 1, X[:, b, :, :], next_stats(b))
                tail_alone(B * NH * NTB - 1, NTB - 1, X[:, B - 1, :, :])
                layer0_image(B - 1)

            def later_layers():
                chain1 = [0]

                def link1(ins):
                    chain1[0] += 1
                    ins.then_inc(dve1_chain, 1)
                    dve.wait_ge(dve1_chain, chain1[0])

                def batch_stats(g, beta, n):
                    for k in range(KT):
                        for i in range(NTB):
                            if n > 1 or i == NTB - 1:
                                last = dve.bn_stats(stats1[:, k, 1, i, :], X[:, 1, k, i * TB:(i + 1) * TB])
                        link1(last)
                    dve.wait_ge(early_stats, 2 * KT * NTB + KT * (NTB - 1) if n == 1 else 3 * KT * NTB + KT * (NTB - 1))
                    for k in range(KT):
                        last = dve.bn_aggr(mv1[:, k, :], stats1[:, k, :, :, :].rearrange("p b i s -> p (b i s)"))
                    last.then_inc(var1_ready, 1)
                    dve.wait_ge(var1_ready, n)
                    dve.wait_ge(sd1_ready, n)
                    link1(dve.reciprocal(bn[:, 1, :], bn[:, 0, :]))
                    link1(dve.tensor_tensor(bn[:, 2, :], bn[:, 1, :], col(g, 0, KT), ALU.mult))
                    link1(dve.tensor_tensor(bn[:, 1, :], mv1[:, :, 0], bn[:, 2, :], ALU.mult))
                    dve.tensor_tensor(bn[:, 3, :], col(beta, 0, KT), bn[:, 1, :], ALU.subtract).then_inc(affine1_ready, 1)

                def centre_wq():
                    for k in range(KT):
                        w = w1[:, k, 0:C].rearrange("p (h d) -> p h d", d=D1)
                        link1(dve.tensor_reduce(q_mean[:, k, :], w, AX.X, ALU.add))
                        link1(dve.tensor_scalar(q_mean[:, k, :], q_mean[:, k, :], 1.0 / D1, None, ALU.mult))
                        dve.tensor_tensor(w, w, q_mean[:, k, :].unsqueeze(2).broadcast_to([P, HEADS1, D1]),
                                          ALU.subtract).then_inc(wq1_ready, 1)

                def convolve(n, name, after=None):

                    def blk(i):
                        steps = conv_steps(n, i)
                        first = PE_TAPS[n % 2]
                        for t in range(first, 9 - SIDE_TAPS):
                            dy, dx = TAPS[t]
                            for k in range(KT):
                                src = H[:, k, ds(i * ROWS + dy, ROWS), dx:dx + IMG]
                                dst = Z[:, k, ds(i * TB, TB)].rearrange("p (r c) -> p r c", c=IMG)
                                w = col(name, k * 9 + t)
                                if t == first:
                                    dve.wait_ge(conv_part, convs(n, i) + (k + 1))
                                    part = bank[k][:, :].rearrange("p (r c) -> p r c", c=IMG)
                                    dve.scalar_tensor_tensor(dst, src, w, part, ALU.mult, ALU.add)\
                                        .then_inc(conv_taken, 1)
                                else:
                                    if t == first + 1:
                                        dve.wait_ge(conv_taken, convs(n, i) + (k + 1 + KT))
                                    else:
                                        dve.wait_ge(conv_step, steps + ((t - first - 2) * KT + k + 1))
                                    dve.scalar_tensor_tensor(dst, src, w, dst, ALU.mult, ALU.add).then_inc(conv_step, 1)
                        for k in range(KT):
                            dve.wait_ge(conv_step, steps + ((9 - SIDE_TAPS - first - 2) * KT + k + 1))
                            dve.wait_ge(side_taps, side_added(n, i) + (k + 1) * (SIDE_TAPS - 1))
                            dst = Z[:, k, ds(i * TB, TB)]
                            dve.tensor_tensor(dst, dst, side[:, 0, k, :], ALU.add).then_inc(conv_step, 1)

                    if after is None:
                        with dve.Fori(0, NTB) as i:
                            blk(i)
                    else:
                        blk(0)
                        with dve.Fori(1, NTB) as i:
                            blk(i)
                            after(i + (-1))
                        after(NTB - 1)

                def downsample(b):
                    dve.wait_ge(conv_step, conv_steps(2 * b + 1, 0))
                    if b > 0:
                        dve.wait_ge(kv_ready, b * JT)
                    weights = []
                    for r in range(1, PERIOD):
                        f = np_f32(r * RATIO - int(r * RATIO))
                        weights.append((np_f32(1.0 - f), f, int(r * RATIO)))
                    for k in range(KT):
                        src = Z[:, k, :].rearrange("p (r c) -> p r c", c=IMG)
                        dst = rows_i[:, k, :, :]
                        last = dve.tensor_copy(dst[:, 0:RS:PERIOD, :], src[:, 0:IMG:PERIOD_ROWS, :])
                        for r, (_, f, i0) in enumerate(weights):
                            tmp = part_i[:, k, r, :].rearrange("p (g c) -> p g c", c=IMG)
                            last = dve.tensor_scalar(tmp, src[:, i0 + 1:i0 + 2 + (GROUPS - 1) * PERIOD_ROWS:PERIOD_ROWS, :],
                                                     f, None, ALU.mult)
                    link1(last)
                    for k in range(KT):
                        src = Z[:, k, :].rearrange("p (r c) -> p r c", c=IMG)
                        dst = rows_i[:, k, :, :]
                        for r, (w0, _, i0) in enumerate(weights):
                            tmp = part_i[:, k, r, :].rearrange("p (g c) -> p g c", c=IMG)
                            last = dve.scalar_tensor_tensor(
                                dst[:, r + 1:r + 2 + (GROUPS - 1) * PERIOD:PERIOD, :],
                                src[:, i0:i0 + 1 + (GROUPS - 1) * PERIOD_ROWS:PERIOD_ROWS, :], w0, tmp, ALU.mult, ALU.add)
                    link1(last)
                    for k in range(KT):
                        src = rows_i[:, k, :, :]
                        dst = zi[:, k, :].rearrange("p (r c) -> p r c", c=RS)
                        last = dve.tensor_copy(dst[:, :, 0:RS:PERIOD], src[:, :, 0:IMG:PERIOD_ROWS])
                        for r, (_, f, i0) in enumerate(weights):
                            tmp = part_i[:, k, r, 0:RS * GROUPS].rearrange("p (r g) -> p r g", g=GROUPS)
                            last = dve.tensor_scalar(tmp, src[:, :, i0 + 1:i0 + 2 + (GROUPS - 1) * PERIOD_ROWS:PERIOD_ROWS],
                                                     f, None, ALU.mult)
                    link1(last)
                    for k in range(KT):
                        src = rows_i[:, k, :, :]
                        dst = zi[:, k, :].rearrange("p (r c) -> p r c", c=RS)
                        for r, (w0, _, i0) in enumerate(weights):
                            tmp = part_i[:, k, r, 0:RS * GROUPS].rearrange("p (r g) -> p r g", g=GROUPS)
                            last = dve.scalar_tensor_tensor(
                                dst[:, :, r + 1:r + 2 + (GROUPS - 1) * PERIOD:PERIOD],
                                src[:, :, i0:i0 + 1 + (GROUPS - 1) * PERIOD_ROWS:PERIOD_ROWS], w0, tmp, ALU.mult, ALU.add)
                    link1(last)
                    for k in range(KT):
                        last = dve.tensor_copy(z_rev[:, k, :], zi[:, k, ::-1])
                    last.then_inc(zi_ready, 1)

                def keys(b):
                    def per_head(a):
                        return a.rearrange("p (h d) -> p h d", d=D1)

                    def spread(a):
                        return a.unsqueeze(2).broadcast_to([P, HEADS1, D1])

                    heads = "p j (h d) -> p j h d"
                    dve.wait_ge(v_got, (b + 1) * JT)
                    for j in range(JT):
                        last = dve.tensor_reduce(k_st[:, 0, j, :], per_head(bank[4 + j][:, 0:C]), AX.X, ALU.add)
                    link1(last)
                    link1(dve.tensor_scalar(k_st[:, 0, :, :], k_st[:, 0, :, :], 1.0 / D1, None, ALU.mult))
                    for j in range(JT):
                        last = dve.tensor_tensor(per_head(kn[:, j, :]), per_head(bank[4 + j][:, 0:C]), spread(k_st[:, 0, j, :]),
                                                 ALU.subtract)
                    link1(last)
                    link1(dve.tensor_tensor(k_sq[:, :, :], kn[:, :, :], kn[:, :, :], ALU.mult))
                    link1(dve.tensor_reduce(k_st[:, 1, :, :], k_sq[:, :, :].rearrange(heads, d=D1), AX.X, ALU.add))
                    dve.tensor_scalar(k_st[:, 1, :, :], k_st[:, 1, :, :], 1.0 / D1, None, ALU.mult).then_inc(k_var_ready, 1)
                    dve.wait_ge(k_sd_ready, b + 1)
                    link1(dve.reciprocal(k_st[:, 3, :, :], k_st[:, 2, :, :]))
                    for j in range(JT):
                        last = dve.tensor_tensor(per_head(kn[:, j, :]), per_head(kn[:, j, :]), spread(k_st[:, 3, j, :]), ALU.mult)
                    link1(last)
                    for j in range(JT):
                        last = dve.tensor_tensor(kn[:, j, :], kn[:, j, :], k_gb[:, 0, :], ALU.mult)
                    link1(last)
                    for j in range(JT):
                        last = dve.tensor_tensor(kn[:, j, :], kn[:, j, :], k_gb[:, 1, :], ALU.add)
                    last.then_inc(kn_ready, 1)
                    for m in range(KT):
                        dve.wait_ge(kk_ready, b * KT + m + 1)
                        link1(dve.tensor_tensor(kv[:, m, :], bank[6][:, m * P:(m + 1) * P], mean32[:, :], ALU.mult))
                        dve.tensor_scalar(kvg[:, m, :], kv[:, m, :], col("nq_g", m), None, ALU.mult).then_inc(kvm_ready, 1)
                    dve.wait_ge(q_sd_ready, b + 1)
                    dve.reciprocal(q_rs[:, :], q_sd[:, :]).then_inc(q_rs_ready, 1)
                    dve.wait_ge(kvc_ready, b + 1)
                    link1(dve.tensor_copy(kv_c[:, :], bank[6][:, C:C + KT]))
                    for m in range(KT):
                        dve.wait_ge(bias_part, b * KT + m + 1)
                        dve.tensor_scalar(bias_v[:, m, :], bank[4 + m][:, 0:NKEY], 1.0 / D1, kv_c[:, m:m + 1],
                                          ALU.mult, ALU.add).then_inc(bias_v_ready, 1)
                    dve.wait_ge(bias_v_ready, (b + 1) * KT)

                def outputs(b):
                    for i in range(NTB):
                        n = (b * NTB + i) * KT
                        for m in range(KT):
                            dve.wait_ge(q_rs_copied, n + m + 1)
                            dve.wait_ge(o_ready, n + m + 1)
                            dve.tensor_tensor(o_part[:, i % 2, m, :], bank[4 + i % 2 * 2 + m][:, :], o_part[:, i % 2, m, :],
                                              ALU.mult).then_inc(o_scaled, 1)
                        for m in range(KT):
                            dve.wait_ge(o_scaled, n + m + 1)
                            for r in range(ROWS // REP):
                                cell = (i * (ROWS // REP) + r) * RS
                                row = 1 + i * ROWS + r * REP
                                last = dve.tensor_tensor(
                                    H[:, m, row:row + REP, 1:1 + IMG].rearrange("p r (a c) -> p r a c", c=REP),
                                    o_part[:, i % 2, m, r * REP * IMG:(r + 1) * REP * IMG]
                                    .rearrange("p (r a c) -> p r a c", a=RS, c=REP),
                                    bias_v[:, m, cell:cell + RS].unsqueeze(1).unsqueeze(3).broadcast_to([P, REP, RS, REP]),
                                    ALU.add)
                            last.then_inc(o_placed, 1)

                def add_attention(b):
                    def f(i):
                        n = (i + b * NTB) * KT
                        for m in range(KT):
                            dve.wait_ge(pw_ready, n + (m + 1))
                            xx = X[:, b, m, ds(i * TB, TB)]
                            dve.tensor_tensor(xx, bank[2 + m][:, :], xx, ALU.add).then_inc(x_added, 1)
                    return f

                def layer1():
                    dve.sem_inc(conv_taken, KT)
                    dve.sem_inc(conv_step, KT)
                    dve.sem_inc(x_added, KT)
                    dve.sem_inc(o_placed, KT)
                    batch_stats("bn1_g", "bn1_b", 1)
                    dve.wait_ge(weights1_loaded, 16 * 3)
                    centre_wq()
                    for b in range(B):
                        convolve(2 * b, "dw1")
                        downsample(b)
                        if b > 0:
                            dve.wait_ge(x_added, b * NTB * KT + KT)
                            for k in range(KT):
                                for i in range(NTB):
                                    dve.bn_stats(stats1[:, k, b - 1, i, :], X[:, b - 1, k, i * TB:(i + 1) * TB])\
                                        .then_inc(early_stats, 1)
                        keys(b)
                        outputs(b)
                        dve.wait_ge(o_placed, (b + 1) * NTB * KT + KT)
                        convolve(2 * b + 1, "dw2", add_attention(b))
                    dve.wait_ge(x_added, B * NTB * KT + KT)
                    batch_stats("bn2_g", "bn2_b", 2)

                def layer2_weights():
                    dve.wait_ge(l2_a, 1)
                    link1(dve.tensor_copy(u_col[:, :], bank[6][:, 0:KT]))
                    for k in range(KT):
                        dve.tensor_scalar(u_all[:, k, :], ones[:, :], u_col[:, k:k + 1], None, ALU.mult)
                    dve.tensor_scalar(b2all[:, 0, :], ones[:, :], col("bq"), None, ALU.mult)
                    dve.tensor_scalar(b2all[:, 1, :], ones[:, :], col("bk"), None, ALU.mult).then_inc(l2_b, 1)
                    dve.wait_ge(l2_a, 2)
                    link1(dve.tensor_copy(c2[:, 2:3], bank[6][:, 8:9]))
                    link1(dve.tensor_tensor(c2[:, 1:2], bank[6][:, 7:8], c2[:, 2:3], ALU.subtract))
                    dve.tensor_scalar(c2[:, 0:1], col("bv"), float(HW), None, ALU.mult).then_inc(l2_b, 1)
                    dve.wait_ge(l2_b, 2)

                def mlp(b):
                    for i in range(NTB):
                        n = b * NTB + i
                        for m in range(KT):
                            dve.wait_ge(mlp_ready, n * KT + m + 1)
                            xx = X[:, b, m, i * TB:(i + 1) * TB]
                            dve.scalar_tensor_tensor(xx, bank[4 + n % 2 * 2 + m][:, :], col("bexp", m), xx, ALU.add, ALU.add,
                                                     accum_out=xsum[:, b, m, i:i + 1]).then_inc(mlp_added, 1)

                def mixing():
                    link1(dve.tensor_reduce(xs[:, :, :], xsum[:, :, :, :], AX.X, ALU.add))
                    for k in range(KT):
                        for b in range(B):
                            last = dve.scalar_tensor_tensor(xs[:, b, k:k + 1], col("bexp", k), -float(HW),
                                                            xs[:, b, k:k + 1], ALU.mult, ALU.add)
                    last.then_inc(mix_a, 1)
                    dve.wait_ge(mix_b, 1)
                    dve.tensor_scalar(v_sum[:, :], bank[3][:, 0:B], c2[:, 0:1], None, ALU.add).then_inc(mix_a, 1)
                    dve.wait_ge(mix_b, 2)
                    for m in range(KT):
                        last = dve.tensor_scalar(mixed[:, :, m], bank[3][:, 4 + m * B:4 + (m + 1) * B], 1.0 / HW, None,
                                                 ALU.mult)
                    link1(last)

                def apply_gates(b):
                    for i in range(NTB):
                        n = b * NTB + i
                        dve.wait_ge(s_relu_ready, n + 1)
                        for k in range(KT):
                            xx = X[:, b, k, i * TB:(i + 1) * TB]
                            dve.scalar_tensor_tensor(xx, s_relu[:, n % 2, :], mixed[:, b, k:k + 1], xx, ALU.mult, ALU.add,
                                                     accum_out=sums3[:, 0, b, k, i:i + 1]).then_inc(x3_ready, 1)

                def evacuate_turned(b):
                    for c in range(HW // P):
                        n = b * (HW // P) + c
                        dve.wait_ge(turned3, n + 1)
                        dve.tensor_copy(xt[:, n % 4, :], bank[2 + n % 2][:, 0:C]).then_inc(xt_ready, 1)

                def layer3():
                    dve.wait_ge(x3_ready, B * NTB * KT)
                    dve.wait_ge(sq3_ready, B * NTB * KT)
                    for q in range(2):
                        for b in range(B):
                            last = dve.tensor_reduce(tot3[:, :, q, b], sums3[:, q, b, :, :], AX.X, ALU.add)
                    last.then_inc(norm3_ready, 1)
                    dve.wait_ge(nrm3_ready, 1)
                    link1(dve.tensor_scalar(st3[:, 1, :, :], st3[:, 0, :, :], 1e-12, None, ALU.max))
                    link1(dve.reciprocal(st3[:, 0, :, :], st3[:, 1, :, :]))
                    for b in range(B):
                        evacuate_turned(b)
                        dve.wait_ge(gram_ready, b + 1)
                        dve.tensor_copy(gram_01[:, :], bank[4][:, P:C]).then_inc(gram_copied, 1)
                        dve.wait_ge(gram_whole, b + 1)
                        for m in range(KT):
                            last = dve.tensor_scalar(gram_s[:, m, :], bank[4 + m][:, 0:C], st3[:, 0, m, b:b + 1], None,
                                                     ALU.mult)
                        last.then_inc(gram_scaled, 1)
                        dve.wait_ge(gram_turned, b + 1)
                        for m in range(KT):
                            if b == 0:
                                last = dve.tensor_scalar(cos[:, m, :], bank[6 + m][:, 0:C], st3[:, 0, m, b:b + 1], None,
                                                         ALU.mult)
                            else:
                                last = dve.scalar_tensor_tensor(cos[:, m, :], bank[6 + m][:, 0:C], st3[:, 0, m, b:b + 1],
                                                                cos[:, m, :], ALU.mult, ALU.add)
                        last.then_inc(cos_added, 1)
                        dve.wait_ge(cos_added, b + 1)
                    for m in range(KT):
                        last = dve.tensor_scalar(gram_s[:, m, :], cos[:, m, :], 1.0 / B, None, ALU.mult)
                    link1(last)
                    for m in range(KT):
                        last = dve.scalar_tensor_tensor(cos[:, m, :], gram_s[:, m, :], -1.0, gram_s[:, m, :],
                                                        ALU.mult, ALU.min)
                    link1(last)
                    dve.wait_ge(diag_ready, CONSTS1)
                    for m in range(KT):
                        last = dve.max(top[:, m, :], cos[:, m, :])
                    link1(last)
                    for m in range(KT):
                        last = dve.max_index(top_i[:, m, :], top[:, m, :], cos[:, m, :])
                    link1(last)
                    link1(dve.tensor_copy(top_f[:, :, :], top_i[:, :, :]))
                    for n in range(1, NSEL):
                        for m in range(KT):
                            one = top_f[:, m, n:n + 1]
                            if n == 1:
                                last = dve.tensor_scalar(pick[:, m, :], count[:, :], one, None, ALU.is_equal)
                            else:
                                last = dve.scalar_tensor_tensor(pick[:, m, :], count[:, :], one, pick[:, m, :],
                                                                ALU.is_equal, ALU.add)
                        if n < NSEL - 1:
                            link1(last)
                    last.then_inc(pick_ready, 1)
                    for d in range(KT):
                        dve.wait_ge(pick_turned, d + 1)
                        dve.tensor_copy(pick_t[:, d, :], bank[d][:, 0:C]).then_inc(pick_t_ready, 1)
                    dve.wait_ge(group_sums, 1)
                    for m in range(KT):
                        last = dve.tensor_tensor(g3[:, m, :, :].rearrange("p q b -> p (q b)"), bank[2][:, m * 4:m * 4 + 4],
                                                 tot3[:, m, :, :].rearrange("p q b -> p (q b)"), ALU.add)
                    link1(last)
                    count3 = 1.0 / (NSEL * HW)
                    mean, sq = g3[:, :, 0, :], g3[:, :, 1, :]
                    link1(dve.tensor_scalar(g3[:, :, :, :], g3[:, :, :, :], count3, None, ALU.mult))
                    link1(dve.tensor_tensor(st3[:, 5, :, :], mean, mean, ALU.mult))
                    dve.tensor_tensor(st3[:, 2, :, :], sq, st3[:, 5, :, :], ALU.subtract).then_inc(var3_ready, 1)
                    dve.wait_ge(sd3_ready, 1)
                    link1(dve.reciprocal(st3[:, 1, :, :], st3[:, 3, :, :]))
                    for k in range(KT):
                        last = dve.tensor_scalar(st3[:, 4, k, :], st3[:, 1, k, :], col("gamma", k), None, ALU.mult)
                    link1(last)
                    link1(dve.tensor_tensor(st3[:, 2, :, :], mean, st3[:, 4, :, :], ALU.mult))
                    for k in range(KT):
                        last = dve.tensor_scalar(st3[:, 5, k, :], st3[:, 2, k, :], -1.0, col("beta", k), ALU.mult, ALU.add)
                    last.then_inc(affine3_ready, 1)
                    dve.wait_ge(affine3_ready, 1)
                    for b in range(B):
                        for half in range(2):
                            xx = X[:, b, 1, half * HW // 2:(half + 1) * HW // 2]
                            dve.tensor_scalar(xx, xx, st3[:, 4, 1, b:b + 1], st3[:, 5, 1, b:b + 1],
                                              ALU.mult, ALU.add).then_inc(out_ready[1], 1)

                layer1()
                layer2_weights()
                for b in range(B):
                    mlp(b)
                dve.wait_ge(mlp_added, B * NTB * KT)
                mixing()
                for b in range(B):
                    apply_gates(b)
                layer3()

            attention_layer()
            later_layers()

        @block.tensor
        def _(pe):
            def attention_layer():
                pe.wait_ge(consts_ready, CONSTS)
                pe.wait_ge(weights_loaded, 16 * 5)
                pe.sem_inc(pv_done, NBUF)

                def group_norm(b, stage):
                    (group_means, group_variances, biases, out_bias)[stage](b)

                def group_means(b):
                    pe.wait_ge(ch_mean_ready, b + 1)
                    pe.wait_ge(y_added, max(b * NH * NTB - 1, 0) * KT + KT)
                    pe.matmul(misc[:, 0:KT], mean8[:, :], gn[:, 0, :], start=True, stop=True).then_inc(group_mean_ready, 1)

                def group_variances(b):
                    pe.wait_ge(ch_spread_ready, b + 1)
                    pe.matmul(misc[:, 4:4 + KT], mean8[:, :], gn[:, 4, :], start=True, stop=True).then_inc(group_var_ready, 1)

                def biases(b):
                    pe.wait_ge(affine_ready, b + 1)
                    for h in range(NH):
                        for k in range(KT):
                            pe.matmul(misc[:, 8 + h:9 + h], wqkv[:, k, h * 2 * DH:(h + 1) * 2 * DH], gn[:, 6, k:k + 1],
                                      start=(k == 0), stop=(k == KT - 1))
                    for m in range(KT):
                        for k in range(KT):
                            last = pe.matmul(misc[:, 16 + m:17 + m], wqkv[:, k, V_COL + m * P:V_COL + (m + 1) * P],
                                             gn[:, 6, k:k + 1], start=(k == 0), stop=(k == KT - 1))
                    last.then_inc(bias_ready, 1)

                def out_bias(b):
                    pe.wait_ge(bv_ready, b + 1)
                    for m in range(KT):
                        for k in range(KT):
                            last = pe.matmul(misc[:, 24 + m:25 + m], wproj[:, k, m * P:(m + 1) * P], b_v[:, k:k + 1],
                                             start=(k == 0), stop=(k == KT - 1))
                    last.then_inc(out_bias_ready, 1)

                def prepare(b, hh, tail):
                    g_last = hh * NTB + (-1)
                    pe.wait_ge(head_w_ready, hh + 1)
                    if tail:
                        weighted_values(g_last, NPAIR - 1)
                    for i in range(NTB + max(LAG, V_LAG)):
                        makes_v = V_LAG <= i < NTB + V_LAG
                        units = range((i - LAG) * SUBS, (i - LAG + 1) * SUBS) if LAG <= i < NTB + LAG else ()
                        if units:
                            pe.wait_ge(hi_done, (hh * NTB + (i - LAG + 1)) * PARTS)
                            pe.wait_ge(lo_done, (hh * NTB + (i - LAG + 1)) * 2)
                            unit(hh * NTB, 0, units[0])
                        if i < NTB:
                            if i >= 4:
                                pe.wait_ge(lo_done, (hh * NTB + (i - 3)) * 2)
                            for k in range(KT):
                                last = pe.matmul(st[i // 2 % 2][:, i % 2, :], w_head[:, k, 0:2 * DH],
                                                 X[:, b, k, i * TB:(i + 1) * TB], start=(k == 0), stop=(k == KT - 1))
                            last.then_inc(qk_ready, 1)
                        if units:
                            unit(hh * NTB, 0, units[1])
                        if makes_v:
                            i_v = i - V_LAG
                            if i_v > 0:
                                pe.wait_ge(v_copied, hh * NTB + i_v)
                            else:
                                pe.wait_ge(o_copied, hh * NTB + 1)
                            for s in range(SUBS):
                                if units and s == 2:
                                    unit(hh * NTB, 0, units[2])
                                tok = (i_v * SUBS + s) * P
                                for k in range(KT):
                                    last = pe.matmul(pvo[:, s * DH:(s + 1) * DH], X[:, b, k, tok:tok + P],
                                                     w_head[:, k, 2 * DH:QKV], start=(k == 0), stop=(k == KT - 1))
                            last.then_inc(v_ready, 1)
                        for u in units[3 if makes_v else 2:]:
                            unit(hh * NTB, 0, u)
                        if tail and i == TAIL_AT:
                            turn_total(g_last)
                        if tail and i == TAIL_AT + 1:
                            spread_inverse(g_last)
                        if tail and 0 <= i - TAIL_AT - 2 < KT:
                            project(g_last, i - TAIL_AT - 2)
                    pe.wait_ge(v_copied, hh * NTB + NTB)
                    pe.wait_ge(y_added, hh * NTB * KT + KT)
                    turn_max(hh * NTB)

                def unit(g, tb, u):
                    pe.wait_ge(mx_free, g * UNITS + (u + 1))
                    keys = slice(u // SUBS * TB, (u // SUBS + 1) * TB)
                    pe.matmul(mx[u % 2][:, :], q_hh[:, ds(tb * TB + u % SUBS * P, P)], k_hl[:, keys],
                              start=True, stop=True).then_inc(mx_ready, 1)

                def turn_max(g):
                    pe.wait_ge(max_cols_ready, g + 1)
                    for s in range(SUBS):
                        last = pe.matmul(misc[0:LO_ROW + 1, s * P:(s + 1) * P], max_cols[:, s, :], ident_bf[:, :],
                                         start=True, stop=True)
                    last.then_inc(max_turned, 1)

                def scores(g, tb, j):
                    cols = ds(tb * TB, TB)
                    for c in range(2):
                        keys = slice((2 * j + c) * P, (2 * j + c + 1) * P)
                        pe.matmul(st[j % 2][:, c, :], k_hl[:, keys], q_hh[:, cols], start=True, stop=False)
                        last = pe.matmul(st[j % 2][:, c, :], k_h1[:, keys], q_lm[:, cols], start=False, stop=True)
                    last.then_inc(st_ready, 1)

                def weighted_values(g, j):
                    pe.wait_ge(exp_done, exps(g, j))
                    for c in range(2):
                        last = pe.matmul(pvo[c * DH:(c + 1) * DH, :], v_sb[:, 2 * j + c, :], prob[:, j % NBUF, c, :],
                                         start=(j == 0), stop=(j == NPAIR - 1))
                    last.then_inc(pv_done, 1)

                def turn_total(g):
                    pe.wait_ge(total_ready, g + 1)
                    for s in range(SUBS):
                        last = pe.matmul(misc[:, s:s + 1], total[:, s * P:(s + 1) * P], ones[:, 0:1], start=True, stop=True)
                    last.then_inc(total_turned, 1)

                def spread_inverse(g):
                    pe.wait_ge(inv_ready, g + 1)
                    for s in range(SUBS):
                        last = pe.matmul(misc[:, s * P:(s + 1) * P], inv_cols[:, s:s + 1].broadcast_to([P, P]), ident[:, :],
                                         start=True, stop=True)
                    last.then_inc(inv_spread, 1)

                def project(g, m):
                    pe.wait_ge(o_norm_ready, g + 1)
                    if m:
                        pe.wait_ge(y_added, g * KT + (m + KT))
                    pe.matmul(misc[:, :], wp_head[:, m * P:(m + 1) * P], o_norm[:, :],
                              start=True, stop=True).then_inc(proj_ready, 1)

                def step(g, tb, tail, turn, norm=False):
                    pe.wait_ge(max_row_ready, g + 1)
                    for j in range(NPAIR):
                        units = SLOTS[j] if turn else []
                        for u in units[0:1]:
                            unit(g + 1, tb + 1, u)
                        scores(g, tb, j)
                        for u in units[1:2]:
                            unit(g + 1, tb + 1, u)
                        if j == 0 and tail:
                            weighted_values(g + (-1), NPAIR - 1)
                        if j == 1:
                            pe.wait_ge(o_copied, g + 1)
                        if j >= 1:
                            weighted_values(g, j - 1)
                        for u in units[2:]:
                            unit(g + 1, tb + 1, u)
                        if tail and j == SUM_SLOT:
                            turn_total(g + (-1))
                        if tail and j == INV_SLOT:
                            spread_inverse(g + (-1))
                        if tail and j in PROJ_SLOTS:
                            project(g + (-1), PROJ_SLOTS.index(j))
                        if norm and j in PE_NORM_SLOTS:
                            group_norm(1, PE_NORM_SLOTS.index(j))
                        if turn and j == TURN_SLOT:
                            if tail:
                                pe.wait_ge(y_added, g * KT + KT)
                            turn_max(g + 1)

                def steps(hh, norm=False):
                    pe.wait_ge(head_wp_ready, hh + 1)
                    step(hh * NTB, 0, tail=False, turn=True)
                    with pe.Fori(1, NTB - 1) as tb:
                        step(hh * NTB + tb, tb, tail=True, turn=True)
                    step(hh * NTB + (NTB - 1), NTB - 1, tail=True, turn=False, norm=norm)

                def tail_alone(g):
                    weighted_values(g, NPAIR - 1)
                    turn_total(g)
                    spread_inverse(g)
                    for m in range(KT):
                        project(g, m)
                    pe.wait_ge(y_added, g * KT + 2 * KT)

                for stage in range(len(PE_NORM_SLOTS)):
                    group_norm(0, stage)
                for b in range(B):
                    prepare(b, b * NH, tail=b > 0)
                    with pe.Fori(0, NH - 1) as h:
                        steps(h + b * NH)
                        prepare(b, h + (b * NH + 1), tail=True)
                    steps(b * NH + NH - 1, norm=b == 0)
                tail_alone(B * NH * NTB - 1)

            def later_layers():
                def taps(n, name_i, i):
                    for k in range(KT):
                        pe.wait_ge(conv_taken, convs(n, i) + (k + 1))
                        for t in range(PE_TAPS[name_i]):
                            dy, dx = TAPS[t]
                            last = pe.matmul(bank[k][:, :], diag[name_i][:, k, t, :],
                                             H[:, k, ds(i * ROWS + dy, ROWS), dx:dx + IMG],
                                             start=(t == 0), stop=(t == PE_TAPS[name_i] - 1))
                        last.then_inc(conv_part, 1)

                def queries(b):
                    pe.wait_ge(conv_step, conv_steps(2 * b + 1, 0))
                    pe.wait_ge(wq1_ready, KT)
                    pe.wait_ge(diag_ready, CONSTS1)
                    for i in range(NTB + 1):
                        n = (b * NTB + i) * KT
                        if i < NTB:
                            if i >= 2:
                                pe.wait_ge(q_sq_ready, n - KT)
                            for m in range(KT):
                                for k in range(KT):
                                    last = pe.matmul(bank[i % 2 * 2 + m][:, :], w1[:, k, m * P:(m + 1) * P],
                                                     Z[:, k, i * TB:(i + 1) * TB], start=(k == 0), stop=(k == KT - 1))
                                last.then_inc(q_ready, 1)
                        if i == KV_AT:
                            pe.wait_ge(zi_ready, b + 1)
                            for j in range(JT):
                                for k in range(KT):
                                    last = pe.matmul(bank[4 + j][:, :], z_rev[:, k, j * P:(j + 1) * P], w1[:, k, C:3 * C],
                                                     start=(k == 0), stop=(k == KT - 1))
                                last.then_inc(kv_ready, 1)
                        if i > 0:
                            pe.wait_ge(q_sq_ready, n)
                            first = (NTB - i) * TILE_HEADS
                            for m in range(KT):
                                last = pe.matmul(bank[7][m * VAR_ROWS:(m + 1) * VAR_ROWS, :], var_cols[:, first:first + VAR_ROWS],
                                                 q_sq[:, m, :], start=(i == 1), stop=(i == NTB))
                                last.then_inc(q_var_part, 1)

                def keys(b):
                    pe.wait_ge(kn_ready, b + 1)
                    for m in range(KT):
                        for j in range(JT):
                            last = pe.matmul(bank[6][:, m * P:(m + 1) * P], kn[:, j, m * P:(m + 1) * P],
                                             vv[:, j, m * P:(m + 1) * P], start=(j == 0), stop=(j == JT - 1))
                    last.then_inc(kk_ready, KT)
                    pe.wait_ge(kvm_ready, (b + 1) * KT)
                    for m in range(KT):
                        last = pe.matmul(bank[6][:, C + m:C + m + 1], kv[:, m, :], col("nq_b", m), start=True, stop=True)
                    last.then_inc(kvc_ready, 1)
                    pe.wait_ge(table_loaded, 16 * (P // RS))
                    for m in range(KT):
                        for h4 in range(P // D1):
                            h = m * (P // D1) + h4
                            for j in range(JT):
                                start = j * (P // RS) * TABLE
                                rhs = table[:, h, start:start + RS * TABLE].rearrange("p (r c) -> p r c", c=TABLE)[:, :, 0:RS]
                                last = pe.matmul(bank[4 + m][h4 * D1:(h4 + 1) * D1, 0:NKEY], vv[:, j, h * D1:(h + 1) * D1],
                                                 rhs, start=(j == 0), stop=(j == JT - 1), tile_position=(0, h4 * D1))
                        last.then_inc(bias_part, 1)
                    pe.wait_ge(bias_v_ready, (b + 1) * KT)

                def outputs(b):
                    pe.wait_ge(q_rs_ready, b + 1)
                    for i in range(NTB):
                        n = (b * NTB + i) * KT
                        for m in range(KT):
                            half = slice(m * VAR_ROWS, (m + 1) * VAR_ROWS)
                            if i > 0:
                                pe.wait_ge(q_rs_copied, n - KT + m + 1)
                            pe.matmul(bank[m][:, :], head_of[half, i * P:(i + 1) * P], q_rs[half, :],
                                      start=True, stop=True).then_inc(q_rs_spread, 1)
                        if i >= 2:
                            pe.wait_ge(o_scaled, n - KT)
                        for m in range(KT):
                            pe.matmul(bank[4 + i % 2 * 2 + m][:, :], kvg[:, m, :],
                                      H[:, m, 1 + i * ROWS:1 + (i + 1) * ROWS, 1:1 + IMG],
                                      start=True, stop=True).then_inc(o_ready, 1)

                def pointwise(b, i):
                    n = (i + b * NTB) * KT
                    pe.wait_ge(conv_step, conv_steps(2 * b + 1, i) + dve_steps(1))
                    for m in range(KT):
                        pe.wait_ge(x_added, n + (m + 1))
                        for k in range(KT):
                            last = pe.matmul(bank[2 + m][:, :], w_out[:, k, m * P:(m + 1) * P], Z[:, k, ds(i * TB, TB)],
                                             start=(k == 0), stop=(k == KT - 1))
                        last.then_inc(pw_ready, 1)

                def layer1():
                    pe.wait_ge(border_ready, 4)
                    pe.wait_ge(diag_ready, KT * sum(PE_TAPS))
                    for b in range(B):
                        with pe.Fori(0, NTB) as i:
                            pe.wait_ge(h_ready, i * KT + (b * (NTB + 1) + 2) * KT)
                            taps(2 * b, 0, i)
                        queries(b)
                        keys(b)
                        pe.wait_ge(q_kept, (b + 1) * NTB * KT)
                        outputs(b)
                        pe.wait_ge(o_placed, (b + 1) * NTB * KT + KT)
                        taps(2 * b + 1, 1, 0)
                        with pe.Fori(1, NTB) as i:
                            taps(2 * b + 1, 1, i)
                            pointwise(b, i + (-1))
                        pointwise(b, NTB - 1)

                def layer2_weights():
                    for k in range(KT):
                        pe.matmul(bank[6][:, k:k + 1], w2q[:, 0, k * P:(k + 1) * P], col("wq_c"), start=True, stop=False)
                        last = pe.matmul(bank[6][:, k:k + 1], w2q[:, 1, k * P:(k + 1) * P], col("wk_c"),
                                         start=False, stop=True)
                    last.then_inc(l2_a, 1)
                    pe.wait_ge(l2_b, 1)
                    pe.matmul(bank[6][:, 7:8], b2all[:, 0, :], col("wq_c"), start=True, stop=False)
                    pe.matmul(bank[6][:, 7:8], b2all[:, 1, :], col("wk_c"), start=False, stop=True)
                    for k in range(KT):
                        last = pe.matmul(bank[6][:, 8:9], u_all[:, k, :], col("bexp", k), start=(k == 0), stop=(k == KT - 1))
                    last.then_inc(l2_a, 1)

                def mlp(b):
                    for i in range(NTB):
                        n = b * NTB + i
                        pe.wait_ge(mlp_in, (n + 1) * KT)
                        if n >= 2:
                            pe.wait_ge(mlp_added, (n - 1) * KT)
                        for m in range(KT):
                            for k in range(KT):
                                last = pe.matmul(bank[4 + n % 2 * 2 + m][:, :], w_mlp[:, k, m * P:(m + 1) * P],
                                                 relu_h[:, n % 2, k, :], start=(k == 0), stop=(k == KT - 1))
                            last.then_inc(mlp_ready, 1)

                def mixing():
                    pe.wait_ge(mix_a, 1)
                    for k in range(KT):
                        last = pe.matmul(bank[3][:, 0:B], w2v[:, k, :], xs[:, :, k], start=(k == 0), stop=(k == KT - 1))
                    last.then_inc(mix_b, 1)
                    pe.wait_ge(mix_a, 2)
                    for m in range(KT):
                        last = pe.matmul(bank[3][:, 4 + m * B:4 + (m + 1) * B], w2e[:, m * P:(m + 1) * P], v_sum[:, :],
                                         start=True, stop=True)
                    last.then_inc(mix_b, 1)

                def gates(b, i):
                    n = b * NTB + i
                    pe.wait_ge(mlp_added, (n + 1) * KT)
                    if n >= 2:
                        pe.wait_ge(s_relu_ready, n - 1)
                    for k in range(KT):
                        last = pe.matmul(bank[n % 2][:, :], u_all[:, k, :], X[:, b, k, i * TB:(i + 1) * TB],
                                         start=(k == 0), stop=(k == KT - 1))
                    last.then_inc(gate_ready, 1)

                def turn(n):
                    b, c = n // (HW // P), n % (HW // P)
                    if n >= 2:
                        pe.wait_ge(xt_ready, n - 1)
                    for k in range(KT):
                        last = pe.transpose(bank[2 + n % 2][:, k * P:(k + 1) * P], X[:, b, k, c * P:(c + 1) * P], ident[:, :])
                    last.then_inc(turned3, 1)

                def gram(n):
                    b, c = n // (HW // P), n % (HW // P)
                    pe.wait_ge(xt_ready, n + 1)
                    for m in range(KT):
                        last = pe.matmul(bank[4 + m][:, m * P:C], xt[:, n % 4, m * P:(m + 1) * P], xt[:, n % 4, m * P:C],
                                         start=(c == 0), stop=(c == HW // P - 1))
                    if c == HW // P - 1:
                        last.then_inc(gram_ready, 1)

                def layer3():
                    pe.wait_ge(x3_ready, B * NTB * KT)
                    chunks = HW // P
                    turn(0)
                    for n in range(B * chunks):
                        if n + 1 < B * chunks:
                            turn(n + 1)
                        gram(n)
                        if n % chunks == chunks - 1:
                            b = n // chunks
                            pe.wait_ge(gram_copied, b + 1)
                            pe.transpose(bank[5][:, 0:P], gram_01[:, :], ident[:, :]).then_inc(gram_whole, 1)
                            pe.wait_ge(gram_scaled, b + 1)
                            if b > 0:
                                pe.wait_ge(cos_added, b)
                            for m in range(KT):
                                for k in range(KT):
                                    last = pe.transpose(bank[6 + m][:, k * P:(k + 1) * P], gram_s[:, k, m * P:(m + 1) * P],
                                                        ident[:, :])
                            last.then_inc(gram_turned, 1)
                    pe.wait_ge(pick_ready, 1)
                    for d in range(KT):
                        for m in range(KT):
                            last = pe.transpose(bank[d][:, m * P:(m + 1) * P], pick[:, m, d * P:(d + 1) * P], ident[:, :])
                        last.then_inc(pick_turned, 1)
                    pe.wait_ge(pick_t_ready, KT)
                    for m in range(KT):
                        for d in range(KT):
                            last = pe.matmul(bank[2][:, m * 4:m * 4 + 4], pick_t[:, d, m * P:(m + 1) * P],
                                             tot3[:, d, :, :].rearrange("p q b -> p (q b)"), start=(d == 0), stop=(d == KT - 1))
                    last.then_inc(group_sums, 1)

                layer1()
                pe.wait_ge(weights2_loaded, 16 * 4)
                layer2_weights()
                pe.wait_ge(l2_b, 2)
                for b in range(B):
                    mlp(b)
                for b in range(B):
                    for i in range(NTB):
                        if b == 0 and i == 2:
                            mixing()
                        gates(b, i)
                layer3()

            attention_layer()
            later_layers()



def kernel(**inputs):
    import numpy as _np
    import concourse.bacc as _bacc
    from concourse import mybir as _mybir
    from concourse.bass_utils import run_bass_kernel_spmd as _run

    def columns(v):
        return _np.asarray(v).reshape(-1, P).T

    def taps(w):
        return _np.asarray(w).reshape(KT, P, 9).transpose(1, 0, 2).reshape(P, KT * 9)

    by_head = _np.arange(C).reshape(D1, HEADS1).T.reshape(-1)
    g = {k: _np.asarray(v) for k, v in inputs.items()}
    w_qkv = g["L0_conv_w_qkv"].reshape(NH, 3, DH, C)
    w_qkv = _np.concatenate([w_qkv[:, 0:2].reshape(V_COL, C), w_qkv[:, 2].reshape(C, C)])
    b_qkv = g["L0_conv_b_qkv"].reshape(NH, 3, DH)
    parts = {
        "gn_scale": columns(g["L0_conv_gn_scale"]), "gn_bias": columns(g["L0_conv_gn_bias"]),
        "b_qk": b_qkv[:, 0:2].reshape(NH, P).T, "b_v": columns(b_qkv[:, 2].reshape(-1)),
        "b_proj": columns(g["L0_conv_b_proj"]),
        "bn1_g": columns(g["L1_conv_bn1_g"]), "bn1_b": columns(g["L1_conv_bn1_b"]),
        "dw1": taps(g["L1_conv_qkv_dw"]), "dw2": taps(g["L1_conv_out_dw"][by_head]),
        "nq_g": columns(g["L1_conv_nq_g"].reshape(-1)), "nq_b": columns(g["L1_conv_nq_b"].reshape(-1)),
        "bn2_g": columns(g["L1_conv_bn2_g"]), "bn2_b": columns(g["L1_conv_bn2_b"]),
        "bexp": columns(g["L2_conv_bexp"]), "bq": columns(g["L2_conv_bq"]), "bk": columns(g["L2_conv_bk"]),
        "bv": columns(g["L2_conv_bv"]), "wq_c": columns(g["L2_conv_Wcat"][0, :E2]),
        "wk_c": columns(g["L2_conv_Wcat"][0, E2:]), "gamma": columns(g["L3_conv_gamma"]),
        "beta": columns(g["L3_conv_beta"]),
    }
    w1 = g["L1_conv_qkv_pw"].reshape(3, C, C)[:, by_head].reshape(3 * C, C)
    k_norm = _np.stack([g["L1_conv_nk_g"].reshape(-1), g["L1_conv_nk_b"].reshape(-1)])
    arrays = {
        "x": g["x"],
        "w_qkv_t": w_qkv.T, "w_proj_t": g["L0_conv_w_proj"].T,
        "vectors": _np.concatenate([parts[n] for n in VEC_NAMES], axis=1),
        "w1_t": w1.T, "w_out_t": g["L1_conv_out_pw"][:, by_head].T, "mlp_t": g["L1_conv_mlp_w"].T,
        "k_norm": _np.broadcast_to(k_norm, (P, 2, C)),
        "rel_table": g["L1_conv_rel_table"].T,
        "w2_qk": _np.stack([g["L2_conv_Wq"], g["L2_conv_Wk"]], axis=1),
        "w2_v_t": g["L2_conv_Wv"].T, "w2_exp_t": g["L2_conv_Wexp"].T,
    }
    arrays = {n: _np.ascontiguousarray(a) for n, a in arrays.items()}
    nc = _bacc.Bacc("TRN2", target_bir_lowering=False, num_devices=1)
    args = [nc.dram_tensor(f"in_{n}", a.shape, _mybir.dt.from_np(a.dtype), kind="ExternalInput").ap()
            for n, a in arrays.items()]
    result = nc.dram_tensor("out_0", (B, C, IMG, IMG), F32, kind="ExternalOutput").ap()
    build(nc, *args, result)
    r = _run(nc, [{f"in_{n}": a for n, a in arrays.items()}], core_ids=[0])
    return r.results[0]["out_0"]
```
